# Optimizing a Trainium2 kernel written in Bass

```python
import numpy as np
import jax
import jax.numpy as jnp

def _softmax(x, axis=-1):
    return jax.nn.softmax(x, axis=axis)

def _gelu(x):
    return jax.nn.gelu(x, approximate=True)

def _silu(x):
    return jax.nn.silu(x)

def _sigmoid(x):
    return jax.nn.sigmoid(x)

def _layernorm(x, axis=-1, eps=1e-05):
    m = jnp.mean(x, axis=axis, keepdims=True)
    v = jnp.var(x, axis=axis, keepdims=True)
    return (x - m) / jnp.sqrt(v + eps)

def _scatter_add(tgt, idx, src, axis=0):
    return tgt.at[idx].add(src)

def _segment_sum(src, seg, n):
    return jax.ops.segment_sum(src, seg, n)
kernel_name = 'mk_adaln_ffn_d4_seqx_r4_0d8495'

def setup_inputs(seed: int=0):
    np.random.seed(seed)
    _w = jnp.asarray

    def _rec_inputs():
        import jax
        import jax.numpy as jnp
        _rk = jax.random.key(seed)
        x = -0.000125 + 0.9999 * jax.random.normal(jax.random.fold_in(_rk, 1), (2, 1024, 256), jnp.float32)
        _lenS = 1024 - jax.random.randint(jax.random.fold_in(_rk, 7), (2,), 0, max(1, 1024 // 4) + 1, jnp.int32)
        _lenS2 = 1024 - jax.random.randint(jax.random.fold_in(_rk, 8), (2,), 0, max(1, 1024 // 4) + 1, jnp.int32)
        cond_1024 = 0.00513981 + 1.0024 * jax.random.normal(jax.random.fold_in(_rk, 11), (2, 256), jnp.float32)
        _validS = jnp.arange(1024)[None, :] < _lenS[:, None]
        _validS2 = jnp.arange(1024)[None, :] < _lenS2[:, None]
        _causal = jnp.tril(jnp.ones((1024, 1024), dtype=bool))
        mask_SxS_bk0 = jnp.logical_not(jnp.broadcast_to(_validS[0:1, :], (1024, 1024)))
        return (x, cond_1024, mask_SxS_bk0)
    x, cond_1024, mask_SxS_bk0 = _rec_inputs()

    def _L0_cond_setup():
        import jax, jax.numpy as jnp
        import numpy as np
        IN_FEATURES = 256
        OUT_FEATURES = 256
        BATCH = 32
        SEQ = 256
        EPS = 1e-08
        key = jax.random.key(seed)
        k1, k2, k3 = jax.random.split(key, 3)
        Efou = jax.random.normal(k1, (BATCH, SEQ, IN_FEATURES), dtype=jnp.float32)
        y = jax.random.normal(k2, (BATCH, IN_FEATURES), dtype=jnp.float32)
        weight = jax.random.normal(k3, (IN_FEATURES, OUT_FEATURES), dtype=jnp.float32)
        return {'Efou': Efou, 'y': y, 'weight': weight}
    _L0_cond_all = _L0_cond_setup()
    _L0_cond_in = {k: v for k, v in _L0_cond_all.items() if k in ('weight',)}
    del _L0_cond_all

    def _L0_ffn_setup():
        import jax, jax.numpy as jnp
        import numpy as np
        H = 256
        I = 512
        E = 32
        B, S = (4, 512)

        def _grouped_mm(a, w, group_sizes):
            return jax.lax.ragged_dot(a, w, group_sizes)

        def _swiglu(x, gw, uw, dw):
            return jax.nn.silu(x @ gw) * (x @ uw) @ dw
        key = jax.random.key(seed)
        ks = jax.random.split(key, 8)
        scale = 0.02
        inp = {'hidden_states': jax.random.normal(ks[0], (B, S, H), dtype=jnp.float32), 'gate_w': jax.random.normal(ks[1], (H, E), dtype=jnp.float32) * scale, 'shared_gate_w': jax.random.normal(ks[2], (H, I), dtype=jnp.float32) * scale, 'shared_up_w': jax.random.normal(ks[3], (H, I), dtype=jnp.float32) * scale, 'shared_down_w': jax.random.normal(ks[4], (I, H), dtype=jnp.float32) * scale, 'routed_gate_w': jax.random.normal(ks[5], (E, H, I), dtype=jnp.float32) * scale, 'routed_up_w': jax.random.normal(ks[6], (E, H, I), dtype=jnp.float32) * scale, 'routed_down_w': jax.random.normal(ks[7], (E, I, H), dtype=jnp.float32) * scale}
        return inp
    _L0_ffn_all = _L0_ffn_setup()
    _L0_ffn_in = {k: v for k, v in _L0_ffn_all.items() if k in ('gate_w', 'shared_gate_w', 'shared_up_w', 'shared_down_w', 'routed_gate_w', 'routed_up_w', 'routed_down_w')}
    del _L0_ffn_all

    def _L1_cond_setup():
        import jax, jax.numpy as jnp
        import numpy as np
        B, T, D, H = (2, 512, 256, 16)
        E = D // H
        key = jax.random.key(seed)
        ks = jax.random.split(key, 7)
        s = 1.0 / np.sqrt(D)
        return {'x': jax.random.normal(ks[0], (B, T, D), dtype=jnp.float32), 't': jax.random.normal(ks[1], (B, D), dtype=jnp.float32), 'mask': jnp.tril(jnp.ones((T, T), dtype=bool)), 'Wq': jax.random.normal(ks[2], (D, D), dtype=jnp.float32) * s, 'Wk': jax.random.normal(ks[3], (D, D), dtype=jnp.float32) * s, 'Wv': jax.random.normal(ks[4], (D, D), dtype=jnp.float32) * s, 'Wt': jax.random.normal(ks[5], (D, D), dtype=jnp.float32) * s, 'Wo': jax.random.normal(ks[6], (D, D), dtype=jnp.float32) * s}
    _L1_cond_all = _L1_cond_setup()
    _L1_cond_in = {k: v for k, v in _L1_cond_all.items() if k in ('Wq', 'Wk', 'Wv', 'Wt', 'Wo')}
    del _L1_cond_all

    def _L1_ffn_setup():
        import jax, jax.numpy as jnp
        import numpy as np
        import math
        HID, HD, E, MIN_E = (256, 128, 16, 2)
        B, T = (4, 512)
        IS_CAUSAL = True

        def _l2norm(x, axis):
            return x / jnp.sqrt(jnp.sum(x * x, axis=axis, keepdims=True) + 1e-12)

        def _gating(hidden_states, sim_matrix, gates):
            b, t, c = hidden_states.shape
            flat = hidden_states.reshape(b * t, c)
            logits = _l2norm(flat, -1) @ _l2norm(sim_matrix, 0) - jax.nn.sigmoid(gates)
            gated = jax.nn.relu(logits)
            mask = (gated > 0).astype(gated.dtype)
            inactive = jnp.sum(mask, axis=1) == 0
            _, top_idx = jax.lax.top_k(logits, MIN_E)
            fb = jnp.sum(jax.nn.one_hot(top_idx, E, dtype=mask.dtype), axis=1)
            mask = mask + inactive[:, None].astype(mask.dtype) * fb
            masked = jnp.where(mask > 0, gated, -jnp.inf)
            probs = jax.nn.softmax(masked, axis=-1)
            return probs
        key = jax.random.key(seed)
        ks = jax.random.split(key, 6)
        a_qkv = math.sqrt(6.0 / (HID + HD))
        a_o = math.sqrt(6.0 / (HD + HID))
        return {'hidden_states': jax.random.normal(ks[0], (B, T, HID), jnp.float32), 'sim_matrix': jax.random.normal(ks[1], (HID, E), jnp.float32), 'gates': jnp.zeros((E,), jnp.float32), 'q_proj': jax.random.uniform(ks[2], (E, HID, HD), jnp.float32, -a_qkv, a_qkv), 'k_proj': jax.random.uniform(ks[3], (E, HID, HD), jnp.float32, -a_qkv, a_qkv), 'v_proj': jax.random.uniform(ks[4], (E, HID, HD), jnp.float32, -a_qkv, a_qkv), 'o_proj': jax.random.uniform(ks[5], (E, HD, HID), jnp.float32, -a_o, a_o)}
    _L1_ffn_all = _L1_ffn_setup()
    _L1_ffn_in = {k: v for k, v in _L1_ffn_all.items() if k in ('sim_matrix', 'gates', 'q_proj', 'k_proj', 'v_proj', 'o_proj')}
    del _L1_ffn_all

    def _L2_cond_setup():
        import jax, jax.numpy as jnp
        import numpy as np
        D_MODEL = 256
        D_FF = 1024
        N_EXPERTS = 8
        TOP_K = 2
        N_SHARED = 2
        B, T = (4, 512)
        key = jax.random.key(seed)
        ks = jax.random.split(key, 9)
        Hs = D_FF // 2
        Hr = D_FF // 4
        inp = {'x': jax.random.normal(ks[0], (B, T, D_MODEL), dtype=jnp.float32), 't_emb': jax.random.normal(ks[1], (B, D_MODEL), dtype=jnp.float32), 'W_router': 0.01 * jax.random.normal(ks[2], (N_EXPERTS, 2 * D_MODEL), dtype=jnp.float32), 'router_bias': jnp.zeros((N_EXPERTS,), dtype=jnp.float32), 's_w1': 0.02 * jax.random.normal(ks[3], (N_SHARED, Hs, D_MODEL), dtype=jnp.float32), 's_w3': 0.02 * jax.random.normal(ks[4], (N_SHARED, Hs, D_MODEL), dtype=jnp.float32), 's_w2': 0.02 * jax.random.normal(ks[5], (N_SHARED, D_MODEL, Hs), dtype=jnp.float32), 'r_w1': 0.02 * jax.random.normal(ks[6], (N_EXPERTS, Hr, D_MODEL), dtype=jnp.float32), 'r_w2': 0.02 * jax.random.normal(ks[7], (N_EXPERTS, D_MODEL, Hr), dtype=jnp.float32)}
        return inp
    _L2_cond_all = _L2_cond_setup()
    _L2_cond_in = {k: v for k, v in _L2_cond_all.items() if k in ('W_router', 'router_bias', 's_w1', 's_w3', 's_w2', 'r_w1', 'r_w2')}
    del _L2_cond_all

    def _L2_ffn_setup():
        import jax, jax.numpy as jnp
        import numpy as np
        B, S, D, F, E, NS, K = (2, 256, 256, 1024, 8, 8, 2)
        FS = F // NS
        key = jax.random.key(seed)
        ks = jax.random.split(key, 8)
        scale = 0.02
        return {'hidden_states': jax.random.normal(ks[0], (B, S, D), jnp.float32), 'gate_W': jax.random.normal(ks[1], (E, D), jnp.float32) * scale, 'w1_e': jax.random.normal(ks[2], (E, D, F), jnp.float32) * scale, 'w3_e': jax.random.normal(ks[3], (E, D, F), jnp.float32) * scale, 'w2_e': jax.random.normal(ks[4], (E, F, D), jnp.float32) * scale, 'w1_s': jax.random.normal(ks[5], (NS, D, FS), jnp.float32) * scale, 'w3_s': jax.random.normal(ks[6], (NS, D, FS), jnp.float32) * scale, 'w2_s': jax.random.normal(ks[7], (NS, FS, D), jnp.float32) * scale}
    _L2_ffn_all = _L2_ffn_setup()
    _L2_ffn_in = {k: v for k, v in _L2_ffn_all.items() if k in ('gate_W', 'w1_e', 'w3_e', 'w2_e', 'w1_s', 'w3_s', 'w2_s')}
    del _L2_ffn_all

    def _L3_cond_setup():
        import jax, jax.numpy as jnp
        import numpy as np
        D, HS, HE, E, K = (256, 512, 256, 8, 2)
        B, T = (4, 256)
        N_SHARED = 1
        key = jax.random.key(seed)
        ks = jax.random.split(key, 9)
        g = lambda k, shape, s: jax.random.normal(k, shape, jnp.float32) * s
        return {'x': g(ks[0], (B, T, D), 1.0), 't_emb': g(ks[1], (B, D), 1.0), 'router_W': g(ks[2], (2 * D, E), 0.01), 'router_bias': jnp.zeros((E,), jnp.float32), 'w1': g(ks[3], (D, HS), 0.02), 'w3': g(ks[4], (D, HS), 0.02), 'w2': g(ks[5], (HS, D), 0.02), 'W1e': g(ks[6], (E, D, HE), 0.02), 'W2e': g(ks[7], (E, HE, D), 0.02)}
    _L3_cond_all = _L3_cond_setup()
    _L3_cond_in = {k: v for k, v in _L3_cond_all.items() if k in ('router_W', 'router_bias', 'w1', 'w3', 'w2', 'W1e', 'W2e')}
    del _L3_cond_all

    def _L3_ffn_setup():
        import math
        import jax, jax.numpy as jnp
        import numpy as np
        B, T, D, N, H = (8, 512, 256, 16, 512)
        CAP_FACTOR = 1.25
        key = jax.random.key(seed)
        ks = jax.random.split(key, 4)
        x = jax.random.normal(ks[0], (B, T, D), jnp.float32)
        Wg = jax.random.normal(ks[1], (D, N), jnp.float32) * D ** (-0.5)
        W1 = jax.random.normal(ks[2], (N, D, H), jnp.float32) * D ** (-0.5)
        b1 = jnp.zeros((N, H), jnp.float32)
        W2 = jax.random.normal(ks[3], (N, H, D), jnp.float32) * H ** (-0.5)
        b2 = jnp.zeros((N, D), jnp.float32)
        return {'x': x, 'Wg': Wg, 'W1': W1, 'b1': b1, 'W2': W2, 'b2': b2}
    _L3_ffn_all = _L3_ffn_setup()
    _L3_ffn_in = {k: v for k, v in _L3_ffn_all.items() if k in ('Wg', 'W1', 'b1', 'W2', 'b2')}
    del _L3_ffn_all
    return {'x': x, 'cond_1024': cond_1024, 'mask_SxS_bk0': mask_SxS_bk0, 'L0_cond_weight': _L0_cond_in['weight'], 'L0_ffn_gate_w': _L0_ffn_in['gate_w'], 'L0_ffn_shared_gate_w': _L0_ffn_in['shared_gate_w'], 'L0_ffn_shared_up_w': _L0_ffn_in['shared_up_w'], 'L0_ffn_shared_down_w': _L0_ffn_in['shared_down_w'], 'L0_ffn_routed_gate_w': _L0_ffn_in['routed_gate_w'], 'L0_ffn_routed_up_w': _L0_ffn_in['routed_up_w'], 'L0_ffn_routed_down_w': _L0_ffn_in['routed_down_w'], 'L1_cond_Wq': _L1_cond_in['Wq'], 'L1_cond_Wk': _L1_cond_in['Wk'], 'L1_cond_Wv': _L1_cond_in['Wv'], 'L1_cond_Wt': _L1_cond_in['Wt'], 'L1_cond_Wo': _L1_cond_in['Wo'], 'L1_ffn_sim_matrix': _L1_ffn_in['sim_matrix'], 'L1_ffn_gates': _L1_ffn_in['gates'], 'L1_ffn_q_proj': _L1_ffn_in['q_proj'], 'L1_ffn_k_proj': _L1_ffn_in['k_proj'], 'L1_ffn_v_proj': _L1_ffn_in['v_proj'], 'L1_ffn_o_proj': _L1_ffn_in['o_proj'], 'L2_cond_W_router': _L2_cond_in['W_router'], 'L2_cond_router_bias': _L2_cond_in['router_bias'], 'L2_cond_s_w1': _L2_cond_in['s_w1'], 'L2_cond_s_w3': _L2_cond_in['s_w3'], 'L2_cond_s_w2': _L2_cond_in['s_w2'], 'L2_cond_r_w1': _L2_cond_in['r_w1'], 'L2_cond_r_w2': _L2_cond_in['r_w2'], 'L2_ffn_gate_W': _L2_ffn_in['gate_W'], 'L2_ffn_w1_e': _L2_ffn_in['w1_e'], 'L2_ffn_w3_e': _L2_ffn_in['w3_e'], 'L2_ffn_w2_e': _L2_ffn_in['w2_e'], 'L2_ffn_w1_s': _L2_ffn_in['w1_s'], 'L2_ffn_w3_s': _L2_ffn_in['w3_s'], 'L2_ffn_w2_s': _L2_ffn_in['w2_s'], 'L3_cond_router_W': _L3_cond_in['router_W'], 'L3_cond_router_bias': _L3_cond_in['router_bias'], 'L3_cond_w1': _L3_cond_in['w1'], 'L3_cond_w3': _L3_cond_in['w3'], 'L3_cond_w2': _L3_cond_in['w2'], 'L3_cond_W1e': _L3_cond_in['W1e'], 'L3_cond_W2e': _L3_cond_in['W2e'], 'L3_ffn_Wg': _L3_ffn_in['Wg'], 'L3_ffn_W1': _L3_ffn_in['W1'], 'L3_ffn_b1': _L3_ffn_in['b1'], 'L3_ffn_W2': _L3_ffn_in['W2'], 'L3_ffn_b2': _L3_ffn_in['b2']}

def reference(x, cond_1024, mask_SxS_bk0, L0_cond_weight, L0_ffn_gate_w, L0_ffn_shared_gate_w, L0_ffn_shared_up_w, L0_ffn_shared_down_w, L0_ffn_routed_gate_w, L0_ffn_routed_up_w, L0_ffn_routed_down_w, L1_cond_Wq, L1_cond_Wk, L1_cond_Wv, L1_cond_Wt, L1_cond_Wo, L1_ffn_sim_matrix, L1_ffn_gates, L1_ffn_q_proj, L1_ffn_k_proj, L1_ffn_v_proj, L1_ffn_o_proj, L2_cond_W_router, L2_cond_router_bias, L2_cond_s_w1, L2_cond_s_w3, L2_cond_s_w2, L2_cond_r_w1, L2_cond_r_w2, L2_ffn_gate_W, L2_ffn_w1_e, L2_ffn_w3_e, L2_ffn_w2_e, L2_ffn_w1_s, L2_ffn_w3_s, L2_ffn_w2_s, L3_cond_router_W, L3_cond_router_bias, L3_cond_w1, L3_cond_w3, L3_cond_w2, L3_cond_W1e, L3_cond_W2e, L3_ffn_Wg, L3_ffn_W1, L3_ffn_b1, L3_ffn_W2, L3_ffn_b2):
    import jax
    import jax.numpy as jnp

    def _L0_cond_ref(Efou, y, weight):
        import jax, jax.numpy as jnp
        import numpy as np
        IN_FEATURES = 256
        OUT_FEATURES = 256
        BATCH = 32
        SEQ = 256
        EPS = 1e-08
        scale = 1.0 / np.sqrt(np.float32(weight.shape[0]))
        ys = y * scale
        d = jax.lax.rsqrt(jnp.einsum('bi,io->bo', ys * ys, weight * weight) + EPS)
        out = jnp.einsum('bsi,io->bso', Efou * ys[:, None, :], weight) * d[:, None, :]
        return out

    def _L0_ffn_ref(hidden_states, gate_w, shared_gate_w, shared_up_w, shared_down_w, routed_gate_w, routed_up_w, routed_down_w):
        import jax, jax.numpy as jnp
        import numpy as np
        H = 256
        I = 512
        E = 32
        B, S = (4, 512)

        def _grouped_mm(a, w, group_sizes):
            return jax.lax.ragged_dot(a, w, group_sizes)

        def _swiglu(x, gw, uw, dw):
            return jax.nn.silu(x @ gw) * (x @ uw) @ dw
        b, s, h = hidden_states.shape
        x = hidden_states.reshape(-1, h)
        shared_out = _swiglu(x, shared_gate_w, shared_up_w, shared_down_w)
        logits = x @ gate_w
        topk_ids = jnp.argmax(logits, axis=-1)
        topk_val = jnp.max(logits, axis=-1)
        scores = jax.nn.sigmoid(topk_val)[:, None]
        xs = x * scores
        tokens_per_expert = jnp.zeros((E,), jnp.int32).at[topk_ids].add(1)
        order = jnp.argsort(topk_ids)
        sorted_x = xs[order]
        g = _grouped_mm(sorted_x, routed_gate_w, tokens_per_expert)
        u = _grouped_mm(sorted_x, routed_up_w, tokens_per_expert)
        d = _grouped_mm(jax.nn.silu(g) * u, routed_down_w, tokens_per_expert)
        inv = jnp.argsort(order)
        routed_out = d[inv]
        return (shared_out + routed_out).reshape(b, s, h)

    def _L1_cond_ref(x, t, mask, Wq, Wk, Wv, Wt, Wo):
        import jax, jax.numpy as jnp
        import numpy as np
        B, T, D, H = (2, 512, 256, 16)
        E = D // H
        b, seq, d = x.shape
        h, e = (H, d // H)
        q = (x @ Wq.T).reshape(b, seq, h, e).transpose(0, 2, 1, 3)
        k = (x @ Wk.T).reshape(b, seq, h, e).transpose(0, 2, 1, 3)
        v = (x @ Wv.T).reshape(b, seq, h, e).transpose(0, 2, 1, 3)
        tp = (t @ Wt.T).reshape(b, h, e)
        a = jnp.einsum('bhe,bhse->bhs', tp, q)
        qmod = jnp.einsum('bhs,bhse->bhe', a, q)
        qmod = jnp.broadcast_to(qmod[:, :, None, :], (b, h, seq, e))
        scores = jnp.einsum('bhte,bhse->bhts', qmod, k) / jnp.sqrt(jnp.asarray(e, x.dtype))
        neg = jnp.asarray(jnp.finfo(scores.dtype).min, scores.dtype)
        scores = jnp.where(mask, scores, neg)
        attn = jax.nn.softmax(scores, axis=-1)
        o = jnp.einsum('bhts,bhse->bhte', attn, v)
        o = o.transpose(0, 2, 1, 3).reshape(b, seq, d)
        return o @ Wo.T

    def _L1_ffn_ref(hidden_states, sim_matrix, gates, q_proj, k_proj, v_proj, o_proj):
        import jax, jax.numpy as jnp
        import numpy as np
        import math
        HID, HD, E, MIN_E = (256, 128, 16, 2)
        B, T = (4, 512)
        IS_CAUSAL = True

        def _l2norm(x, axis):
            return x / jnp.sqrt(jnp.sum(x * x, axis=axis, keepdims=True) + 1e-12)

        def _gating(hidden_states, sim_matrix, gates):
            b, t, c = hidden_states.shape
            flat = hidden_states.reshape(b * t, c)
            logits = _l2norm(flat, -1) @ _l2norm(sim_matrix, 0) - jax.nn.sigmoid(gates)
            gated = jax.nn.relu(logits)
            mask = (gated > 0).astype(gated.dtype)
            inactive = jnp.sum(mask, axis=1) == 0
            _, top_idx = jax.lax.top_k(logits, MIN_E)
            fb = jnp.sum(jax.nn.one_hot(top_idx, E, dtype=mask.dtype), axis=1)
            mask = mask + inactive[:, None].astype(mask.dtype) * fb
            masked = jnp.where(mask > 0, gated, -jnp.inf)
            probs = jax.nn.softmax(masked, axis=-1)
            return probs
        b, t, c = hidden_states.shape
        rw = _gating(hidden_states, sim_matrix, gates).reshape(b, t, E)
        q = jnp.einsum('btc,ech,bte->bth', hidden_states, q_proj, rw)
        k = jnp.einsum('btc,ech,bte->bth', hidden_states, k_proj, rw)
        v = jnp.einsum('btc,ech,bte->bth', hidden_states, v_proj, rw)
        scale = 1.0 / math.sqrt(HD)
        scores = jnp.einsum('bqh,bkh->bqk', q, k) * scale
        if IS_CAUSAL:
            causal = jnp.tril(jnp.ones((t, t), dtype=bool))
            scores = jnp.where(causal[None], scores, -jnp.inf)
        attn = jax.nn.softmax(scores, axis=-1)
        ao = jnp.einsum('bqk,bkh->bqh', attn, v)
        out = jnp.einsum('bth,ehc,bte->btc', ao, o_proj, rw)
        return out

    def _L2_cond_ref(x, t_emb, W_router, router_bias, s_w1, s_w3, s_w2, r_w1, r_w2):
        import jax, jax.numpy as jnp
        import numpy as np
        D_MODEL = 256
        D_FF = 1024
        N_EXPERTS = 8
        TOP_K = 2
        N_SHARED = 2
        B, T = (4, 512)
        Bn, Tn, C = x.shape
        N = Bn * Tn
        x_flat = x.reshape(N, C)
        t_flat = jnp.broadcast_to(t_emb[:, None, :], (Bn, Tn, C)).reshape(N, C)
        shared_out = jnp.zeros_like(x_flat)
        for e in range(N_SHARED):
            h = jax.nn.silu(x_flat @ s_w1[e].T) * (x_flat @ s_w3[e].T)
            shared_out = shared_out + h @ s_w2[e].T
        shared_out = shared_out / N_SHARED
        router_in = jnp.concatenate([x_flat, t_flat], axis=-1)
        s = jax.nn.sigmoid((router_in @ W_router.T).astype(jnp.float32))
        sel_scores = s + router_bias
        _, topk_idx = jax.lax.top_k(sel_scores, TOP_K)
        s_sel = jnp.take_along_axis(s, topk_idx, axis=1)
        denom = jnp.sum(s_sel, axis=1, keepdims=True)
        gates = jnp.where(denom > 1e-09, s_sel / (denom + 1e-09), 1.0 / TOP_K).astype(x.dtype)
        gates_full = jnp.sum(jax.nn.one_hot(topk_idx, N_EXPERTS, dtype=x.dtype) * gates[..., None], axis=1)
        routed_out = jnp.zeros_like(x_flat)
        for e in range(N_EXPERTS):
            h = jax.nn.gelu(x_flat @ r_w1[e].T, approximate=False)
            routed_out = routed_out + h @ r_w2[e].T * gates_full[:, e:e + 1]
        out = (shared_out + routed_out) / (N_SHARED + TOP_K)
        return out.reshape(Bn, Tn, C)

    def _L2_ffn_ref(hidden_states, gate_W, w1_e, w3_e, w2_e, w1_s, w3_s, w2_s):
        import jax, jax.numpy as jnp
        import numpy as np
        B, S, D, F, E, NS, K = (2, 256, 256, 1024, 8, 8, 2)
        FS = F // NS
        b, s, d = hidden_states.shape
        e = gate_W.shape[0]
        flat = hidden_states.reshape(-1, d)
        T = flat.shape[0]
        logits = (flat @ gate_W.T).astype(jnp.float32)
        probs = jax.nn.softmax(logits, axis=-1)
        top_v, top_i = jax.lax.top_k(probs, K)
        gates = jnp.zeros((T, e), probs.dtype).at[jnp.arange(T)[:, None], top_i].set(top_v)
        g = jax.nn.silu(jnp.einsum('td,edf->etf', flat, w1_e))
        u = jnp.einsum('td,edf->etf', flat, w3_e)
        out_e = jnp.einsum('etf,efd->etd', g * u, w2_e)
        routed = jnp.einsum('te,etd->td', gates, out_e).reshape(b, s, d)
        gs = jax.nn.silu(jnp.einsum('bsd,ndf->nbsf', hidden_states, w1_s))
        us = jnp.einsum('bsd,ndf->nbsf', hidden_states, w3_s)
        shared = jnp.einsum('nbsf,nfd->bsd', gs * us, w2_s) / w1_s.shape[0]
        alpha = 0.5
        return alpha * shared + (1.0 - alpha) * routed

    def _L3_cond_ref(x, t_emb, router_W, router_bias, w1, w3, w2, W1e, W2e):
        import jax, jax.numpy as jnp
        import numpy as np
        D, HS, HE, E, K = (256, 512, 256, 8, 2)
        B, T = (4, 256)
        N_SHARED = 1
        Bb, Tt, C = x.shape
        xf = x.reshape(-1, C)
        tf = jnp.broadcast_to(t_emb[:, None, :], (Bb, Tt, C)).reshape(-1, C)
        N = xf.shape[0]
        shared = jax.nn.silu(xf @ w1) * (xf @ w3) @ w2
        s = jax.nn.sigmoid((jnp.concatenate([xf, tf], axis=-1) @ router_W).astype(jnp.float32))
        sel_scores = s + router_bias
        _, topk_idx = jax.lax.top_k(sel_scores, K)
        s_sel = jnp.take_along_axis(s, topk_idx, axis=1)
        denom = s_sel.sum(axis=1, keepdims=True)
        gates = jnp.where(denom > 1e-09, s_sel / (denom + 1e-09), 1.0 / K).astype(x.dtype)
        combine = jnp.zeros((N, E), x.dtype).at[jnp.arange(N)[:, None], topk_idx].add(gates)
        h = jax.nn.gelu(jnp.einsum('nc,ech->enh', xf, W1e), approximate=False)
        y = jnp.einsum('enh,ehc->enc', h, W2e)
        routed = jnp.einsum('ne,enc->nc', combine, y)
        return ((shared + routed) / (N_SHARED + K)).reshape(Bb, Tt, C)

    def _L3_ffn_ref(x, Wg, W1, b1, W2, b2):
        import math
        import jax, jax.numpy as jnp
        import numpy as np
        B, T, D, N, H = (8, 512, 256, 16, 512)
        CAP_FACTOR = 1.25
        b, t, d = x.shape
        n = Wg.shape[1]
        bt = b * t
        cap = math.ceil(CAP_FACTOR * bt / n)
        logits = jnp.einsum('btd,dn->btn', x, Wg)
        probs = jax.nn.softmax(logits, axis=-1)
        top1_val = probs.max(axis=-1).reshape(bt)
        top1_idx = probs.argmax(axis=-1).reshape(bt)
        x_flat = x.reshape(bt, d)
        masked = jnp.where(top1_idx[None, :] == jnp.arange(n)[:, None], top1_val[None, :], -jnp.inf)
        vals, idx = jax.lax.top_k(masked, cap)
        valid = jnp.isfinite(vals)
        xe = x_flat[idx]
        h = jax.nn.gelu(jnp.einsum('ncd,ndh->nch', xe, W1) + b1[:, None, :])
        out = jnp.einsum('nch,nhd->ncd', h, W2) + b2[:, None, :]
        safe_idx = jnp.where(valid, idx, bt)
        y_flat = x_flat.at[safe_idx.reshape(-1)].set(out.reshape(-1, d), mode='drop')
        return y_flat.reshape(b, t, d)
    x = x + _L0_ffn_ref(_L0_cond_ref(x, cond_1024, L0_cond_weight), L0_ffn_gate_w, L0_ffn_shared_gate_w, L0_ffn_shared_up_w, L0_ffn_shared_down_w, L0_ffn_routed_gate_w, L0_ffn_routed_up_w, L0_ffn_routed_down_w)
    x = x + _L1_ffn_ref(_L1_cond_ref(x, cond_1024, mask_SxS_bk0, L1_cond_Wq, L1_cond_Wk, L1_cond_Wv, L1_cond_Wt, L1_cond_Wo), L1_ffn_sim_matrix, L1_ffn_gates, L1_ffn_q_proj, L1_ffn_k_proj, L1_ffn_v_proj, L1_ffn_o_proj)
    x = x + _L2_ffn_ref(_L2_cond_ref(x, cond_1024, L2_cond_W_router, L2_cond_router_bias, L2_cond_s_w1, L2_cond_s_w3, L2_cond_s_w2, L2_cond_r_w1, L2_cond_r_w2), L2_ffn_gate_W, L2_ffn_w1_e, L2_ffn_w3_e, L2_ffn_w2_e, L2_ffn_w1_s, L2_ffn_w3_s, L2_ffn_w2_s)
    x = x + _L3_ffn_ref(_L3_cond_ref(x, cond_1024, L3_cond_router_W, L3_cond_router_bias, L3_cond_w1, L3_cond_w3, L3_cond_w2, L3_cond_W1e, L3_cond_W2e), L3_ffn_Wg, L3_ffn_W1, L3_ffn_b1, L3_ffn_W2, L3_ffn_b2)
    return x

_drawn_inputs = setup_inputs


def setup_inputs(seed=0):
    import zlib

    import numpy as np

    out = dict(_drawn_inputs(seed))
    spreads = {'L1_ffn_gates': (0.0, 0.1),
     'L2_cond_router_bias': (0.0, 0.1),
     'L3_cond_router_bias': (0.0, 0.1),
     'L3_ffn_b1': (0.0, 0.1),
     'L3_ffn_b2': (0.0, 0.1)}
    factors = {}
    for name, (base, spread) in spreads.items():
        noise = np.random.default_rng([zlib.crc32(name.encode()), seed]).standard_normal(out[name].shape)
        drawn = base * np.exp(spread * noise) if base else spread * noise
        out[name] = jnp.asarray(drawn.astype(out[name].dtype))
    for name, factor in factors.items():
        out[name] = (out[name] * factor).astype(out[name].dtype)
    return out
```

```python
from contextlib import ExitStack

import concourse.bass as bass
from concourse import mybir

F32 = mybir.dt.float32
I32 = mybir.dt.int32
U32 = mybir.dt.uint32
U8 = mybir.dt.uint8
ALU = mybir.AluOpType
ACT = mybir.ActivationFunctionType
AX_X = mybir.AxisListType.X

P = 128
B, S, D = 2, 1024, 256
T = B * S
NT = T // P
KD = D // P
CH = 512
NCH = T // CH
TPC = CH // P
TPB = S // P
FU = 512
UNIT = KD * FU * 2 + FU // P * D
BIG = 1000.0
E0, E1, E2, E3 = 32, 16, 8, 16
H1 = 128
SLOT_TILES0 = NT + E0
SLOT_TILES2 = 2 * NT + E2
CAP = 160
DROPPED = 4096
FMAX = 3.4028234663852886e38
HEADS, HW = 16, 16


def build(nc, a, out):
    ctx = ExitStack()
    with ctx:
        def sb(name, shape, dt=F32, on=ctx):
            return on.enter_context(nc.sbuf_tensor("sb_" + name, shape, dt))

        def sem(name):
            return nc.alloc_semaphore(name=name)

        def scratch(name, rows):
            return nc.dram_tensor(name, [rows, D], F32, kind="Internal").ap()

        rows0_in, rows0_out = scratch("rows0_in", SLOT_TILES0 * P), scratch("rows0_out", SLOT_TILES0 * P)
        rows2_in, rows2_out = scratch("rows2_in", SLOT_TILES2 * P), scratch("rows2_out", SLOT_TILES2 * P)
        rows3_in, rows3_out = scratch("rows3_in", E3 * CAP), scratch("rows3_out", E3 * CAP)

        xtok = sb("xtok", [P, NT, D])
        ctok = sb("ctok", [P, NT, D])
        acc = sb("acc", [P, NT, D])
        fx = sb("fx", [P, KD, T])
        fc = sb("fc", [P, KD, T])
        wbuf = sb("wbuf", [P, 2, 2 * UNIT])
        ident = sb("ident", [P, P])
        tri = sb("tri", [P, P])
        ones = sb("ones", [P, P])
        iota_e = sb("iota_e", [P, E0])
        condT = sb("condT", [P, KD, B])
        psum = ctx.enter_context(nc.psum_tensor("ps", [P, 8, 512], F32))

        def stage_load():
            loaded, cleared, made, zeroed = sem("ld_in"), sem("ld_cleared"), sem("ld_made"), sem("ld_zeroed")
            with nc.Block() as block:
                @block.sync
                def _(sp):
                    sp.dma_start(xtok[:], a["x"].rearrange("(i p) d -> p i d", p=P)).then_inc(loaded, 16)
                    sp.dma_start(condT[:], a["condT"]).then_inc(loaded, 16)
                    sp.wait_ge(cleared, 1)
                    n = 0
                    for table in (rows0_in, rows2_in, rows3_in):
                        tiles = table.shape[0] // P
                        for i in range(0, tiles, NT):
                            m = min(NT, tiles - i)
                            sp.dma_start(table[i * P:(i + m) * P, :].rearrange("(i p) d -> p i d", p=P),
                                         acc[:, 0:m, :]).then_inc(zeroed, 16)
                            n += 1
                    sp.wait_ge(loaded, 32)
                    sp.wait_ge(zeroed, 16 * n)

                @block.vector
                def _(dve):
                    dve.memset(acc[:], 0.0).then_inc(cleared, 1)
                    dve.memset(ones[:], 1.0).then_inc(made, 1)

                @block.gpsimd
                def _(pool):
                    pool.iota(iota_e[:], pattern=[[1, E0]], base=-int(BIG), channel_multiplier=0,
                              allow_small_or_imprecise_dtypes=True)
                    pool.wait_ge(made, 1)
                    pool.affine_select(out=ident[:], in_=ones[:], compare_op=ALU.is_equal, fill=0.0,
                                       base=0, pattern=[[-1, P]], channel_multiplier=1)
                    pool.affine_select(out=tri[:], in_=ones[:], compare_op=ALU.is_gt, fill=0.0,
                                       base=0, pattern=[[1, P]], channel_multiplier=-1)

        def stage_to_features(tag, tok, feat):
            turned, used = sem(tag + "_turned"), sem(tag + "_used")
            with nc.Block() as block:
                @block.tensor
                def _(pe):
                    for b in range(8):
                        k, c = b // NCH, b % NCH
                        for q in range(TPC):
                            last = pe.transpose(psum[:, b, q * P:(q + 1) * P],
                                                tok[:, c * TPC + q, k * P:(k + 1) * P], ident[:])
                        last.then_inc(turned, 1)

                @block.vector
                def _(dve):
                    for b in range(0, 8, 2):
                        dve.wait_ge(turned, b + 1)
                        dve.tensor_copy(feat[:, b // NCH, (b % NCH) * CH:(b % NCH + 1) * CH], psum[:, b, :])

                @block.scalar
                def _(act):
                    for b in range(1, 8, 2):
                        act.wait_ge(turned, b + 1)
                        act.copy(feat[:, b // NCH, (b % NCH) * CH:(b % NCH + 1) * CH], psum[:, b, :])

        def stage_to_tokens(tag, feat, tok):
            turned = sem(tag + "_turned")
            with nc.Block() as block:
                @block.tensor
                def _(pe):
                    for b in range(8):
                        for q in range(2):
                            for k in range(KD):
                                t0 = (2 * b + q) * P
                                last = pe.transpose(psum[:, b, (q * KD + k) * P:(q * KD + k + 1) * P],
                                                    feat[:, k, t0:t0 + P], ident[:])
                        last.then_inc(turned, 1)

                @block.vector
                def _(dve):
                    for b in range(0, 8, 2):
                        dve.wait_ge(turned, b + 1)
                        dve.tensor_copy(tok[:, 2 * b:2 * b + 2, :].rearrange("p i d -> p (i d)"), psum[:, b, :])

                @block.scalar
                def _(act):
                    for b in range(1, 8, 2):
                        act.wait_ge(turned, b + 1)
                        act.copy(tok[:, 2 * b:2 * b + 2, :].rearrange("p i d -> p (i d)"), psum[:, b, :])

        def stage_l0_cond():
            with ExitStack() as own:
                w = sb("l0c_w", [P, KD, D], on=own)
                w2 = sb("l0c_w2", [P, KD, D], on=own)
                wb = sb("l0c_wb", [P, B, KD, D], on=own)
                ys = sb("l0c_ys", [P, KD, B], on=own)
                ys2 = sb("l0c_ys2", [P, KD, B], on=own)
                d = sb("l0c_d", [P, KD, B], on=own)
                loaded, order, squares, norm, root, demod, folded, done = (
                    sem("l0c_" + n) for n in ("loaded", "order", "squares", "norm", "root", "demod", "folded", "done"))
                with nc.Block() as block:
                    @block.sync
                    def _(sp):
                        sp.dma_start(w[:], a["l0_cond_w"]).then_inc(loaded, 16)

                    @block.vector
                    def _(dve):
                        dve.tensor_scalar(ys[:], condT[:], float(D) ** -0.5, None, ALU.mult).then_inc(order, 1)
                        dve.wait_ge(order, 1)
                        dve.tensor_tensor(ys2[:], ys[:], ys[:], ALU.mult)
                        dve.wait_ge(loaded, 16)
                        dve.tensor_tensor(w2[:], w[:], w[:], ALU.mult).then_inc(squares, 1)
                        for b in range(B):
                            for k in range(KD):
                                last = dve.tensor_scalar(wb[:, b, k, :], w[:, k, :], ys[:, k, b:b + 1], None, ALU.mult)
                        last.then_inc(folded, 1)
                        dve.wait_ge(norm, 1)
                        dve.tensor_scalar(d[:], psum[:, 0, 0:KD * B].rearrange("p (k b) -> p k b", k=KD),
                                          1e-8, None, ALU.add).then_inc(order, 1)
                        dve.wait_ge(root, 1)
                        dve.reciprocal(d[:], d[:]).then_inc(demod, 1)
                        dve.wait_ge(demod, 1)
                        for n in range(8):
                            dve.wait_ge(done, n + 1)
                            b, c, o = n // 4, n // 2 % 2, n % 2
                            t0 = b * S + c * CH
                            dve.tensor_scalar(fc[:, o, t0:t0 + CH], psum[:, n, :], d[:, o, b:b + 1], None, ALU.mult)

                    @block.scalar
                    def _(act):
                        act.wait_ge(order, 2)
                        act.activation(d[:], d[:], ACT.Sqrt).then_inc(root, 1)

                    @block.tensor
                    def _(pe):
                        pe.wait_ge(squares, 1)
                        for o in range(KD):
                            for k in range(KD):
                                last = pe.matmul(psum[:, 0, o * B:(o + 1) * B], w2[:, k, o * P:(o + 1) * P],
                                                 ys2[:, k, :], start=(k == 0), stop=(k == KD - 1))
                        last.then_inc(norm, 1)
                        pe.wait_ge(folded, 1)
                        pe.wait_ge(demod, 1)
                        for n in range(8):
                            b, c, o = n // 4, n // 2 % 2, n % 2
                            t0 = b * S + c * CH
                            for k in range(KD):
                                last = pe.matmul(psum[:, n, :], wb[:, b, k, o * P:(o + 1) * P],
                                                 fx[:, k, t0:t0 + CH], start=(k == 0), stop=(k == KD - 1))
                            last.then_inc(done, 1)

        def stage_glu(tag, feat, units):
            NU = units.shape[0]
            N = NU * NCH
            NF = FU // P
            with ExitStack() as own:
                sg = sb(tag + "_sg", [P, 2, CH], on=own)
                h = sb(tag + "_h", [P, 2, NF, CH], on=own)
                loaded = [sem(f"{tag}_w{u}") for u in range(NU)]
                both, gated, hidden, down, added = (sem(f"{tag}_{n}") for n in ("both", "gated", "hidden", "down", "added"))
                with nc.Block() as block:
                    @block.sync
                    def _(sp):
                        for u in range(NU):
                            sp.dma_start(wbuf[:, u, 0:UNIT], units[u]).then_inc(loaded[u], 16)

                    def wgate(u, k, f):
                        return wbuf[:, u, k * FU + f * P:k * FU + (f + 1) * P]

                    def wup(u, k, f):
                        return wbuf[:, u, (KD + k) * FU + f * P:(KD + k) * FU + (f + 1) * P]

                    def wdown(u, f):
                        return wbuf[:, u, 2 * KD * FU + f * D:2 * KD * FU + (f + 1) * D]

                    @block.tensor
                    def _(pe):
                        def gate_up(n):
                            u, c = n // NCH, n % NCH
                            if c == 0:
                                pe.wait_ge(loaded[u], 16)
                            for f in range(NF):
                                m = n * NF + f
                                if m >= 2:
                                    pe.wait_ge(hidden, m - 1)
                                for j, w in enumerate((wgate, wup)):
                                    for k in range(KD):
                                        last = pe.matmul(psum[:, m % 2 * 2 + j, :], w(u, k, f),
                                                         feat[:, k, c * CH:(c + 1) * CH],
                                                         start=(k == 0), stop=(k == KD - 1))
                                last.then_inc(both, 1)

                        gate_up(0)
                        for n in range(N):
                            if n + 1 < N:
                                gate_up(n + 1)
                            pe.wait_ge(hidden, NF * (n + 1))
                            for half in range(2):
                                if n >= 1:
                                    pe.wait_ge(added, 2 * (n - 1) + half + 1)
                                for q in range(2):
                                    for f in range(NF):
                                        t0 = (2 * half + q) * P
                                        last = pe.matmul(psum[:, 4 + half, q * D:(q + 1) * D],
                                                         h[:, n % 2, f, t0:t0 + P], wdown(n // NCH, f),
                                                         start=(f == 0), stop=(f == NF - 1))
                                last.then_inc(down, 1)

                    @block.scalar
                    def _(act):
                        for m in range(N * NF):
                            act.wait_ge(both, m + 1)
                            if m >= 2:
                                act.wait_ge(hidden, m - 1)
                            act.activation(sg[:, m % 2, :], psum[:, m % 2 * 2, :], ACT.Silu).then_inc(gated, 1)

                    @block.vector
                    def _(dve):
                        def multiply(n):
                            if n >= 2:
                                dve.wait_ge(down, 2 * (n - 1))
                            for f in range(NF):
                                m = n * NF + f
                                dve.wait_ge(gated, m + 1)
                                dve.tensor_tensor(h[:, n % 2, f, :], sg[:, m % 2, :], psum[:, m % 2 * 2 + 1, :],
                                                  ALU.mult).then_inc(hidden, 1)

                        multiply(0)
                        for n in range(N):
                            if n + 1 < N:
                                multiply(n + 1)
                            u, c = n // NCH, n % NCH
                            for half in range(2):
                                dve.wait_ge(down, 2 * n + half + 1)
                                to = acc[:, c * TPC + 2 * half:c * TPC + 2 * half + 2, :].rearrange("p i d -> p (i d)")
                                if u == 0:
                                    ins = dve.tensor_copy(to, psum[:, 4 + half, :])
                                else:
                                    ins = dve.tensor_tensor(to, psum[:, 4 + half, :], to, ALU.add)
                                ins.then_inc(added, 1)

        def stage_gelu_experts(tag, feat, experts, gates, scale_before, scale_after):
            NF = 2
            W = KD * NF * P + NF * D
            NE = experts.shape[0]
            with ExitStack() as own:
                h = sb(tag + "_h", [P, 2, NF, CH], on=own)
                loaded = [sem(f"{tag}_w{r}") for r in range(2)]
                up, hidden, down, added, scaled = (sem(f"{tag}_{n}") for n in ("up", "hidden", "down", "added", "scaled"))
                with nc.Block() as block:
                    @block.sync
                    def _(sp):
                        for r in range(2):
                            sp.dma_start(wbuf[:, r, 0:W], experts[r]).then_inc(loaded[r], 16)
                        with sp.Fori(1, NE // 2) as i:
                            for r in range(2):
                                sp.wait_ge(down, 8 * (2 * i + r - 1))
                                sp.dma_start(wbuf[:, r, 0:W], experts[bass.ds(2 * i + r, 1)].rearrange("e p n -> p (e n)")
                                             ).then_inc(loaded[r], 16)

                    def w1(r, k, f):
                        return wbuf[:, r, k * NF * P + f * P:k * NF * P + (f + 1) * P]

                    def w2(r, f):
                        return wbuf[:, r, KD * NF * P + f * D:KD * NF * P + (f + 1) * D]

                    @block.tensor
                    def _(pe):
                        def up_part(i, m, first):
                            r, c = m // NCH, m % NCH
                            if c == 0:
                                pe.wait_ge(loaded[r], 16 * (i + 1))
                            for f in range(NF):
                                if not first:
                                    pe.wait_ge(hidden, 16 * i + 2 * m + f - 3)
                                for k in range(KD):
                                    last = pe.matmul(psum[:, (2 * m + f) % 4, :], w1(r, k, f),
                                                     feat[:, k, c * CH:(c + 1) * CH],
                                                     start=(k == 0), stop=(k == KD - 1))
                                last.then_inc(up, 1)

                        def down_part(i, m, first):
                            pe.wait_ge(hidden, 16 * i + 2 * m + 2)
                            for half in range(2):
                                if not first:
                                    pe.wait_ge(added, 16 * i + 2 * m + half - 1)
                                for q in range(2):
                                    for f in range(NF):
                                        t0 = (2 * half + q) * P
                                        last = pe.matmul(psum[:, 4 + half, q * D:(q + 1) * D],
                                                         h[:, m % 2, f, t0:t0 + P], w2(m // NCH, f),
                                                         start=(f == 0), stop=(f == NF - 1))
                                last.then_inc(down, 1)

                        def pair(i, first):
                            up_part(i, 0, first)
                            for m in range(2 * NCH):
                                if m + 1 < 2 * NCH:
                                    up_part(i, m + 1, first and m + 1 < 2)
                                down_part(i, m, first and m == 0)

                        pair(0, True)
                        with pe.Fori(1, NE // 2) as i:
                            pair(i, False)

                    @block.scalar
                    def _(act):
                        def pair(i, first):
                            for m in range(2 * NCH):
                                for f in range(NF):
                                    act.wait_ge(up, 16 * i + 2 * m + f + 1)
                                    if not (first and m < 2):
                                        act.wait_ge(down, 16 * i + 2 * m - 2)
                                    act.activation(h[:, m % 2, f, :], psum[:, (2 * m + f) % 4, :],
                                                   ACT.Gelu).then_inc(hidden, 1)

                        pair(0, True)
                        with act.Fori(1, NE // 2) as i:
                            pair(i, False)

                    @block.vector
                    def _(dve):
                        dve.tensor_scalar(acc[:], acc[:], scale_before, None, ALU.mult).then_inc(scaled, 1)
                        dve.wait_ge(scaled, 1)

                        def pair(i, first):
                            for m in range(2 * NCH):
                                r, c = m // NCH, m % NCH
                                for half in range(2):
                                    dve.wait_ge(down, 16 * i + 2 * m + half + 1)
                                    if not (first and m < NCH):
                                        dve.wait_ge(added, 16 * i + 2 * (m - NCH) + half + 1)
                                    for q in range(2):
                                        t = c * TPC + 2 * half + q
                                        ins = dve.scalar_tensor_tensor(
                                            out=acc[:, t, :], in0=psum[:, 4 + half, q * D:(q + 1) * D],
                                            scalar=gates[:, t, bass.ds(2 * i + r, 1)], in1=acc[:, t, :],
                                            op0=ALU.mult, op1=ALU.add)
                                    ins.then_inc(added, 1)

                        pair(0, True)
                        with dve.Fori(1, NE // 2) as i:
                            pair(i, False)
                        dve.wait_ge(added, 8 * NE)
                        dve.tensor_scalar(ctok[:], acc[:], scale_after, None, ALU.mult)

        def logits_on_pe(pe, feat, wr, E, extra=None):
            for i in range(NT):
                parts = [(feat[:, k, i * P:(i + 1) * P], wr[:, k, :]) for k in range(KD)]
                if extra is not None:
                    parts += [(extra[:, k, i // TPB, :], wr[:, KD + k, :]) for k in range(KD)]
                for n, (x, w) in enumerate(parts):
                    last = pe.matmul(psum[:, 0, i * E:(i + 1) * E], x, w, start=(n == 0), stop=(n == len(parts) - 1))
            return last

        def over_e(v, E):
            return v.unsqueeze(2).to_broadcast([P, NT, E])

        def e_index(E):
            return iota_e[:, 0:E].unsqueeze(1).to_broadcast([P, NT, E])

        def pick(dve, link, L, top, onehot, tmp, small, E):
            link(dve.tensor_reduce(top, L, AX_X, ALU.max))
            link(dve.tensor_tensor(tmp, L, over_e(top, E), ALU.is_equal))
            link(dve.tensor_tensor(tmp, tmp, e_index(E), ALU.mult))
            link(dve.tensor_reduce(small, tmp, AX_X, ALU.min))
            link(dve.tensor_tensor(onehot, e_index(E), over_e(small, E), ALU.is_equal))

        def chain(dve, order):
            n = [0]

            def link(ins):
                n[0] += 1
                ins.then_inc(order, 1)
                dve.wait_ge(order, n[0])
            return link

        def stage_slots(tag, onehots, E, tiles, slots, tile_expert):
            K = len(onehots)
            N = K * T
            with ExitStack() as own:
                ohT = sb(tag + "_ohT", [E, N], on=own)
                cum = sb(tag + "_cum", [E, N], on=own)
                steps = sb(tag + "_steps", [E, N // P], on=own)
                tiles_i = sb(tag + "_tiles", [E, tiles], on=own)
                ends = sb(tag + "_ends", [E, tiles], on=own)
                v = sb(tag + "_v", [E, 4], on=own)
                te = sb(tag + "_te", [1, tiles], on=own)
                turned, copied, iotas, counted, started, ended, cols, order, experts = (
                    sem(f"{tag}_{n}") for n in ("turned", "copied", "iotas", "counted", "started", "ended", "cols",
                                                "order", "experts"))
                G = N // CH
                with nc.Block() as block:
                    @block.gpsimd
                    def _(pool):
                        pool.iota(steps[:], pattern=[[P, N // P]], base=0, channel_multiplier=0,
                                  allow_small_or_imprecise_dtypes=True)
                        pool.iota(tiles_i[:], pattern=[[1, tiles]], base=0, channel_multiplier=0,
                                  allow_small_or_imprecise_dtypes=True).then_inc(iotas, 1)

                    @block.tensor
                    def _(pe):
                        for g in range(G):
                            if g >= 4:
                                pe.wait_ge(copied, g - 3)
                            for q in range(TPC):
                                i = g * TPC + q
                                last = pe.transpose(psum[0:E, g % 4, q * P:(q + 1) * P],
                                                    onehots[i // NT][:, i % NT, :], ident[:])
                            last.then_inc(turned, 1)
                        pe.wait_ge(counted, 1)
                        pe.matmul(psum[0:E, 4, 0:1], tri[0:E, 0:E], v[:, 0:1], start=True, stop=True).then_inc(started, 1)
                        pe.wait_ge(ended, 1)
                        pe.matmul(psum[0:1, 5, 0:tiles], ones[0:E, 0:1], ends[:], start=True, stop=True).then_inc(experts, 1)
                        for i in range(N // P):
                            last = pe.matmul(psum[:, 6, i:i + 1], cum[:, i * P:(i + 1) * P], ones[0:E, 0:1],
                                             start=True, stop=True)
                        last.then_inc(cols, 1)

                    @block.scalar
                    def _(act):
                        for g in range(G):
                            act.wait_ge(turned, g + 1)
                            act.copy(ohT[:, g * CH:(g + 1) * CH], psum[0:E, g % 4, :]).then_inc(copied, 1)

                    @block.vector
                    def _(dve):
                        link = chain(dve, order)
                        dve.wait_ge(copied, G)
                        link(dve.tensor_tensor_scan(cum[:], ones[0:E, 0:1].to_broadcast([E, N]), ohT[:], 0.0,
                                                    ALU.mult, ALU.add))
                        dve.wait_ge(iotas, 1)
                        link(dve.tensor_scalar(steps[:], steps[:], cum[:, N - 1:N], None, ALU.is_lt))
                        dve.tensor_reduce(v[:, 0:1], steps[:], AX_X, ALU.add).then_inc(counted, 1)
                        dve.wait_ge(counted, 1)
                        dve.wait_ge(started, 1)
                        link(dve.tensor_tensor(v[:, 1:2], psum[0:E, 4, 0:1], v[:, 0:1], ALU.add))
                        link(dve.tensor_scalar(v[:, 2:3], psum[0:E, 4, 0:1], float(P), -1.0, ALU.mult, ALU.add))
                        link(dve.tensor_scalar(ends[:], tiles_i[:], v[:, 1:2], None, ALU.is_ge))
                        dve.scalar_tensor_tensor(out=cum[:], in0=cum[:], scalar=v[:, 2:3], in1=ohT[:],
                                                 op0=ALU.add, op1=ALU.mult).then_inc(ended, 1)
                        dve.wait_ge(experts, 1)
                        link(dve.tensor_scalar(te[:], psum[0:1, 5, 0:tiles], float(E - 1), None, ALU.min))
                        dve.tensor_copy(tile_expert[:], te[:])
                        dve.wait_ge(cols, 1)
                        dve.tensor_copy(slots[:], psum[:, 6, 0:N // P])

        def stage_scatter(tag, rows, table, slots, K, bound=None):
            sent = sem(tag + "_sent")
            with nc.Block() as block:
                @block.gpsimd
                def _(pool):
                    for n in range(K * NT):
                        extra = {} if bound is None else dict(bounds_check=bound, oob_is_err=False)
                        pool.indirect_dma_start(
                            out=table, out_offset=bass.IndirectOffsetOnAxis(ap=slots[:, n:n + 1], axis=0),
                            in_=rows[:, n % NT, :], in_offset=None, **extra).then_inc(sent, 16)
                    pool.wait_ge(sent, 16 * K * NT)

        def stage_gather(tag, table, slots, bufs, bound=None):
            got = sem(tag + "_got")
            with nc.Block() as block:
                @block.gpsimd
                def _(pool):
                    for k, buf in enumerate(bufs):
                        for i in range(NT):
                            n = k * NT + i
                            extra = {} if bound is None else dict(bounds_check=bound, oob_is_err=False)
                            pool.indirect_dma_start(
                                out=buf[:, i, :], out_offset=None, in_=table,
                                in_offset=bass.IndirectOffsetOnAxis(ap=slots[:, n:n + 1], axis=0),
                                **extra).then_inc(got, 16)
                    pool.wait_ge(got, 16 * NT * len(bufs))

        def stage_sorted_glu(tag, tiles, halves, weights, tile_expert, rows_in, rows_out):
            F = halves * FU
            NF = F // P
            W = halves * UNIT
            with ExitStack() as own:
                r_in = sb(tag + "_rin", [P, 2, D], on=own)
                rT = sb(tag + "_rT", [P, 2, KD, P], on=own)
                sg = sb(tag + "_sg", [P, halves, FU], on=own)
                h = sb(tag + "_h", [P, halves, FU], on=own)
                hT = sb(tag + "_hT", [P, halves, FU], on=own)
                r_out = sb(tag + "_rout", [P, 2, D], on=own)
                w_in = [sem(f"{tag}_w_in{r}") for r in range(2)]
                x_in = [sem(f"{tag}_x_in{r}") for r in range(2)]
                stored = [sem(f"{tag}_stored{r}") for r in range(2)]
                rows_t, rows_c, gate, silu, up, hidden, hid_t, hid_c, down, outc = (
                    sem(f"{tag}_{n}") for n in ("rows_t", "rows_c", "gate", "silu", "up", "hidden",
                                                "hid_t", "hid_c", "down", "outc"))
                src = rows_in.rearrange("(j p) d -> j p d", p=P)
                dst = rows_out.rearrange("(j p) d -> j p d", p=P)
                with nc.Block() as block:
                    @block.sync
                    def _(sp):
                        def load(i, r, first):
                            j = 2 * i + r
                            e = sp.value_load(tile_expert[0:1, bass.ds(j, 1)], min_val=0, max_val=weights.shape[0] - 1)
                            if not first:
                                sp.wait_ge(rows_t, j - 1)
                            sp.dma_start(r_in[:, r, :], src[bass.ds(j, 1)].rearrange("j p d -> p (j d)")
                                         ).then_inc(x_in[r], 16)
                            if not first:
                                sp.wait_ge(down, j - 1)
                            sp.dma_start(wbuf[:, r, 0:W], weights[bass.ds(e, 1)].rearrange("e p n -> p (e n)")
                                         ).then_inc(w_in[r], 16)
                        load(0, 0, True)
                        load(0, 1, True)
                        with sp.Fori(1, tiles // 2) as i:
                            load(i, 0, False)
                            load(i, 1, False)

                    def wgate(r, k, v):
                        return wbuf[:, r, k * F + v * FU:k * F + (v + 1) * FU]

                    def wup(r, k, v):
                        return wbuf[:, r, (KD + k) * F + v * FU:(KD + k) * F + (v + 1) * FU]

                    def wdown(r, f):
                        return wbuf[:, r, 2 * KD * F + f * D:2 * KD * F + (f + 1) * D]

                    @block.tensor
                    def _(pe):
                        def turn_rows(i, r, first=False):
                            pe.wait_ge(x_in[r], 16 * i + 16)
                            if not first:
                                pe.wait_ge(rows_c, 2 * i + r)
                            for k in range(KD):
                                last = pe.transpose(psum[:, 6, k * P:(k + 1) * P], r_in[:, r, k * P:(k + 1) * P], ident[:])
                            last.then_inc(rows_t, 1)

                        def turn_hidden(j):
                            for v in range(halves):
                                pe.wait_ge(hidden, j * halves + v + 1)
                                for q in range(TPC):
                                    last = pe.transpose(psum[:, 4 + v, q * P:(q + 1) * P], h[:, v, q * P:(q + 1) * P], ident[:])
                                last.then_inc(hid_t, 1)

                        def down_product(j, r, first=False):
                            pe.wait_ge(hid_c, j * halves + halves)
                            if not first:
                                pe.wait_ge(outc, j)
                            for f in range(NF):
                                last = pe.matmul(psum[:, 7, 0:D], hT[:, f // TPC, (f % TPC) * P:(f % TPC + 1) * P],
                                                 wdown(r, f), start=(f == 0), stop=(f == NF - 1))
                            last.then_inc(down, 1)

                        def tile(i, r, first=False, second=False, last_tile=False):
                            j = 2 * i + r
                            pe.wait_ge(rows_c, j + 1)
                            pe.wait_ge(w_in[r], 16 * i + 16)
                            for v in range(halves):
                                if not first:
                                    pe.wait_ge(silu, (j - 1) * halves + v + 1)
                                for k in range(KD):
                                    last = pe.matmul(psum[:, v, :], rT[:, r, k, :], wgate(r, k, v),
                                                     start=(k == 0), stop=(k == KD - 1))
                                last.then_inc(gate, 1)
                            if not first:
                                turn_hidden(j - 1)
                            if not last_tile:
                                turn_rows(i + r, 1 - r)
                            for v in range(halves):
                                if not first:
                                    pe.wait_ge(hidden, (j - 1) * halves + v + 1)
                                for k in range(KD):
                                    last = pe.matmul(psum[:, 2 + v, :], rT[:, r, k, :], wup(r, k, v),
                                                     start=(k == 0), stop=(k == KD - 1))
                                last.then_inc(up, 1)
                            if not first:
                                down_product(j - 1, 1 - r, first=second)

                        turn_rows(0, 0, first=True)
                        tile(0, 0, first=True)
                        tile(0, 1, second=True)
                        with pe.Fori(1, tiles // 2 - 1) as i:
                            tile(i, 0)
                            tile(i, 1)
                        tile(tiles // 2 - 1, 0)
                        tile(tiles // 2 - 1, 1, last_tile=True)
                        turn_hidden(tiles - 1)
                        down_product(tiles - 1, 1)

                    @block.scalar
                    def _(act):
                        def silu_part(j, first=False):
                            for v in range(halves):
                                act.wait_ge(gate, j * halves + v + 1)
                                if not first:
                                    act.wait_ge(hidden, (j - 1) * halves + v + 1)
                                act.activation(sg[:, v, :], psum[:, v, :], ACT.Silu).then_inc(silu, 1)

                        def rows_part(j, r, first=False):
                            act.wait_ge(rows_t, j + 1)
                            if not first:
                                act.wait_ge(up, (j - 1) * halves)
                            act.copy(rT[:, r, :, :].rearrange("p k t -> p (k t)"), psum[:, 6, 0:D]).then_inc(rows_c, 1)

                        def out_part(i, r, first=False):
                            j = 2 * i + r
                            act.wait_ge(down, j + 1)
                            if not first:
                                act.wait_ge(stored[r], 16 * i)
                            act.copy(r_out[:, r, :], psum[:, 7, 0:D]).then_inc(outc, 1)
                            act.wait_ge(outc, j + 1)
                            act.dma_start(dst[bass.ds(j, 1)].rearrange("j p d -> p (j d)"), r_out[:, r, :]
                                          ).then_inc(stored[r], 16)

                        rows_part(0, 0, first=True)
                        silu_part(0, first=True)
                        rows_part(1, 1, first=True)
                        silu_part(1)
                        rows_part(2, 0)
                        out_part(0, 0, first=True)
                        silu_part(2)
                        rows_part(3, 1)
                        out_part(0, 1, first=True)
                        with act.Fori(1, tiles // 2 - 1) as i:
                            silu_part(2 * i + 1)
                            rows_part(2 * i + 2, 0)
                            out_part(i, 0)
                            silu_part(2 * i + 2)
                            rows_part(2 * i + 3, 1)
                            out_part(i, 1)
                        silu_part(tiles - 1)
                        out_part(tiles // 2 - 1, 0)
                        out_part(tiles // 2 - 1, 1)
                        for r in range(2):
                            act.wait_ge(stored[r], 16 * (tiles // 2))

                    @block.vector
                    def _(dve):
                        def multiply(j, first):
                            for v in range(halves):
                                dve.wait_ge(up, j * halves + v + 1)
                                dve.wait_ge(silu, j * halves + v + 1)
                                if not first:
                                    dve.wait_ge(hid_t, (j - 1) * halves + v + 1)
                                dve.tensor_tensor(h[:, v, :], sg[:, v, :], psum[:, 2 + v, :], ALU.mult).then_inc(hidden, 1)

                        def copy_hidden(j, first):
                            for v in range(halves):
                                dve.wait_ge(hid_t, j * halves + v + 1)
                                if not first:
                                    dve.wait_ge(down, j)
                                dve.tensor_copy(hT[:, v, :], psum[:, 4 + v, :]).then_inc(hid_c, 1)

                        multiply(0, True)
                        copy_hidden(0, True)
                        with dve.Fori(1, tiles) as j:
                            multiply(j, False)
                            copy_hidden(j, False)

        def as_tokens(feat):
            return feat[:].rearrange("p k t -> p (k t)").rearrange("p (i d) -> p i d", d=D)

        def stage_l0_route(own, rows):
            E = E0
            wr = sb("r0_w", [P, KD, E], on=own)
            L = sb("r0_L", [P, NT, E], on=own)
            tmp = sb("r0_tmp", [P, NT, E], on=own)
            onehot = sb("r0_oh", [P, NT, E], on=own)
            top = sb("r0_top", [P, NT], on=own)
            small = sb("r0_small", [P, NT], on=own)
            loaded, done, order, toped, score = (sem("r0_" + n) for n in ("loaded", "done", "order", "toped", "score"))
            with nc.Block() as block:
                @block.sync
                def _(sp):
                    sp.dma_start(wr[:], a["l0_gate"]).then_inc(loaded, 16)

                @block.tensor
                def _(pe):
                    pe.wait_ge(loaded, 16)
                    logits_on_pe(pe, fc, wr, E).then_inc(done, 1)

                @block.scalar
                def _(act):
                    act.wait_ge(toped, 1)
                    act.activation(small[:], top[:], ACT.Sigmoid).then_inc(score, 1)

                @block.vector
                def _(dve):
                    link = chain(dve, order)
                    dve.wait_ge(done, 1)
                    link(dve.tensor_copy(L[:].rearrange("p i e -> p (i e)"), psum[:, 0, 0:NT * E]))
                    pick(dve, link, L[:], top[:], onehot[:], tmp[:], small[:], E)
                    dve.engine_nop().then_inc(toped, 1)
                    dve.wait_ge(score, 1)
                    for i in range(NT):
                        dve.tensor_scalar(rows[:, i, :], ctok[:, i, :], small[:, i:i + 1], None, ALU.mult)
            return onehot

        def stage_add_to_x(tag, terms):
            order = sem(tag + "_order")
            with nc.Block() as block:
                @block.vector
                def _(dve):
                    link = chain(dve, order)
                    for buf, factor in terms:
                        if isinstance(factor, float):
                            link(dve.scalar_tensor_tensor(
                                out=xtok[:].rearrange("p i d -> p (i d)"), in0=buf.rearrange("p i d -> p (i d)"),
                                scalar=factor, in1=xtok[:].rearrange("p i d -> p (i d)"), op0=ALU.mult, op1=ALU.add))
                        else:
                            for i in range(NT):
                                ins = dve.scalar_tensor_tensor(out=xtok[:, i, :], in0=buf[:, i, :],
                                                               scalar=factor[:, i:i + 1], in1=xtok[:, i, :],
                                                               op0=ALU.mult, op1=ALU.add)
                            link(ins)

        def layer0():
            stage_to_features("a0", xtok, fx)
            stage_l0_cond()
            stage_to_tokens("b0", fc, ctok)
            with ExitStack() as own:
                slots = sb("slots0", [P, NT], U32, on=own)
                tile_expert = sb("tile_expert0", [1, SLOT_TILES0], I32, on=own)
                rows = as_tokens(fx)
                with ExitStack() as route:
                    onehot = stage_l0_route(route, rows)
                    stage_slots("s0", [onehot], E0, SLOT_TILES0, slots, tile_expert)
                stage_scatter("sc0", rows, rows0_in, slots, 1)
                stage_glu("g0", fc, a["l0_shared"])
                stage_sorted_glu("e0", SLOT_TILES0, 1, a["l0_routed"], tile_expert, rows0_in, rows0_out)
                stage_gather("ga0", rows0_out, slots, [rows])
                stage_add_to_x("x0", [(acc[:], 1.0), (rows, 1.0)])

        def stage_l1_project(w5, U):
            q = acc[:].rearrange("p i d -> p (i d)").rearrange("p (o t) -> p o t", o=KD)
            WQ, WK, WV, WT = 0, 1, 2, 3
            with ExitStack() as own:
                tp = sb("l1_tp", [P, KD, B], on=own)
                hm = sb("l1_headmask", [P, 8, HW], on=own)
                bd = sb("l1_bd", [P, KD, B, P], on=own)
                part = sb("l1_part", [P, KD, B, 2], on=own)
                junk = sb("l1_junk", [P, CH], on=own)
                qmod = sb("l1_qmod", [P, KD, B], on=own)
                qm = sb("l1_qm", [P, KD, B, HEADS], on=own)
                masks, hm1, loaded, tpd, qd, qc, vd, vc, order, ad, asum, qmd, ud = (
                    sem("l1p_" + n) for n in ("masks", "hm1", "loaded", "tpd", "qd", "qc", "vd", "vc", "order", "ad",
                                              "asum", "qmd", "ud"))
                with nc.Block() as block:
                    @block.sync
                    def _(sp):
                        sp.dma_start(w5[:], a["l1_w"]).then_inc(loaded, 16)

                    @block.gpsimd
                    def _(pool):
                        full = ones[:].rearrange("p (h e) -> p h e", h=8)
                        pool.affine_select(out=hm[:], in_=full, compare_op=ALU.is_ge, fill=0.0, base=0,
                                           pattern=[[-HW, 8], [0, HW]], channel_multiplier=1).then_inc(hm1, 1)
                        pool.wait_ge(hm1, 1)
                        pool.affine_select(out=hm[:], in_=hm[:], compare_op=ALU.is_ge, fill=0.0, base=HW - 1,
                                           pattern=[[HW, 8], [0, HW]], channel_multiplier=-1).then_inc(masks, 1)

                    @block.tensor
                    def _(pe):
                        pe.wait_ge(loaded, 16)
                        for o in range(KD):
                            for k in range(KD):
                                last = pe.matmul(psum[:, 7, o * B:(o + 1) * B], w5[:, WT, k, o * P:(o + 1) * P],
                                                 condT[:, k, :], start=(k == 0), stop=(k == KD - 1))
                        last.then_inc(tpd, 1)
                        for n in range(8):
                            o, c = n // NCH, n % NCH
                            if n >= 4:
                                pe.wait_ge(qc, n - 3)
                            for k in range(KD):
                                last = pe.matmul(psum[:, n % 4, :], w5[:, WQ, k, o * P:(o + 1) * P],
                                                 fx[:, k, c * CH:(c + 1) * CH], start=(k == 0), stop=(k == KD - 1))
                            last.then_inc(qd, 1)
                        for n in range(8):
                            if n >= 2:
                                pe.wait_ge(vc, n - 1)
                            for i in range(2):
                                for k in range(KD):
                                    last = pe.matmul(psum[:, 4 + n % 2, i * D:(i + 1) * D],
                                                     fx[:, k, (2 * n + i) * P:(2 * n + i + 1) * P], w5[:, WV, k, :],
                                                     start=(k == 0), stop=(k == KD - 1))
                            last.then_inc(vd, 1)
                        pe.wait_ge(order, 1)
                        pe.wait_ge(qc, 8)
                        for n in range(8):
                            o, b, c = n // 4, n // 2 % 2, n % 2
                            if n >= 4:
                                pe.wait_ge(asum, n - 3)
                            last = pe.matmul(psum[:, n % 4, :], bd[:, o, b, :],
                                             q[:, o, b * S + c * CH:b * S + (c + 1) * CH], start=True, stop=True)
                            last.then_inc(ad, 1)
                        pe.wait_ge(qmd, 1)
                        for d in range(KD):
                            for b in range(B):
                                for o in range(KD):
                                    g = (d * B + b) * HEADS
                                    last = pe.matmul(psum[:, 7, g:g + HEADS], w5[:, WK, o, d * P:(d + 1) * P],
                                                     qm[:, o, b, :], start=(o == 0), stop=(o == KD - 1))
                        last.then_inc(ud, 1)

                    @block.scalar
                    def _(act):
                        for n in range(8):
                            act.wait_ge(qd, n + 1)
                            act.copy(q[:, n // NCH, n % NCH * CH:(n % NCH + 1) * CH], psum[:, n % 4, :]).then_inc(qc, 1)

                    @block.vector
                    def _(dve):
                        dve.memset(qm[:], 0.0)
                        dve.wait_ge(tpd, 1)
                        dve.tensor_copy(tp[:].rearrange("p o b -> p (o b)"), psum[:, 7, 0:KD * B]).then_inc(masks, 1)
                        dve.wait_ge(masks, 2)
                        for o in range(KD):
                            for b in range(B):
                                last = dve.tensor_scalar(bd[:, o, b, :], hm[:].rearrange("p h e -> p (h e)"),
                                                         tp[:, o, b:b + 1], None, ALU.mult)
                        last.then_inc(order, 1)
                        for n in range(8):
                            dve.wait_ge(vd, n + 1)
                            dve.tensor_copy(ctok[:, 2 * n:2 * n + 2, :].rearrange("p i d -> p (i d)"),
                                            psum[:, 4 + n % 2, :]).then_inc(vc, 1)
                        for n in range(8):
                            o, b, c = n // 4, n // 2 % 2, n % 2
                            dve.wait_ge(ad, n + 1)
                            if n:
                                dve.wait_ge(asum, n)
                            dve.tensor_tensor_reduce(junk[:], q[:, o, b * S + c * CH:b * S + (c + 1) * CH],
                                                     psum[:, n % 4, :], 1.0, 0.0, ALU.mult, ALU.add,
                                                     part[:, o, b, c:c + 1]).then_inc(asum, 1)
                        dve.wait_ge(asum, 8)
                        dve.tensor_tensor(qmod[:], part[:, :, :, 0], part[:, :, :, 1], ALU.add).then_inc(order, 1)
                        dve.wait_ge(order, 2)
                        for o in range(KD):
                            for b in range(B):
                                last = dve.tensor_scalar(qm[:, o, b, o * 8:(o + 1) * 8], hm[:, :, 0],
                                                         qmod[:, o, b:b + 1], float(HW) ** -0.5, ALU.mult, ALU.mult)
                        last.then_inc(qmd, 1)
                        dve.wait_ge(ud, 1)
                        dve.tensor_copy(U[:].rearrange("p d b h -> p (d b h)"), psum[:, 7, 0:KD * B * HEADS])

        def stage_l1_attend(U):
            with ExitStack() as own:
                m8 = sb("l1_m8", [P, TPB, S], U8, on=own)
                lim = sb("l1_lim", [P, TPB, S], on=own)
                ub = sb("l1_ub", [P, KD, P], on=own)
                row = sb("l1_row", [P, S], on=own)
                ms = sb("l1_ms", [P, 2, S], on=own)
                pT = sb("l1_pT", [P, S], on=own)
                mx = sb("l1_mx", [P, TPB], on=own)
                spare = sb("l1_spare", [P, 1], on=own)
                sums = sb("l1_sums", [P, TPB], on=own)
                rs = sb("l1_rs", [P, TPB], on=own)
                loaded, lims, ubd, sd, rowc, masked, negd, expd, td, tcv, tca, pvd, rsd, od = (
                    sem("l1a_" + n) for n in ("loaded", "lims", "ubd", "sd", "rowc", "masked", "negd", "expd", "td",
                                              "tcv", "tca", "pvd", "rsd", "od"))
                half = S // 2
                with nc.Block() as block:
                    @block.sync
                    def _(sp):
                        sp.dma_start(m8[:], a["mask"].rearrange("(i p) s -> p i s", p=P)).then_inc(loaded, 16)

                    def heads(eng, body):
                        body(0, 0, 0, True)
                        with eng.Fori(1, HEADS) as h:
                            body(0, h, h, False)
                        with eng.Fori(0, HEADS) as h:
                            body(1, h, h + HEADS, False)

                    @block.tensor
                    def _(pe):
                        def body(b, h, g, first):
                            pe.wait_ge(ubd, g + 1)
                            if not first:
                                pe.wait_ge(rowc, g)
                            for c in range(2):
                                for k in range(KD):
                                    last = pe.matmul(psum[:, c, :], ub[:, k, :],
                                                     fx[:, k, b * S + c * CH:b * S + (c + 1) * CH],
                                                     start=(k == 0), stop=(k == KD - 1))
                            last.then_inc(sd, 1)
                            for i in range(TPB):
                                pe.wait_ge(expd, TPB * g + i + 1)
                                if not (first and i == 0):
                                    pe.wait_ge(tcv, TPB * g + i)
                                    pe.wait_ge(tca, TPB * g + i)
                                for s in range(8):
                                    last = pe.transpose(psum[:, 2 + s // 4, (s % 4) * P:(s % 4 + 1) * P],
                                                        ms[:, i % 2, s * P:(s + 1) * P], ident[:])
                                last.then_inc(td, 1)
                                pe.wait_ge(tcv, TPB * g + i + 1)
                                pe.wait_ge(tca, TPB * g + i + 1)
                                if i == 0 and not first:
                                    pe.wait_ge(od, g)
                                for s in range(8):
                                    last = pe.matmul(psum[:, 6, i * HW:(i + 1) * HW], pT[:, s * P:(s + 1) * P],
                                                     ctok[:, b * TPB + s, bass.ds(h * HW, HW)],
                                                     start=(s == 0), stop=(s == 7))
                                last.then_inc(pvd, 1)
                        heads(pe, body)

                    @block.scalar
                    def _(act):
                        def body(b, h, g, first):
                            act.wait_ge(sd, g + 1)
                            if not first:
                                act.wait_ge(masked, TPB * g)
                            act.copy(row[:], psum[:, 0:2, :].rearrange("p c t -> p (c t)")).then_inc(rowc, 1)
                            for i in range(TPB):
                                act.wait_ge(negd, TPB * g + i + 1)
                                if i == 0 and not first:
                                    act.wait_ge(rsd, g)
                                act.activation(ms[:, i % 2, :], ms[:, i % 2, :], ACT.Exp, bias=mx[:, i:i + 1],
                                               accum_out=sums[:, i:i + 1]).then_inc(expd, 1)
                                act.wait_ge(td, TPB * g + i + 1)
                                if not (first and i == 0):
                                    act.wait_ge(pvd, TPB * g + i)
                                act.copy(pT[:, half:S], psum[:, 3, :]).then_inc(tca, 1)
                        heads(act, body)

                    @block.vector
                    def _(dve):
                        dve.wait_ge(loaded, 16)
                        dve.tensor_scalar(lim[:], m8[:], FMAX, -FMAX, ALU.mult, ALU.add).then_inc(lims, 1)
                        dve.wait_ge(lims, 1)

                        def body(b, h, g, first):
                            if not first:
                                dve.wait_ge(sd, g)
                            dve.tensor_copy(ub[:], U[:, :, b, bass.ds(h, 1)].to_broadcast([P, KD, P])).then_inc(ubd, 1)
                            for i in range(TPB):
                                if i == 0:
                                    dve.wait_ge(rowc, g + 1)
                                if not (first and i < 2):
                                    dve.wait_ge(td, TPB * g + i - 1)
                                    if i < 2:
                                        dve.wait_ge(expd, TPB * g)
                                dve.memset(spare[:], 0.0)
                                dve.tensor_tensor_reduce(ms[:, i % 2, :], row[:], lim[:, i, :], 1.0, -FMAX, ALU.add,
                                                         ALU.max, mx[:, i:i + 1]).then_inc(masked, 1)
                                dve.wait_ge(masked, TPB * g + i + 1)
                                dve.tensor_scalar(mx[:, i:i + 1], mx[:, i:i + 1], -1.0, None, ALU.mult).then_inc(negd, 1)
                                if i >= 1:
                                    transposed(g, i - 1, first)
                            transposed(g, TPB - 1, first)
                            dve.wait_ge(expd, TPB * g + TPB)
                            dve.reciprocal(rs[:], sums[:]).then_inc(rsd, 1)
                            dve.wait_ge(rsd, g + 1)
                            dve.wait_ge(pvd, TPB * g + TPB)
                            dve.tensor_tensor(acc[:, b * TPB:(b + 1) * TPB, bass.ds(h * HW, HW)],
                                              psum[:, 6, 0:TPB * HW].rearrange("p (i e) -> p i e", e=HW),
                                              rs[:].unsqueeze(2).to_broadcast([P, TPB, HW]), ALU.mult).then_inc(od, 1)

                        def transposed(g, i, first):
                            dve.wait_ge(td, TPB * g + i + 1)
                            if not (first and i == 0):
                                dve.wait_ge(pvd, TPB * g + i)
                            dve.tensor_copy(pT[:, 0:half], psum[:, 2, :]).then_inc(tcv, 1)
                        heads(dve, body)

        def stage_rows_times(tag, feat, w, tok):
            done, copied = sem(tag + "_done"), sem(tag + "_copied")
            with nc.Block() as block:
                @block.tensor
                def _(pe):
                    for n in range(8):
                        if n >= 4:
                            pe.wait_ge(copied, n - 3)
                        for i in range(2):
                            for k in range(KD):
                                last = pe.matmul(psum[:, n % 4, i * D:(i + 1) * D],
                                                 feat[:, k, (2 * n + i) * P:(2 * n + i + 1) * P], w[:, k, :],
                                                 start=(k == 0), stop=(k == KD - 1))
                        last.then_inc(done, 1)

                @block.vector
                def _(dve):
                    for n in range(8):
                        dve.wait_ge(done, n + 1)
                        dve.tensor_copy(tok[:, 2 * n:2 * n + 2, :].rearrange("p i d -> p (i d)"),
                                        psum[:, n % 4, :]).then_inc(copied, 1)

        def stage_l1_gating(rw):
            E = E1
            with ExitStack() as own:
                sim = sb("g1_sim", [P, KD, E], on=own)
                sim2 = sb("g1_sim2", [P, KD, E], on=own)
                gb = sb("g1_gb", [P, E], on=own)
                ns = sb("g1_ns", [P, E], on=own)
                ss = sb("g1_ss", [P, NT], on=own)
                junk = sb("g1_junk", [P, D], on=own)
                L, tmp, oh1, oh2, gated = (sb("g1_" + n, [P, NT, E], on=own) for n in ("L", "tmp", "oh1", "oh2", "gated"))
                top, small = (sb("g1_" + n, [P, NT], on=own) for n in ("top", "small"))
                loaded, sq, done, order, roots, rooted, shifted, expd = (
                    sem("g1_" + n) for n in ("loaded", "sq", "done", "order", "roots", "rooted", "shifted", "expd"))
                with nc.Block() as block:
                    @block.sync
                    def _(sp):
                        sp.dma_start(sim[:], a["l1_sim"]).then_inc(loaded, 16)
                        sp.dma_start(gb[:], a["l1_gates"].partition_broadcast(P)).then_inc(loaded, 16)

                    @block.tensor
                    def _(pe):
                        pe.wait_ge(loaded, 32)
                        logits_on_pe(pe, fc, sim, E)
                        pe.wait_ge(sq, 1)
                        for k in range(KD):
                            last = pe.matmul(psum[:, 1, 0:E], ones[:], sim2[:, k, :], start=(k == 0), stop=(k == KD - 1))
                        last.then_inc(done, 1)

                    @block.scalar
                    def _(act):
                        act.wait_ge(loaded, 32)
                        act.activation(gb[:], gb[:], ACT.Sigmoid).then_inc(rooted, 1)
                        act.wait_ge(roots, 1)
                        act.activation(ns[:], ns[:], ACT.Sqrt)
                        act.activation(ss[:], ss[:], ACT.Sqrt).then_inc(rooted, 1)
                        act.wait_ge(shifted, 1)
                        act.activation(tmp[:], tmp[:], ACT.Exp).then_inc(expd, 1)

                    @block.vector
                    def _(dve):
                        link = chain(dve, order)
                        dve.wait_ge(loaded, 32)
                        dve.tensor_tensor(sim2[:], sim[:], sim[:], ALU.mult).then_inc(sq, 1)
                        for i in range(NT):
                            link(dve.tensor_tensor_reduce(junk[:], ctok[:, i, :], ctok[:, i, :], 1.0, 0.0, ALU.mult,
                                                          ALU.add, ss[:, i:i + 1]))
                        link(dve.tensor_scalar(ss[:], ss[:], 1e-12, None, ALU.add))
                        dve.wait_ge(done, 1)
                        dve.tensor_scalar(ns[:], psum[:, 1, 0:E], 1e-12, None, ALU.add).then_inc(roots, 1)
                        dve.wait_ge(rooted, 2)
                        link(dve.reciprocal(ns[:], ns[:]))
                        link(dve.reciprocal(ss[:], ss[:]))
                        link(dve.tensor_tensor(L[:], psum[:, 0, 0:NT * E].rearrange("p (i e) -> p i e", e=E),
                                               over_e(ss[:], E), ALU.mult))
                        link(dve.tensor_tensor(L[:], L[:], ns[:].unsqueeze(1).to_broadcast([P, NT, E]), ALU.mult))
                        link(dve.tensor_tensor(L[:], L[:], gb[:].unsqueeze(1).to_broadcast([P, NT, E]), ALU.subtract))
                        pick(dve, link, L[:], top[:], oh1[:], tmp[:], small[:], E)
                        link(dve.scalar_tensor_tensor(out=gated[:], in0=oh1[:], scalar=-1e30, in1=L[:],
                                                      op0=ALU.mult, op1=ALU.add))
                        pick(dve, link, gated[:], small[:], oh2[:], tmp[:], top[:], E)
                        link(dve.tensor_tensor(oh1[:], oh1[:], oh2[:], ALU.add))
                        link(dve.tensor_scalar(gated[:], L[:], 0.0, None, ALU.max))
                        link(dve.tensor_scalar(L[:], gated[:], 0.0, None, ALU.is_gt))
                        link(dve.tensor_reduce(small[:], L[:], AX_X, ALU.max))
                        link(dve.tensor_scalar(small[:], small[:], 0.0, None, ALU.is_equal))
                        link(dve.tensor_tensor(oh1[:], oh1[:], over_e(small[:], E), ALU.mult))
                        link(dve.tensor_tensor(L[:], L[:], oh1[:], ALU.add))
                        link(dve.tensor_reduce(top[:], gated[:], AX_X, ALU.max))
                        dve.tensor_tensor(tmp[:], gated[:], over_e(top[:], E), ALU.subtract).then_inc(shifted, 1)
                        dve.wait_ge(expd, 1)
                        link(dve.tensor_tensor(tmp[:], tmp[:], L[:], ALU.mult))
                        link(dve.tensor_reduce(small[:], tmp[:], AX_X, ALU.add))
                        link(dve.reciprocal(small[:], small[:]))
                        dve.tensor_tensor(rw[:], tmp[:], over_e(small[:], E), ALU.mult)

        def stage_l1_qkv(rw, qkv):
            C3 = 3 * H1
            w = wbuf[:].rearrange("p r n -> p (r n)").rearrange("p (e k c) -> p e k c", e=E1, k=KD)
            loaded, cleared, done, added = (sem("q1_" + n) for n in ("loaded", "cleared", "done", "added"))
            with nc.Block() as block:
                @block.sync
                def _(sp):
                    sp.dma_start(w, a["l1_qkv"]).then_inc(loaded, 16)

                @block.tensor
                def _(pe):
                    def expert(e, first):
                        for i in range(NT):
                            if not (first and i < 4):
                                pe.wait_ge(added, NT * e + i - 3)
                            for k in range(KD):
                                last = pe.matmul(psum[:, i % 4, 0:C3], fc[:, k, i * P:(i + 1) * P],
                                                 w[:, bass.ds(e, 1), k, :].rearrange("p e c -> p (e c)"),
                                                 start=(k == 0), stop=(k == KD - 1))
                            last.then_inc(done, 1)
                    pe.wait_ge(loaded, 16)
                    expert(0, True)
                    with pe.Fori(1, E1) as e:
                        expert(e, False)

                @block.vector
                def _(dve):
                    dve.memset(qkv[:], 0.0).then_inc(cleared, 1)
                    dve.wait_ge(cleared, 1)

                    def expert(e, first):
                        for i in range(NT):
                            dve.wait_ge(done, NT * e + i + 1)
                            if not first:
                                dve.wait_ge(added, NT * (e - 1) + i + 1)
                            dve.scalar_tensor_tensor(out=qkv[:, i, :], in0=psum[:, i % 4, 0:C3],
                                                     scalar=rw[:, i, bass.ds(e, 1)], in1=qkv[:, i, :],
                                                     op0=ALU.mult, op1=ALU.add).then_inc(added, 1)
                    expert(0, True)
                    with dve.Fori(1, E1) as e:
                        expert(e, False)

        def stage_l1_causal(qkv, aoT, rinv):
            qk = acc[:].rearrange("p i d -> p (i d)").rearrange("p (o t) -> p o t", o=2)
            scale = float(H1) ** -0.5
            with ExitStack() as own:
                cm = sb("c1_cm", [P, P], on=own)
                zero = sb("c1_zero", [P, P], on=own)
                sm = sb("c1_sm", [P, 2, S], on=own)
                pT = sb("c1_pT", [P, 2, S], on=own)
                mx = sb("c1_mx", [P, NT], on=own)
                sums = sb("c1_sums", [P, NT], on=own)
                cleared, cmd, td, tc, sd, scaled, sc2, maxd, negd, expd, ptd, ptc, pvd, pvc = (
                    sem("c1_" + n) for n in ("cleared", "cmd", "td", "tc", "sd", "scaled", "sc2", "maxd", "negd", "expd",
                                             "ptd", "ptc", "pvd", "pvc"))
                with nc.Block() as block:
                    @block.gpsimd
                    def _(pool):
                        pool.memset(zero[:], 0.0).then_inc(cleared, 1)
                        pool.wait_ge(cleared, 1)
                        pool.affine_select(out=cm[:], in_=zero[:], compare_op=ALU.is_ge, fill=-FMAX, base=0,
                                           pattern=[[-1, P]], channel_multiplier=1).then_inc(cmd, 1)

                    @block.tensor
                    def _(pe):
                        for n in range(8):
                            o, c = n // NCH, n % NCH
                            if n >= 2:
                                pe.wait_ge(tc, n - 1)
                            for t in range(TPC):
                                last = pe.transpose(psum[:, n % 2, t * P:(t + 1) * P],
                                                    qkv[:, c * TPC + t, o * H1:(o + 1) * H1], ident[:])
                            last.then_inc(td, 1)
                        pe.wait_ge(tc, 8)

                        def scores(n):
                            b, i = n // TPB, n % TPB
                            if n >= 1:
                                pe.wait_ge(sc2, n)
                            for c in range(i // TPC + 1):
                                w = min(CH, (i + 1) * P - c * CH)
                                last = pe.matmul(psum[:, c, 0:w], qk[:, 0, n * P:(n + 1) * P],
                                                 qk[:, 1, b * S + c * CH:b * S + c * CH + w], start=True, stop=True)
                            last.then_inc(sd, 1)

                        scores(0)
                        for n in range(NT):
                            b, i = n // TPB, n % TPB
                            if n + 1 < NT:
                                scores(n + 1)
                            pe.wait_ge(expd, n + 1)
                            if n >= 1:
                                pe.wait_ge(ptc, n)
                            for s in range(i + 1):
                                last = pe.transpose(psum[:, 2 + s // TPC, (s % TPC) * P:(s % TPC + 1) * P],
                                                    sm[:, n % 2, s * P:(s + 1) * P], ident[:])
                            last.then_inc(ptd, 1)
                            pe.wait_ge(ptc, n + 1)
                            if n >= 2:
                                pe.wait_ge(pvc, n - 1)
                            for s in range(i + 1):
                                last = pe.matmul(psum[:, 4 + n % 2, 0:P], qkv[:, b * TPB + s, 2 * H1:3 * H1],
                                                 pT[:, n % 2, s * P:(s + 1) * P], start=(s == 0), stop=(s == i))
                            last.then_inc(pvd, 1)

                    @block.scalar
                    def _(act):
                        for n in range(8):
                            act.wait_ge(td, n + 1)
                            act.copy(qk[:, n // NCH, n % NCH * CH:(n % NCH + 1) * CH], psum[:, n % 2, :]).then_inc(tc, 1)
                        for n in range(NT):
                            w = (n % TPB + 1) * P
                            act.wait_ge(negd, n + 1)
                            act.activation(sm[:, n % 2, 0:w], sm[:, n % 2, 0:w], ACT.Exp, bias=mx[:, n:n + 1],
                                           accum_out=sums[:, n:n + 1]).then_inc(expd, 1)
                            act.wait_ge(pvd, n + 1)
                            act.copy(aoT[:, n * P:(n + 1) * P], psum[:, 4 + n % 2, 0:P]).then_inc(pvc, 1)

                    @block.vector
                    def _(dve):
                        dve.wait_ge(cmd, 1)

                        def softmax_rows(n):
                            i = n % TPB
                            w = (i + 1) * P
                            dve.wait_ge(sd, n + 1)
                            if n >= 2:
                                dve.wait_ge(ptd, n - 1)
                            flat = psum[:, 0:2, :].rearrange("p c t -> p (c t)")
                            if i:
                                dve.tensor_scalar(sm[:, n % 2, 0:w - P], flat[:, 0:w - P], scale, None, ALU.mult)
                            dve.scalar_tensor_tensor(out=sm[:, n % 2, w - P:w], in0=flat[:, w - P:w], scalar=scale,
                                                     in1=cm[:], op0=ALU.mult, op1=ALU.add).then_inc(sc2, 1)
                            dve.wait_ge(sc2, n + 1)
                            dve.tensor_reduce(mx[:, n:n + 1], sm[:, n % 2, 0:w], AX_X, ALU.max).then_inc(maxd, 1)
                            dve.wait_ge(maxd, n + 1)
                            dve.tensor_scalar(mx[:, n:n + 1], mx[:, n:n + 1], -1.0, None, ALU.mult).then_inc(negd, 1)

                        softmax_rows(0)
                        for n in range(NT):
                            if n + 1 < NT:
                                softmax_rows(n + 1)
                            w = (n % TPB + 1) * P
                            dve.wait_ge(ptd, n + 1)
                            if n >= 2:
                                dve.wait_ge(pvd, n - 1)
                            dve.tensor_copy(pT[:, n % 2, 0:w], psum[:, 2:4, :].rearrange("p c t -> p (c t)")[:, 0:w]
                                            ).then_inc(ptc, 1)
                        dve.wait_ge(expd, NT)
                        dve.reciprocal(rinv[:], sums[:])

        def stage_l1_out(rw, rinv, aoT):
            w = wbuf[:, 0, 0:E1 * D].rearrange("p (e c) -> p e c", c=D)
            loaded, ready, done, added = (sem("o1_" + n) for n in ("loaded", "ready", "done", "added"))
            with nc.Block() as block:
                @block.sync
                def _(sp):
                    sp.dma_start(w, a["l1_o"]).then_inc(loaded, 16)

                @block.tensor
                def _(pe):
                    def expert(e, first):
                        for i in range(NT):
                            if not (first and i < 4):
                                pe.wait_ge(added, NT * e + i - 3)
                            pe.matmul(psum[:, i % 4, 0:D], aoT[:, i * P:(i + 1) * P],
                                      w[:, bass.ds(e, 1), :].rearrange("p e c -> p (e c)"),
                                      start=True, stop=True).then_inc(done, 1)
                    pe.wait_ge(loaded, 16)
                    expert(0, True)
                    with pe.Fori(1, E1) as e:
                        expert(e, False)

                @block.vector
                def _(dve):
                    dve.tensor_tensor(rw[:], rw[:], over_e(rinv[:], E1), ALU.mult).then_inc(ready, 1)
                    dve.wait_ge(ready, 1)

                    def expert(e, first):
                        for i in range(NT):
                            dve.wait_ge(done, NT * e + i + 1)
                            if not first:
                                dve.wait_ge(added, NT * (e - 1) + i + 1)
                            dve.scalar_tensor_tensor(out=xtok[:, i, :], in0=psum[:, i % 4, 0:D],
                                                     scalar=rw[:, i, bass.ds(e, 1)], in1=xtok[:, i, :],
                                                     op0=ALU.mult, op1=ALU.add).then_inc(added, 1)
                    expert(0, True)
                    with dve.Fori(1, E1) as e:
                        expert(e, False)

        def layer1():
            stage_to_features("a1", xtok, fx)
            with ExitStack() as own:
                w5 = sb("l1_w5", [P, 5, KD, D], on=own)
                U = sb("l1_U", [P, KD, B, HEADS], on=own)
                stage_l1_project(w5, U)
                stage_l1_attend(U)
                stage_to_features("o1", acc, fc)
                stage_rows_times("w1", fc, w5[:, 4, :, :], ctok)
            stage_to_features("b1", ctok, fc)
            with ExitStack() as own:
                rw = sb("l1_rw", [P, NT, E1], on=own)
                rinv = sb("l1_rinv", [P, NT], on=own)
                qkv = sb("l1_qkv", [P, NT, 3 * H1], on=own)
                aoT = fx[:, 0, :]
                stage_l1_gating(rw)
                stage_l1_qkv(rw, qkv)
                stage_l1_causal(qkv, aoT, rinv)
                stage_l1_out(rw, rinv, aoT)

        def stage_sigmoid_top2(tag, router, bias, gates):
            E = E2
            with ExitStack() as own:
                wr = sb(tag + "_w", [P, 2 * KD, E], on=own)
                bb = sb(tag + "_b", [P, E], on=own)
                cb = sb(tag + "_cb", [P, KD, B, P], on=own)
                s, sel, tmp, oh1, oh2 = (sb(f"{tag}_{n}", [P, NT, E], on=own) for n in ("s", "sel", "tmp", "oh1", "oh2"))
                top, small, good = (sb(f"{tag}_{n}", [P, NT], on=own) for n in ("top", "small", "good"))
                loaded, spread, done, sig, order = (sem(f"{tag}_{n}") for n in ("loaded", "spread", "done", "sig", "order"))
                with nc.Block() as block:
                    @block.sync
                    def _(sp):
                        sp.dma_start(wr[:], router).then_inc(loaded, 16)
                        sp.dma_start(bb[:], bias.partition_broadcast(P)).then_inc(loaded, 16)

                    @block.tensor
                    def _(pe):
                        pe.wait_ge(loaded, 32)
                        pe.wait_ge(spread, 1)
                        logits_on_pe(pe, fx, wr, E, extra=cb).then_inc(done, 1)

                    @block.scalar
                    def _(act):
                        act.wait_ge(done, 1)
                        act.activation(s[:].rearrange("p i e -> p (i e)"), psum[:, 0, 0:NT * E], ACT.Sigmoid).then_inc(sig, 1)

                    @block.vector
                    def _(dve):
                        link = chain(dve, order)
                        dve.tensor_copy(cb[:], condT[:].unsqueeze(3).to_broadcast([P, KD, B, P])).then_inc(spread, 1)
                        dve.wait_ge(loaded, 32)
                        dve.wait_ge(sig, 1)
                        link(dve.tensor_tensor(sel[:], s[:], bb[:].unsqueeze(1).to_broadcast([P, NT, E]), ALU.add))
                        pick(dve, link, sel[:], top[:], oh1[:], tmp[:], small[:], E)
                        link(dve.scalar_tensor_tensor(out=sel[:], in0=oh1[:], scalar=-1e30, in1=sel[:],
                                                      op0=ALU.mult, op1=ALU.add))
                        pick(dve, link, sel[:], top[:], oh2[:], tmp[:], small[:], E)
                        link(dve.tensor_tensor(oh1[:], oh1[:], oh2[:], ALU.add))
                        link(dve.tensor_tensor(tmp[:], s[:], oh1[:], ALU.mult))
                        link(dve.tensor_reduce(top[:], tmp[:], AX_X, ALU.add))
                        link(dve.tensor_scalar(good[:], top[:], 1e-9, None, ALU.is_gt))
                        link(dve.tensor_scalar(top[:], top[:], 1e-9, None, ALU.add))
                        link(dve.reciprocal(top[:], top[:]))
                        link(dve.tensor_tensor(top[:], top[:], good[:], ALU.mult))
                        link(dve.tensor_scalar(good[:], good[:], -0.5, 0.5, ALU.mult, ALU.add))
                        link(dve.tensor_tensor(tmp[:], tmp[:], over_e(top[:], E), ALU.mult))
                        link(dve.tensor_tensor(oh1[:], oh1[:], over_e(good[:], E), ALU.mult))
                        dve.tensor_tensor(gates[:], tmp[:], oh1[:], ALU.add)

        def stage_softmax_route(tag, own, E, router, picks):
            wr = sb(tag + "_w", [P, KD, E], on=own)
            pr, tmp = (sb(f"{tag}_{n}", [P, NT, E], on=own) for n in ("pr", "tmp"))
            ohs = [sb(f"{tag}_oh{n}", [P, NT, E], on=own) for n in range(picks)]
            tops = [sb(f"{tag}_top{n}", [P, NT], on=own) for n in range(picks)]
            small = sb(tag + "_small", [P, NT], on=own)
            loaded, done, shifted, expd, order = (sem(f"{tag}_{n}") for n in ("loaded", "done", "shifted", "expd", "order"))
            with nc.Block() as block:
                @block.sync
                def _(sp):
                    sp.dma_start(wr[:], router).then_inc(loaded, 16)

                @block.tensor
                def _(pe):
                    pe.wait_ge(loaded, 16)
                    logits_on_pe(pe, fc, wr, E).then_inc(done, 1)

                @block.scalar
                def _(act):
                    act.wait_ge(shifted, 1)
                    act.activation(pr[:], pr[:], ACT.Exp).then_inc(expd, 1)

                @block.vector
                def _(dve):
                    link = chain(dve, order)
                    dve.wait_ge(done, 1)
                    link(dve.tensor_copy(tmp[:].rearrange("p i e -> p (i e)"), psum[:, 0, 0:NT * E]))
                    link(dve.tensor_reduce(small[:], tmp[:], AX_X, ALU.max))
                    dve.tensor_tensor(pr[:], tmp[:], over_e(small[:], E), ALU.subtract).then_inc(shifted, 1)
                    dve.wait_ge(expd, 1)
                    link(dve.tensor_reduce(small[:], pr[:], AX_X, ALU.add))
                    link(dve.reciprocal(small[:], small[:]))
                    link(dve.tensor_tensor(pr[:], pr[:], over_e(small[:], E), ALU.mult))
                    for n in range(picks):
                        pick(dve, link, pr[:], tops[n][:], ohs[n][:], tmp[:], small[:], E)
                        if n + 1 < picks:
                            link(dve.scalar_tensor_tensor(out=pr[:], in0=ohs[n][:], scalar=-BIG, in1=pr[:],
                                                          op0=ALU.mult, op1=ALU.add))
            return ohs, tops

        def layer2():
            stage_to_features("a2", xtok, fx)
            with ExitStack() as own:
                gates = sb("gates2", [P, NT, E2], on=own)
                stage_sigmoid_top2("t2", a["l2_router"], a["l2_bias"], gates)
                stage_glu("g2", fx, a["l2c_shared"])
                stage_gelu_experts("x2", fx, a["l2c_routed"], gates, 0.5, 0.25)
            stage_to_features("b2", ctok, fc)
            with ExitStack() as own:
                slots = sb("slots2", [P, 2 * NT], U32, on=own)
                tile_expert = sb("tile_expert2", [1, SLOT_TILES2], I32, on=own)
                halves = [sb(f"half_top{n}", [P, NT], on=own) for n in range(2)]
                with ExitStack() as route:
                    ohs, tops = stage_softmax_route("r2", route, E2, a["l2_gate"], 2)
                    with nc.Block() as block:
                        @block.vector
                        def _(dve):
                            for n in range(2):
                                dve.tensor_scalar(halves[n][:], tops[n][:], 0.5, None, ALU.mult)
                    stage_slots("s2", ohs, E2, SLOT_TILES2, slots, tile_expert)
                stage_scatter("sc2", ctok, rows2_in, slots, 2)
                stage_glu("h2", fc, a["l2f_shared"])
                stage_sorted_glu("e2", SLOT_TILES2, 2, a["l2f_routed"], tile_expert, rows2_in, rows2_out)
                bufs = [as_tokens(fx), as_tokens(fc)]
                stage_gather("ga2", rows2_out, slots, bufs)
                stage_add_to_x("x2", [(acc[:], 0.5 / 8), (bufs[0], halves[0]), (bufs[1], halves[1])])

        def stage_capacity_slots(onehot, top, slots):
            E = E3
            with ExitStack() as own:
                val = sb("s3_val", [P, NT, E], on=own)
                vT = sb("s3_vT", [E, T], on=own)
                work = sb("s3_work", [E, T], on=own)
                best = sb("s3_best", [E, 8], on=own)
                base = sb("s3_base", [E, 1], on=own)
                cum = sb("s3_cum", [E, T], on=own)
                valued, turned, copied, iotas, cols, order = (
                    sem("s3_" + n) for n in ("valued", "turned", "copied", "iotas", "cols", "order"))
                with nc.Block() as block:
                    @block.gpsimd
                    def _(pool):
                        pool.iota(base[:], pattern=[[0, 1]], base=-1 - DROPPED, channel_multiplier=CAP,
                                  allow_small_or_imprecise_dtypes=True).then_inc(iotas, 1)

                    @block.tensor
                    def _(pe):
                        pe.wait_ge(valued, 1)
                        for g in range(NCH):
                            for q in range(TPC):
                                last = pe.transpose(psum[0:E, g, q * P:(q + 1) * P], val[:, g * TPC + q, :], ident[:])
                            last.then_inc(turned, 1)
                        pe.wait_ge(iotas, 2)
                        for i in range(NT):
                            last = pe.matmul(psum[:, 6, i:i + 1], cum[:, i * P:(i + 1) * P], ones[0:E, 0:1],
                                             start=True, stop=True)
                        last.then_inc(cols, 1)

                    @block.scalar
                    def _(act):
                        for g in range(NCH):
                            act.wait_ge(turned, g + 1)
                            act.copy(vT[:, g * CH:(g + 1) * CH], psum[0:E, g, :])
                            act.copy(work[:, g * CH:(g + 1) * CH], psum[0:E, g, :]).then_inc(copied, 1)

                    @block.vector
                    def _(dve):
                        link = chain(dve, order)
                        dve.tensor_tensor(val[:], onehot[:], over_e(top[:], E), ALU.mult).then_inc(valued, 1)
                        dve.wait_ge(copied, NCH)
                        for _ in range(CAP // 8):
                            link(dve.max(best[:], work[:]))
                            link(dve.match_replace(work[:], best[:], work[:], -1.0))
                        link(dve.tensor_scalar(work[:], work[:], 0.0, None, ALU.is_lt))
                        link(dve.tensor_scalar(vT[:], vT[:], 0.0, None, ALU.is_gt))
                        link(dve.tensor_tensor(vT[:], vT[:], work[:], ALU.mult))
                        link(dve.tensor_tensor_scan(cum[:], ones[0:E, 0:1].to_broadcast([E, T]), vT[:], 0.0,
                                                    ALU.mult, ALU.add))
                        dve.wait_ge(iotas, 1)
                        dve.scalar_tensor_tensor(out=cum[:], in0=cum[:], scalar=base[:, 0:1], in1=vT[:],
                                                 op0=ALU.add, op1=ALU.mult).then_inc(iotas, 1)
                        dve.wait_ge(cols, 1)
                        dve.tensor_scalar(slots[:], psum[:, 6, 0:NT], float(DROPPED), None, ALU.add)

        def stage_capacity_experts():
            NF = 4
            W = KD * FU + NF * D
            R2 = CAP - P
            with ExitStack() as own:
                w = sb("e3_w", [P, 2, W + NF], on=own)
                b2 = sb("e3_b2", [P, 2, D], on=own)
                ra = sb("e3_ra", [P, 2, D], on=own)
                rb = sb("e3_rb", [R2, 2, D], on=own)
                rT = sb("e3_rT", [P, 2, KD, CAP], on=own)
                hT = sb("e3_hT", [P, NF, CAP], on=own)
                oa = sb("e3_oa", [P, 2, D], on=own)
                ob = sb("e3_ob", [R2, 2, D], on=own)
                x_in = [sem(f"e3_x_in{r}") for r in range(2)]
                w_in = [sem(f"e3_w_in{r}") for r in range(2)]
                stored = [sem(f"e3_stored{r}") for r in range(2)]
                rows_t, rows_c, up, hidden, down, outc = (
                    sem("e3_" + n) for n in ("rows_t", "rows_c", "up", "hidden", "down", "outc"))
                src = rows3_in.rearrange("(e c) d -> e c d", c=CAP)
                dst = rows3_out.rearrange("(e c) d -> e c d", c=CAP)
                with nc.Block() as block:
                    @block.sync
                    def _(sp):
                        def load(i, r, first):
                            e = 2 * i + r
                            if not first:
                                sp.wait_ge(rows_t, e - 1)
                            sp.dma_start(ra[:, r, :], src[bass.ds(e, 1), 0:P].rearrange("e c d -> c (e d)")).then_inc(x_in[r], 16)
                            sp.dma_start(rb[:, r, :], src[bass.ds(e, 1), P:CAP].rearrange("e c d -> c (e d)")).then_inc(x_in[r], 16)
                            if not first:
                                sp.wait_ge(outc, 2 * (e - 1))
                            sp.dma_start(w[:, r, :], a["l3_experts"][bass.ds(e, 1)].rearrange("e p n -> p (e n)")
                                         ).then_inc(w_in[r], 16)
                            sp.dma_start(b2[:, r, :], a["l3_b2"][bass.ds(e, 1)].rearrange("e d -> (e d)").partition_broadcast(P)
                                         ).then_inc(w_in[r], 16)
                        load(0, 0, True)
                        load(0, 1, True)
                        with sp.Fori(1, E3 // 2) as i:
                            load(i, 0, False)
                            load(i, 1, False)

                    @block.tensor
                    def _(pe):
                        def turn(i, r, first=False):
                            pe.wait_ge(x_in[r], 32 * i + 32)
                            if not first:
                                pe.wait_ge(rows_c, 2 * i + r)
                            for k in range(KD):
                                pe.transpose(psum[:, 6, k * CAP:k * CAP + P], ra[:, r, k * P:(k + 1) * P], ident[:])
                                last = pe.transpose(psum[:, 6, k * CAP + P:(k + 1) * CAP], rb[:, r, k * P:(k + 1) * P],
                                                    ident[0:R2, 0:R2])
                            last.then_inc(rows_t, 1)

                        def expert(i, r, first=False, last_expert=False):
                            e = 2 * i + r
                            pe.wait_ge(rows_c, e + 1)
                            pe.wait_ge(w_in[r], 32 * i + 32)
                            if not first:
                                pe.wait_ge(hidden, NF * e)
                            for f in range(NF):
                                for k in range(KD):
                                    last = pe.matmul(psum[:, f, 0:CAP],
                                                     w[:, r, k * FU + f * P:k * FU + (f + 1) * P], rT[:, r, k, :],
                                                     start=(k == 0), stop=(k == KD - 1))
                                last.then_inc(up, 1)
                            if not last_expert:
                                turn(i + r, 1 - r)
                            pe.wait_ge(hidden, NF * e + NF)
                            for part, (c0, c1) in enumerate(((0, P), (P, CAP))):
                                if not first:
                                    pe.wait_ge(outc, 2 * (e - 1) + part + 1)
                                for f in range(NF):
                                    last = pe.matmul(psum[0:c1 - c0, 4 + part, 0:D], hT[:, f, c0:c1],
                                                     w[:, r, KD * FU + f * D:KD * FU + (f + 1) * D],
                                                     start=(f == 0), stop=(f == NF - 1))
                                last.then_inc(down, 1)

                        turn(0, 0, first=True)
                        expert(0, 0, first=True)
                        expert(0, 1)
                        with pe.Fori(1, E3 // 2 - 1) as i:
                            expert(i, 0)
                            expert(i, 1)
                        expert(E3 // 2 - 1, 0)
                        expert(E3 // 2 - 1, 1, last_expert=True)

                    @block.scalar
                    def _(act):
                        def rows(i, r, first):
                            e = 2 * i + r
                            act.wait_ge(rows_t, e + 1)
                            if not first:
                                act.wait_ge(up, NF * (e - 1))
                            act.copy(rT[:, r, :, :].rearrange("p k t -> p (k t)"), psum[:, 6, 0:KD * CAP]).then_inc(rows_c, 1)

                        def gelu(i, r, first):
                            e = 2 * i + r
                            for f in range(NF):
                                act.wait_ge(up, NF * e + f + 1)
                                if not first:
                                    act.wait_ge(down, 2 * e)
                                act.activation(hT[:, f, :], psum[:, f, 0:CAP],
                                               ACT.Gelu_apprx_tanh, bias=w[:, r, W + f:W + f + 1]).then_inc(hidden, 1)
                        rows(0, 0, True)
                        gelu(0, 0, True)
                        rows(0, 1, True)
                        gelu(0, 1, False)
                        with act.Fori(1, E3 // 2) as i:
                            for r in range(2):
                                rows(i, r, False)
                                gelu(i, r, False)

                    @block.vector
                    def _(dve):
                        def outs(i, r, first):
                            e = 2 * i + r
                            if not first:
                                dve.wait_ge(stored[r], 32 * i)
                            dve.wait_ge(w_in[r], 32 * i + 32)
                            dve.wait_ge(down, 2 * e + 1)
                            dve.tensor_tensor(oa[:, r, :], psum[:, 4, 0:D], b2[:, r, :], ALU.add).then_inc(outc, 1)
                            dve.wait_ge(down, 2 * e + 2)
                            dve.tensor_tensor(ob[:, r, :], psum[0:R2, 5, 0:D], b2[0:R2, r, :], ALU.add).then_inc(outc, 1)
                        outs(0, 0, True)
                        outs(0, 1, True)
                        with dve.Fori(1, E3 // 2) as i:
                            outs(i, 0, False)
                            outs(i, 1, False)

                    @block.gpsimd
                    def _(pool):
                        with pool.Fori(0, E3 // 2) as i:
                            for r in range(2):
                                e = 2 * i + r
                                pool.wait_ge(outc, 2 * e + 2)
                                pool.dma_start(dst[bass.ds(e, 1), 0:P].rearrange("e c d -> c (e d)"), oa[:, r, :]).then_inc(stored[r], 16)
                                pool.dma_start(dst[bass.ds(e, 1), P:CAP].rearrange("e c d -> c (e d)"), ob[:, r, :]).then_inc(stored[r], 16)
                        for r in range(2):
                            pool.wait_ge(stored[r], 32 * (E3 // 2))

        def layer3():
            stage_to_features("a3", xtok, fx)
            with ExitStack() as own:
                gates = sb("gates3", [P, NT, E2], on=own)
                stage_sigmoid_top2("t3", a["l3_router"], a["l3_bias"], gates)
                stage_glu("g3", fx, a["l3c_shared"])
                stage_gelu_experts("x3", fx, a["l3c_routed"], gates, 1.0, 1.0 / 3.0)
            stage_to_features("b3", ctok, fc)
            with ExitStack() as own:
                slots = sb("slots3", [P, NT], U32, on=own)
                ohs, tops = stage_softmax_route("r3", own, E3, a["l3_gate"], 1)
                stage_capacity_slots(ohs[0], tops[0], slots)
                stage_scatter("sc3", ctok, rows3_in, slots, 1, bound=E3 * CAP - 1)
                stage_capacity_experts()
                stage_gather("ga3", rows3_out, slots, [ctok], bound=E3 * CAP - 1)
                stage_add_to_x("x3", [(ctok[:], 1.0)])

        def stage_store():
            stored = sem("stored")
            with nc.Block() as block:
                @block.sync
                def _(sp):
                    sp.dma_start(out.rearrange("(i p) d -> p i d", p=P), xtok[:]).then_inc(stored, 16)
                    sp.wait_ge(stored, 16)

        for part in (stage_load, layer0, layer1, layer2, layer3, stage_store):
            before = nc.snapshot_sems()
            part()
            nc.clear_and_free_semaphores(nc.allocated_since(before))
            nc.all_engine_barrier()


def kernel(**inputs):
    import numpy as np
    import concourse.bacc as bacc
    from concourse.bass_utils import run_bass_kernel_spmd

    v = {k: np.asarray(x) for k, x in inputs.items()}

    def rows(w):
        *lead, n, m = w.shape
        w = w.reshape(*lead, n // P, P, m)
        return np.moveaxis(w, -3, -2).reshape(*lead, P, n // P * m)

    def unit(gate, up, down):
        return np.concatenate([rows(gate), rows(up), rows(down)], axis=-1)

    def swap(w):
        return np.swapaxes(w, -1, -2)

    w1s = v["L2_ffn_w1_s"].transpose(1, 0, 2).reshape(D, 2, FU).transpose(1, 0, 2)
    w3s = v["L2_ffn_w3_s"].transpose(1, 0, 2).reshape(D, 2, FU).transpose(1, 0, 2)
    w2s = v["L2_ffn_w2_s"].reshape(2, FU, D)
    arrays = {
        "x": v["x"].reshape(T, D),
        "condT": rows(swap(v["cond_1024"])).reshape(P, KD, B),
        "mask": v["mask_SxS_bk0"],
        "l0_cond_w": rows(v["L0_cond_weight"]).reshape(P, KD, D),
        "l0_gate": rows(v["L0_ffn_gate_w"]).reshape(P, KD, E0),
        "l0_shared": unit(v["L0_ffn_shared_gate_w"], v["L0_ffn_shared_up_w"], v["L0_ffn_shared_down_w"])[None],
        "l0_routed": unit(v["L0_ffn_routed_gate_w"], v["L0_ffn_routed_up_w"], v["L0_ffn_routed_down_w"]),
        "l1_w": np.stack([rows(w).reshape(P, KD, D) for w in (
            swap(v["L1_cond_Wq"]), v["L1_cond_Wk"], swap(v["L1_cond_Wv"]), swap(v["L1_cond_Wt"]),
            swap(v["L1_cond_Wo"]))], axis=1),
        "l1_sim": rows(v["L1_ffn_sim_matrix"]).reshape(P, KD, E1),
        "l1_gates": v["L1_ffn_gates"],
        "l1_qkv": rows(np.concatenate([v["L1_ffn_q_proj"], v["L1_ffn_k_proj"], v["L1_ffn_v_proj"]], axis=-1)
                       ).reshape(E1, P, KD, 3 * H1).transpose(1, 0, 2, 3),
        "l1_o": v["L1_ffn_o_proj"].transpose(1, 0, 2),
        "l2_router": rows(swap(v["L2_cond_W_router"])).reshape(P, 2 * KD, E2),
        "l2_bias": v["L2_cond_router_bias"],
        "l2c_shared": unit(swap(v["L2_cond_s_w1"]), swap(v["L2_cond_s_w3"]), swap(v["L2_cond_s_w2"])),
        "l2c_routed": np.concatenate([rows(swap(v["L2_cond_r_w1"])), rows(swap(v["L2_cond_r_w2"]))], axis=-1),
        "l2_gate": rows(swap(v["L2_ffn_gate_W"])).reshape(P, KD, E2),
        "l2f_shared": unit(w1s, w3s, w2s),
        "l2f_routed": unit(v["L2_ffn_w1_e"], v["L2_ffn_w3_e"], v["L2_ffn_w2_e"]),
        "l3_router": rows(v["L3_cond_router_W"]).reshape(P, 2 * KD, E2),
        "l3_bias": v["L3_cond_router_bias"],
        "l3c_shared": unit(v["L3_cond_w1"], v["L3_cond_w3"], v["L3_cond_w2"])[None],
        "l3c_routed": np.concatenate([rows(v["L3_cond_W1e"]), rows(v["L3_cond_W2e"])], axis=-1),
        "l3_gate": rows(v["L3_ffn_Wg"]).reshape(P, KD, E3),
        "l3_experts": np.concatenate([rows(v["L3_ffn_W1"]), rows(v["L3_ffn_W2"]),
                                      rows(v["L3_ffn_b1"][:, :, None])], axis=-1),
        "l3_b2": v["L3_ffn_b2"],
    }
    nc = bacc.Bacc("TRN2", target_bir_lowering=False, num_devices=1)
    arrays = {f"in_{k}": np.ascontiguousarray(x) for k, x in arrays.items()}
    args = {k[3:]: nc.dram_tensor(k, x.shape, mybir.dt.from_np(x.dtype), kind="ExternalInput").ap()
            for k, x in arrays.items()}
    out = nc.dram_tensor("out_x", (T, D), F32, kind="ExternalOutput").ap()
    build(nc, args, out)
    got = run_bass_kernel_spmd(nc, [arrays], core_ids=[0]).results[0]["out_x"]
    return got.reshape(B, S, D)
```

```python
from contextlib import ExitStack

import concourse.bass as bass
from concourse import mybir

F32 = mybir.dt.float32
F32R = mybir.dt.float32r
I32 = mybir.dt.int32
U32 = mybir.dt.uint32
U8 = mybir.dt.uint8
ALU = mybir.AluOpType
ACT = mybir.ActivationFunctionType
AX_X = mybir.AxisListType.X

P = 128
B, S, D = 2, 1024, 256
T = B * S
NT = T // P
KD = D // P
CH = 512
NCH = T // CH
TPC = CH // P
TPB = S // P
FU = 512
UNIT = KD * FU * 2 + FU // P * D
BIG = 1000.0
E0, E1, E2, E3 = 32, 16, 8, 16
H1 = 128
SLOT_TILES0 = NT + E0
SLOT_TILES2 = 2 * NT + E2
CAP = 160
DROPPED = 4096
FMAX = 3.4028234663852886e38
HEADS, HW = 16, 16


def build(nc, a, out):
    ctx = ExitStack()
    with ctx:
        def sb(name, shape, dt=F32, on=ctx):
            return on.enter_context(nc.sbuf_tensor("sb_" + name, shape, dt))

        def sem(name):
            return nc.alloc_semaphore(name=name)

        def scratch(name, rows):
            return nc.dram_tensor(name, [rows, D], F32, kind="Internal").ap()

        rows0_in, rows0_out = scratch("rows0_in", SLOT_TILES0 * P), scratch("rows0_out", SLOT_TILES0 * P)
        rows2_in, rows2_out = scratch("rows2_in", SLOT_TILES2 * P), scratch("rows2_out", SLOT_TILES2 * P)
        rows3_in, rows3_out = scratch("rows3_in", E3 * CAP), scratch("rows3_out", E3 * CAP)

        xtok = sb("xtok", [P, NT, D])
        ctok = sb("ctok", [P, NT, D])
        acc = sb("acc", [P, NT, D])
        fx = sb("fx", [P, KD, T])
        fc = sb("fc", [P, KD, T])
        ident = sb("ident", [P, P])
        tri = sb("tri", [P, P])
        ones = sb("ones", [P, P])
        iota_e = sb("iota_e", [P, E0])
        condT = sb("condT", [P, KD, B])
        psum = ctx.enter_context(nc.psum_tensor("ps", [P, 8, 512], F32))

        zeroed = sem("zeroed")
        ZEROINGS = [(table, i, min(NT, table.shape[0] // P - i)) for table in (rows0_in, rows2_in, rows3_in)
                    for i in range(0, table.shape[0] // P, NT)]

        def stage_tables_zeroed():
            with nc.Block() as block:
                @block.gpsimd
                def _(pool):
                    pool.wait_ge(zeroed, 16 * len(ZEROINGS))

        def stage_load():
            loaded, cleared, made = sem("ld_in"), sem("ld_cleared"), sem("ld_made")
            with nc.Block() as block:
                @block.sync
                def _(sp):
                    sp.dma_start(xtok[:], a["x"].rearrange("(i p) d -> p i d", p=P)).then_inc(loaded, 16)
                    sp.dma_start(condT[:], a["condT"]).then_inc(loaded, 16)
                    sp.wait_ge(cleared, 1)
                    for table, i, m in ZEROINGS:
                        sp.dma_start(table[i * P:(i + m) * P, :].rearrange("(i p) d -> p i d", p=P),
                                     acc[:, 0:m, :]).then_inc(zeroed, 16)
                    sp.wait_ge(loaded, 32)

                @block.vector
                def _(dve):
                    dve.memset(acc[:], 0.0).then_inc(cleared, 1)
                    dve.memset(ones[:], 1.0).then_inc(made, 1)

                @block.gpsimd
                def _(pool):
                    pool.iota(iota_e[:], pattern=[[1, E0]], base=-int(BIG), channel_multiplier=0,
                              allow_small_or_imprecise_dtypes=True)
                    pool.wait_ge(made, 1)
                    pool.affine_select(out=ident[:], in_=ones[:], compare_op=ALU.is_equal, fill=0.0,
                                       base=0, pattern=[[-1, P]], channel_multiplier=1)
                    pool.affine_select(out=tri[:], in_=ones[:], compare_op=ALU.is_gt, fill=0.0,
                                       base=0, pattern=[[1, P]], channel_multiplier=-1)

        def stage_to_features(tag, tok, feat):
            turned, used = sem(tag + "_turned"), sem(tag + "_used")
            with nc.Block() as block:
                @block.tensor
                def _(pe):
                    for b in range(8):
                        k, c = b // NCH, b % NCH
                        for q in range(TPC):
                            last = pe.transpose(psum[:, b, q * P:(q + 1) * P],
                                                tok[:, c * TPC + q, k * P:(k + 1) * P], ident[:])
                        last.then_inc(turned, 1)

                @block.vector
                def _(dve):
                    for b in range(0, 8, 2):
                        dve.wait_ge(turned, b + 1)
                        dve.tensor_copy(feat[:, b // NCH, (b % NCH) * CH:(b % NCH + 1) * CH], psum[:, b, :])

                @block.scalar
                def _(act):
                    for b in range(1, 8, 2):
                        act.wait_ge(turned, b + 1)
                        act.copy(feat[:, b // NCH, (b % NCH) * CH:(b % NCH + 1) * CH], psum[:, b, :])

        def stage_to_tokens(tag, feat, tok):
            turned = sem(tag + "_turned")
            with nc.Block() as block:
                @block.tensor
                def _(pe):
                    for b in range(8):
                        for q in range(2):
                            for k in range(KD):
                                t0 = (2 * b + q) * P
                                last = pe.transpose(psum[:, b, (q * KD + k) * P:(q * KD + k + 1) * P],
                                                    feat[:, k, t0:t0 + P], ident[:])
                        last.then_inc(turned, 1)

                @block.vector
                def _(dve):
                    for b in range(0, 8, 2):
                        dve.wait_ge(turned, b + 1)
                        dve.tensor_copy(tok[:, 2 * b:2 * b + 2, :].rearrange("p i d -> p (i d)"), psum[:, b, :])

                @block.scalar
                def _(act):
                    for b in range(1, 8, 2):
                        act.wait_ge(turned, b + 1)
                        act.copy(tok[:, 2 * b:2 * b + 2, :].rearrange("p i d -> p (i d)"), psum[:, b, :])

        def stage_l0_cond():
            with ExitStack() as own:
                w = sb("l0c_w", [P, KD, D], on=own)
                w2 = sb("l0c_w2", [P, KD, D], on=own)
                wb = sb("l0c_wb", [P, B, KD, D], on=own)
                ys = sb("l0c_ys", [P, KD, B], on=own)
                ys2 = sb("l0c_ys2", [P, KD, B], on=own)
                d = sb("l0c_d", [P, KD, B], on=own)
                loaded, order, squares, norm, root, demod, folded, done = (
                    sem("l0c_" + n) for n in ("loaded", "order", "squares", "norm", "root", "demod", "folded", "done"))
                with nc.Block() as block:
                    @block.sync
                    def _(sp):
                        sp.dma_start(w[:], a["l0_cond_w"]).then_inc(loaded, 16)

                    @block.vector
                    def _(dve):
                        dve.tensor_scalar(ys[:], condT[:], float(D) ** -0.5, None, ALU.mult).then_inc(order, 1)
                        dve.wait_ge(order, 1)
                        dve.tensor_tensor(ys2[:], ys[:], ys[:], ALU.mult)
                        dve.wait_ge(loaded, 16)
                        dve.tensor_tensor(w2[:], w[:], w[:], ALU.mult).then_inc(squares, 1)
                        for b in range(B):
                            for k in range(KD):
                                last = dve.tensor_scalar(wb[:, b, k, :], w[:, k, :], ys[:, k, b:b + 1], None, ALU.mult)
                        last.then_inc(folded, 1)
                        dve.wait_ge(norm, 1)
                        dve.tensor_scalar(d[:], psum[:, 0, 0:KD * B].rearrange("p (k b) -> p k b", k=KD),
                                          1e-8, None, ALU.add).then_inc(order, 1)
                        dve.wait_ge(root, 1)
                        dve.reciprocal(d[:], d[:]).then_inc(demod, 1)
                        dve.wait_ge(demod, 1)
                        for n in range(8):
                            dve.wait_ge(done, n + 1)
                            b, c, o = n // 4, n // 2 % 2, n % 2
                            t0 = b * S + c * CH
                            dve.tensor_scalar(fc[:, o, t0:t0 + CH], psum[:, n, :], d[:, o, b:b + 1], None, ALU.mult)

                    @block.scalar
                    def _(act):
                        act.wait_ge(order, 2)
                        act.activation(d[:], d[:], ACT.Sqrt).then_inc(root, 1)

                    @block.tensor
                    def _(pe):
                        pe.wait_ge(squares, 1)
                        for o in range(KD):
                            for k in range(KD):
                                last = pe.matmul(psum[:, 0, o * B:(o + 1) * B], w2[:, k, o * P:(o + 1) * P],
                                                 ys2[:, k, :], start=(k == 0), stop=(k == KD - 1))
                        last.then_inc(norm, 1)
                        pe.wait_ge(folded, 1)
                        pe.wait_ge(demod, 1)
                        for n in range(8):
                            b, c, o = n // 4, n // 2 % 2, n % 2
                            t0 = b * S + c * CH
                            for k in range(KD):
                                last = pe.matmul(psum[:, n, :], wb[:, b, k, o * P:(o + 1) * P],
                                                 fx[:, k, t0:t0 + CH], start=(k == 0), stop=(k == KD - 1))
                            last.then_inc(done, 1)

        def matmul_split(pe, to, w, x, start, stop):
            pe.matmul(to, w[0], x[0], start=start, stop=False)
            pe.matmul(to, w[0], x[1], start=False, stop=False)
            return pe.matmul(to, w[1], x[0], start=False, stop=stop)

        def stage_glu(tag, feat, units, beside=None):
            NU = units.shape[0]
            N = NU * NCH
            NF = FU // P
            with ExitStack() as own:
                sg = sb(tag + "_sg", [P, 2, CH], on=own)
                product = sb(tag + "_product", [P, 2, CH], on=own)
                wbuf = sb(tag + "_wbuf", [P, NU, UNIT], on=own)
                ws = sb(tag + "_ws", [P, 2, UNIT], F32R, on=own)
                fs = sb(tag + "_fs", [P, 2, 2, KD, CH], F32R, on=own)
                hs = sb(tag + "_hs", [P, 2, 2, NF, CH], F32R, on=own)
                loaded = [sem(f"{tag}_w{u}") for u in range(NU)]
                whigh, wsplit, fhigh, fsplit, both, gated, multiplied, high, hidden, down, added = (
                    sem(f"{tag}_{n}") for n in ("whigh", "wsplit", "fhigh", "fsplit", "both", "gated", "multiplied",
                                                "high", "hidden", "down", "added"))
                with nc.Block() as block:
                    @block.sync
                    def _(sp):
                        for u in range(NU):
                            sp.dma_start(wbuf[:, u, 0:UNIT], units[u]).then_inc(loaded[u], 16)

                    if beside is not None:
                        block.gpsimd(beside)

                    UP_END = 2 * KD * FU
                    parts = [(0, UP_END), (UP_END, UNIT)]

                    def wgate(k, f):
                        return [ws[:, part, k * FU + f * P:k * FU + (f + 1) * P] for part in range(2)]

                    def wup(k, f):
                        return [ws[:, part, (KD + k) * FU + f * P:(KD + k) * FU + (f + 1) * P] for part in range(2)]

                    def wdown(f):
                        return [ws[:, part, UP_END + f * D:UP_END + (f + 1) * D] for part in range(2)]

                    @block.tensor
                    def _(pe):
                        def gate_up(n):
                            u, c = n // NCH, n % NCH
                            if c == 0:
                                pe.wait_ge(wsplit, 2 * u + 1)
                            pe.wait_ge(fsplit, n + 1)
                            for f in range(NF):
                                m = n * NF + f
                                if m >= 2:
                                    pe.wait_ge(multiplied, m - 1)
                                for j, w in enumerate((wgate, wup)):
                                    for k in range(KD):
                                        last = matmul_split(pe, psum[:, m % 2 * 2 + j, :], w(k, f),
                                                            [fs[:, n % 2, part, k, :] for part in range(2)],
                                                            k == 0, k == KD - 1)
                                last.then_inc(both, 1)

                        def down_all(n):
                            if n % NCH == 0:
                                pe.wait_ge(wsplit, 2 * (n // NCH) + 2)
                            pe.wait_ge(hidden, NF * (n + 1))
                            for half in range(2):
                                if n >= 1:
                                    pe.wait_ge(added, 2 * (n - 1) + half + 1)
                                for q in range(2):
                                    for f in range(NF):
                                        t0 = (2 * half + q) * P
                                        last = matmul_split(pe, psum[:, 4 + half, q * D:(q + 1) * D],
                                                            [hs[:, n % 2, part, f, t0:t0 + P] for part in range(2)],
                                                            wdown(f), f == 0, f == NF - 1)
                                last.then_inc(down, 1)

                        gate_up(0)
                        for n in range(N):
                            if n + 1 < N and (n + 1) % NCH:
                                gate_up(n + 1)
                            down_all(n)
                            if n + 1 < N and (n + 1) % NCH == 0:
                                gate_up(n + 1)

                    @block.scalar
                    def _(act):
                        def weights_high(u):
                            act.wait_ge(loaded[u], 16)
                            if u:
                                act.wait_ge(down, 2 * NCH * u)
                            for lo, hi in parts:
                                act.copy(ws[:, 0, lo:hi], wbuf[:, u, lo:hi]).then_inc(whigh, 1)

                        def features_high(n):
                            if n >= 2:
                                act.wait_ge(both, NF * (n - 1))
                            c = n % NCH
                            act.copy(fs[:, n % 2, 0, :, :], feat[:, :, c * CH:(c + 1) * CH]).then_inc(fhigh, 1)

                        def hidden_high(m):
                            n, f = m // NF, m % NF
                            if n >= 2 and f == 0:
                                act.wait_ge(down, 2 * (n - 1))
                            act.wait_ge(multiplied, m + 1)
                            act.copy(hs[:, n % 2, 0, f, :], product[:, m % 2, :]).then_inc(high, 1)

                        features_high(0)
                        weights_high(0)
                        for m in range(N * NF):
                            n, f = m // NF, m % NF
                            if f == 0 and n and n % NCH == 0:
                                hidden_high(m - 1)
                                weights_high(n // NCH)
                            if f == 0 and n + 1 < N:
                                features_high(n + 1)
                            act.wait_ge(both, m + 1)
                            if m >= 2:
                                act.wait_ge(multiplied, m - 1)
                            act.activation(sg[:, m % 2, :], psum[:, m % 2 * 2, :], ACT.Silu).then_inc(gated, 1)
                            if m and not (f == 0 and n % NCH == 0):
                                hidden_high(m - 1)
                        hidden_high(N * NF - 1)

                    @block.vector
                    def _(dve):
                        def weights_low(u):
                            for q, (lo, hi) in enumerate(parts):
                                dve.wait_ge(whigh, 2 * u + q + 1)
                                dve.tensor_tensor(ws[:, 1, lo:hi], wbuf[:, u, lo:hi], ws[:, 0, lo:hi],
                                                  ALU.subtract).then_inc(wsplit, 1)

                        def features_low(n):
                            dve.wait_ge(fhigh, n + 1)
                            c = n % NCH
                            dve.tensor_tensor(fs[:, n % 2, 1, :, :], feat[:, :, c * CH:(c + 1) * CH],
                                              fs[:, n % 2, 0, :, :], ALU.subtract).then_inc(fsplit, 1)

                        def multiply(m):
                            dve.wait_ge(gated, m + 1)
                            if m >= 2:
                                dve.wait_ge(hidden, m - 1)
                            dve.tensor_tensor(product[:, m % 2, :], sg[:, m % 2, :], psum[:, m % 2 * 2 + 1, :],
                                              ALU.mult).then_inc(multiplied, 1)

                        def hidden_low(m):
                            dve.wait_ge(high, m + 1)
                            parity, f = m // NF % 2, m % NF
                            dve.tensor_tensor(hs[:, parity, 1, f, :], product[:, m % 2, :], hs[:, parity, 0, f, :],
                                              ALU.subtract).then_inc(hidden, 1)

                        def add(n):
                            u, c = n // NCH, n % NCH
                            for half in range(2):
                                dve.wait_ge(down, 2 * n + half + 1)
                                to = acc[:, c * TPC + 2 * half:c * TPC + 2 * half + 2, :].rearrange("p i d -> p (i d)")
                                if u == 0:
                                    ins = dve.tensor_copy(to, psum[:, 4 + half, :])
                                else:
                                    ins = dve.tensor_tensor(to, psum[:, 4 + half, :], to, ALU.add)
                                ins.then_inc(added, 1)

                        features_low(0)
                        weights_low(0)
                        for m in range(N * NF):
                            n, f = m // NF, m % NF
                            new_unit = f == 0 and n and n % NCH == 0
                            if new_unit:
                                hidden_low(m - 1)
                                add(n - 1)
                                weights_low(n // NCH)
                            if f == 0 and n + 1 < N:
                                features_low(n + 1)
                            multiply(m)
                            if m and not new_unit:
                                hidden_low(m - 1)
                            if f == NF - 1 and n % NCH:
                                add(n - 1)
                        hidden_low(N * NF - 1)
                        add(N - 1)

        def stage_gelu_experts(tag, feat, experts, gates, scale_before, scale_after):
            NF = 2
            W = KD * NF * P + NF * D
            NE = experts.shape[0]
            with ExitStack() as own:
                h = sb(tag + "_h", [P, 2, NF, CH], on=own)
                hs = sb(tag + "_hs", [P, 2, 2, NF, CH], F32R, on=own)
                fs = sb(tag + "_fs", [P, 2, KD, T], F32R, on=own)
                wbuf = sb(tag + "_wbuf", [P, 2, W], on=own)
                ws = sb(tag + "_ws", [P, 2, 2, W], F32R, on=own)
                loaded = [sem(f"{tag}_w{r}") for r in range(2)]
                whigh, wsplit, fhigh, fsplit, up, raw, high, hidden, down, added, scaled = (
                    sem(f"{tag}_{n}") for n in ("whigh", "wsplit", "fhigh", "fsplit", "up", "raw", "high", "hidden",
                                                "down", "added", "scaled"))
                with nc.Block() as block:
                    @block.sync
                    def _(sp):
                        for r in range(2):
                            sp.dma_start(wbuf[:, r, 0:W], experts[r]).then_inc(loaded[r], 16)
                        with sp.Fori(1, NE // 2) as i:
                            for r in range(2):
                                sp.wait_ge(wsplit, 2 * i + r - 1)
                                sp.dma_start(wbuf[:, r, 0:W], experts[bass.ds(2 * i + r, 1)].rearrange("e p n -> p (e n)")
                                             ).then_inc(loaded[r], 16)

                    def w1(r, k, f):
                        return [ws[:, r, part, k * NF * P + f * P:k * NF * P + (f + 1) * P] for part in range(2)]

                    def w2(r, f):
                        return [ws[:, r, part, KD * NF * P + f * D:KD * NF * P + (f + 1) * D] for part in range(2)]

                    def pairs(pair, engine):
                        pair(0, True, False)
                        with engine.Fori(1, NE // 2 - 1) as i:
                            pair(i, False, False)
                        pair(NE // 2 - 1, False, True)

                    def expert_to_split(m, last):
                        return {1: (1, 1), 5: None if last else (2, 0)}.get(m)

                    @block.tensor
                    def _(pe):
                        def up_part(i, m, first):
                            r, c = m // NCH, m % NCH
                            if c == 0:
                                pe.wait_ge(wsplit, 2 * i + r + 1)
                            if first and r == 0:
                                pe.wait_ge(fsplit, c + 1)
                            for f in range(NF):
                                if not (first and m < 2):
                                    pe.wait_ge(raw, 16 * i + 2 * m + f - 3)
                                for k in range(KD):
                                    last = matmul_split(pe, psum[:, (2 * m + f) % 4, :], w1(r, k, f),
                                                        [fs[:, part, k, c * CH:(c + 1) * CH] for part in range(2)],
                                                        k == 0, k == KD - 1)
                                last.then_inc(up, 1)

                        def down_part(i, m, first):
                            pe.wait_ge(hidden, 16 * i + 2 * m + 2)
                            for half in range(2):
                                if not first:
                                    pe.wait_ge(added, 16 * i + 2 * m + half - 1)
                                for q in range(2):
                                    for f in range(NF):
                                        t0 = (2 * half + q) * P
                                        last = matmul_split(pe, psum[:, 4 + half, q * D:(q + 1) * D],
                                                            [hs[:, m % 2, part, f, t0:t0 + P] for part in range(2)],
                                                            w2(m // NCH, f), f == 0, f == NF - 1)
                                last.then_inc(down, 1)

                        def pair(i, first, last):
                            up_part(i, 0, first)
                            for m in range(2 * NCH):
                                if m + 1 < 2 * NCH:
                                    up_part(i, m + 1, first)
                                down_part(i, m, first and m == 0)

                        pairs(pair, pe)

                    @block.scalar
                    def _(act):
                        def weights_high(i, e, r):
                            act.wait_ge(loaded[r], 16 * (i + e // 2 + 1))
                            act.copy(ws[:, r, 0, :], wbuf[:, r, 0:W]).then_inc(whigh, 1)

                        def pair(i, first, last):
                            for m in range(2 * NCH):
                                split = expert_to_split(m, last)
                                if split:
                                    if not (first and m == 1):
                                        act.wait_ge(down, 16 * i + 2 * m - 2)
                                    weights_high(i, *split)
                                for f in range(NF):
                                    act.wait_ge(up, 16 * i + 2 * m + f + 1)
                                    if not (first and m < 2):
                                        act.wait_ge(hidden, 16 * i + 2 * m + f - 3)
                                    act.activation(h[:, m % 2, f, :], psum[:, (2 * m + f) % 4, :],
                                                   ACT.Gelu).then_inc(raw, 1)
                                    if not (first and m < 2):
                                        act.wait_ge(down, 16 * i + 2 * m - 2)
                                    act.wait_ge(raw, 16 * i + 2 * m + f + 1)
                                    act.copy(hs[:, m % 2, 0, f, :], h[:, m % 2, f, :]).then_inc(high, 1)

                        weights_high(0, 0, 0)
                        for c in range(NCH):
                            act.copy(fs[:, 0, :, c * CH:(c + 1) * CH], feat[:, :, c * CH:(c + 1) * CH]).then_inc(fhigh, 1)
                        pairs(pair, act)

                    @block.vector
                    def _(dve):
                        def weights_low(i, e, r):
                            dve.wait_ge(whigh, 2 * i + e + 1)
                            dve.tensor_tensor(ws[:, r, 1, :], wbuf[:, r, 0:W], ws[:, r, 0, :],
                                              ALU.subtract).then_inc(wsplit, 1)

                        weights_low(0, 0, 0)
                        for c in range(NCH):
                            dve.wait_ge(fhigh, c + 1)
                            dve.tensor_tensor(fs[:, 1, :, c * CH:(c + 1) * CH], feat[:, :, c * CH:(c + 1) * CH],
                                              fs[:, 0, :, c * CH:(c + 1) * CH], ALU.subtract).then_inc(fsplit, 1)
                        dve.tensor_scalar(acc[:], acc[:], scale_before, None, ALU.mult).then_inc(scaled, 1)
                        dve.wait_ge(scaled, 1)

                        def pair(i, first, last):
                            for m in range(2 * NCH):
                                split = expert_to_split(m, last)
                                if split:
                                    weights_low(i, *split)
                                for f in range(NF):
                                    dve.wait_ge(high, 16 * i + 2 * m + f + 1)
                                    dve.tensor_tensor(hs[:, m % 2, 1, f, :], h[:, m % 2, f, :], hs[:, m % 2, 0, f, :],
                                                      ALU.subtract).then_inc(hidden, 1)
                                r, c = m // NCH, m % NCH
                                for half in range(2):
                                    dve.wait_ge(down, 16 * i + 2 * m + half + 1)
                                    if not (first and m < NCH):
                                        dve.wait_ge(added, 16 * i + 2 * (m - NCH) + half + 1)
                                    for q in range(2):
                                        t = c * TPC + 2 * half + q
                                        ins = dve.scalar_tensor_tensor(
                                            out=acc[:, t, :], in0=psum[:, 4 + half, q * D:(q + 1) * D],
                                            scalar=gates[:, t, bass.ds(2 * i + r, 1)], in1=acc[:, t, :],
                                            op0=ALU.mult, op1=ALU.add)
                                    ins.then_inc(added, 1)

                        pairs(pair, dve)
                        dve.wait_ge(added, 8 * NE)
                        dve.tensor_scalar(ctok[:], acc[:], scale_after, None, ALU.mult)

        def logits_on_pe(pe, feat, wr, E, extra=None):
            for i in range(NT):
                parts = [(feat[:, k, i * P:(i + 1) * P], wr[:, k, :]) for k in range(KD)]
                if extra is not None:
                    parts += [(extra[:, k, i // TPB, :], wr[:, KD + k, :]) for k in range(KD)]
                for n, (x, w) in enumerate(parts):
                    last = pe.matmul(psum[:, 0, i * E:(i + 1) * E], x, w, start=(n == 0), stop=(n == len(parts) - 1))
            return last

        def over_e(v, E, n=NT):
            return v.unsqueeze(2).to_broadcast([P, n, E])

        def e_index(E, n=NT):
            return iota_e[:, 0:E].unsqueeze(1).to_broadcast([P, n, E])

        def pick(dve, link, L, top, onehot, tmp, small, E, n=NT):
            link(dve.tensor_reduce(top, L, AX_X, ALU.max))
            link(dve.tensor_tensor(tmp, L, over_e(top, E, n), ALU.is_equal))
            link(dve.tensor_tensor(tmp, tmp, e_index(E, n), ALU.mult))
            link(dve.tensor_reduce(small, tmp, AX_X, ALU.min))
            link(dve.tensor_tensor(onehot, e_index(E, n), over_e(small, E, n), ALU.is_equal))

        def chain(dve, order):
            n = [0]

            def link(ins):
                n[0] += 1
                ins.then_inc(order, 1)
                dve.wait_ge(order, n[0])
            return link

        def stage_slots(tag, onehots, E, tiles, slots, tile_expert, last_tile):
            K = len(onehots)
            N = K * T
            with ExitStack() as own:
                ohT = sb(tag + "_ohT", [E, N], on=own)
                cum = sb(tag + "_cum", [E, N], on=own)
                steps = sb(tag + "_steps", [E, N // P], on=own)
                tiles_i = sb(tag + "_tiles", [E, tiles], on=own)
                ends = sb(tag + "_ends", [E, tiles], on=own)
                v = sb(tag + "_v", [E, 4], on=own)
                te = sb(tag + "_te", [1, tiles], on=own)
                upto = sb(tag + "_upto", [E, E], on=own)
                turned, copied, iotas, counted, started, ended, cols, order, experts = (
                    sem(f"{tag}_{n}") for n in ("turned", "copied", "iotas", "counted", "started", "ended", "cols",
                                                "order", "experts"))
                G = N // CH
                with nc.Block() as block:
                    @block.gpsimd
                    def _(pool):
                        pool.iota(steps[:], pattern=[[P, N // P]], base=0, channel_multiplier=0,
                                  allow_small_or_imprecise_dtypes=True)
                        pool.iota(tiles_i[:], pattern=[[1, tiles]], base=0, channel_multiplier=0,
                                  allow_small_or_imprecise_dtypes=True).then_inc(iotas, 1)

                    @block.tensor
                    def _(pe):
                        for g in range(G):
                            if g >= 4:
                                pe.wait_ge(copied, g - 3)
                            for q in range(TPC):
                                i = g * TPC + q
                                last = pe.transpose(psum[0:E, g % 4, q * P:(q + 1) * P],
                                                    onehots[i // NT][:, i % NT, :], ident[:])
                            last.then_inc(turned, 1)
                        pe.wait_ge(counted, 1)
                        pe.matmul(psum[0:E, 4, 0:1], tri[0:E, 0:E], v[:, 0:1], start=True, stop=True).then_inc(started, 1)
                        pe.wait_ge(ended, 1)
                        pe.matmul(psum[0:1, 5, 0:tiles], ones[0:E, 0:1], ends[:], start=True, stop=True)
                        pe.matmul(psum[0:1, 5, 64:64 + E], v[:, 0:1], upto[:], start=True, stop=True).then_inc(experts, 1)
                        for i in range(N // P):
                            last = pe.matmul(psum[:, 6, i:i + 1], cum[:, i * P:(i + 1) * P], ones[0:E, 0:1],
                                             start=True, stop=True)
                        last.then_inc(cols, 1)

                    @block.scalar
                    def _(act):
                        for g in range(G):
                            act.wait_ge(turned, g + 1)
                            act.copy(ohT[:, g * CH:(g + 1) * CH], psum[0:E, g % 4, :]).then_inc(copied, 1)

                    @block.vector
                    def _(dve):
                        link = chain(dve, order)
                        dve.wait_ge(copied, G)
                        link(dve.tensor_tensor_scan(cum[:], ones[0:E, 0:1].to_broadcast([E, N]), ohT[:], 0.0,
                                                    ALU.mult, ALU.add))
                        dve.wait_ge(iotas, 1)
                        link(dve.tensor_tensor(upto[:], tri[0:E, 0:E], ident[0:E, 0:E], ALU.add))
                        link(dve.tensor_scalar(steps[:], steps[:], cum[:, N - 1:N], None, ALU.is_lt))
                        dve.tensor_reduce(v[:, 0:1], steps[:], AX_X, ALU.add).then_inc(counted, 1)
                        dve.wait_ge(counted, 1)
                        dve.wait_ge(started, 1)
                        link(dve.tensor_tensor(v[:, 1:2], psum[0:E, 4, 0:1], v[:, 0:1], ALU.add))
                        link(dve.tensor_scalar(v[:, 2:3], psum[0:E, 4, 0:1], float(P), -1.0, ALU.mult, ALU.add))
                        link(dve.tensor_scalar(ends[:], tiles_i[:], v[:, 1:2], None, ALU.is_ge))
                        dve.scalar_tensor_tensor(out=cum[:], in0=cum[:], scalar=v[:, 2:3], in1=ohT[:],
                                                 op0=ALU.add, op1=ALU.mult).then_inc(ended, 1)
                        dve.wait_ge(experts, 1)
                        link(dve.tensor_scalar(te[:], psum[0:1, 5, 0:tiles], float(E - 1), None, ALU.min))
                        dve.tensor_copy(tile_expert[:], te[:])
                        dve.tensor_scalar(last_tile[:], psum[0:1, 5, 64:64 + E], 1.0, None, ALU.add)
                        dve.wait_ge(cols, 1)
                        dve.tensor_copy(slots[:], psum[:, 6, 0:N // P])

        def scatter_rows(tag, rows, table, slots, K, bound=None):
            sent = sem(tag + "_sent")

            def on_gpsimd(pool):
                for n in range(K * NT):
                    extra = {} if bound is None else dict(bounds_check=bound, oob_is_err=False)
                    pool.indirect_dma_start(
                        out=table, out_offset=bass.IndirectOffsetOnAxis(ap=slots[:, n:n + 1], axis=0),
                        in_=rows[:, n % NT, :], in_offset=None, **extra).then_inc(sent, 16)
                pool.wait_ge(sent, 16 * K * NT)
            return on_gpsimd

        def stage_scatter(*given, **named):
            with nc.Block() as block:
                block.gpsimd(scatter_rows(*given, **named))

        def stage_gather(tag, table, slots, bufs, bound=None):
            got = sem(tag + "_got")
            with nc.Block() as block:
                @block.gpsimd
                def _(pool):
                    for k, buf in enumerate(bufs):
                        for i in range(NT):
                            n = k * NT + i
                            extra = {} if bound is None else dict(bounds_check=bound, oob_is_err=False)
                            pool.indirect_dma_start(
                                out=buf[:, i, :], out_offset=None, in_=table,
                                in_offset=bass.IndirectOffsetOnAxis(ap=slots[:, n:n + 1], axis=0),
                                **extra).then_inc(got, 16)
                    pool.wait_ge(got, 16 * NT * len(bufs))

        def stage_sorted_glu(tag, tiles, halves, weights, tile_expert, last_tile, rows_in, rows_out):
            NE = weights.shape[0]
            ring = 4 // halves
            F = halves * FU
            NF = F // P
            W = halves * UNIT
            with ExitStack() as own:
                r_in = sb(tag + "_rin", [P, 2, D], on=own)
                rT = sb(tag + "_rT", [P, 2, KD, P], on=own)
                sg = sb(tag + "_sg", [P, halves, FU], on=own)
                h = sb(tag + "_h", [P, halves, FU], on=own)
                hT = sb(tag + "_hT", [P, halves, FU], on=own)
                r_out = sb(tag + "_rout", [P, 2, D], on=own)
                w_in = [sem(f"{tag}_w_in{r}") for r in range(2)]
                x_in = [sem(f"{tag}_x_in{r}") for r in range(2)]
                stored = [sem(f"{tag}_stored{r}") for r in range(2)]
                wring = sb(tag + "_wring", [P, ring, W], on=own)
                rows_t, rows_c, gate, silu, up, hidden, hid_t, hid_c, down, outc = (
                    sem(f"{tag}_{n}") for n in ("rows_t", "rows_c", "gate", "silu", "up", "hidden",
                                                "hid_t", "hid_c", "down", "outc"))
                src = rows_in.rearrange("(j p) d -> j p d", p=P)
                dst = rows_out.rearrange("(j p) d -> j p d", p=P)
                with nc.Block() as block:
                    @block.sync
                    def _(sp):
                        def load(e, r, place, first):
                            if not first:
                                sp.wait_ge(down, sp.value_load(last_tile[0:1, bass.ds(e - ring, 1)], min_val=1,
                                                               max_val=tiles + 1))
                            sp.dma_start(wring[:, place, :], weights[bass.ds(e, 1)].rearrange("e p n -> p (e n)")
                                         ).then_inc(w_in[r], 16)
                        for place in range(ring):
                            if place >= 2:
                                sp.wait_ge(w_in[place % 2], 16 * (place // 2) + place % 2)
                            load(place, place % 2, place, True)
                        with sp.Fori(1, NE // ring) as i:
                            for place in range(ring):
                                e = ring * i + place
                                r = place % 2
                                sp.wait_ge(w_in[r], 8 * (e - r) + r)
                                load(e, r, place, False)

                    @block.gpsimd
                    def _(pool):
                        def load(i, r, first):
                            j = 2 * i + r
                            if not first:
                                pool.wait_ge(rows_t, j - 1)
                            pool.dma_start(r_in[:, r, :], src[bass.ds(j, 1)].rearrange("j p d -> p (j d)")
                                           ).then_inc(x_in[r], 16)
                        load(0, 0, True)
                        load(0, 1, True)
                        with pool.Fori(1, tiles // 2) as i:
                            load(i, 0, False)
                            load(i, 1, False)

                    def wgate(place, k, v):
                        return wring[:, place, k * F + v * FU:k * F + (v + 1) * FU].rearrange("p s n -> p (s n)")

                    def wup(place, k, v):
                        return wring[:, place, (KD + k) * F + v * FU:(KD + k) * F + (v + 1) * FU].rearrange("p s n -> p (s n)")

                    def wdown(place, f):
                        return wring[:, place, 2 * KD * F + f * D:2 * KD * F + (f + 1) * D].rearrange("p s n -> p (s n)")

                    @block.tensor
                    def _(pe):
                        def turn_rows(i, r, first=False):
                            pe.wait_ge(x_in[r], 16 * i + 16)
                            if not first:
                                pe.wait_ge(rows_c, 2 * i + r)
                            for k in range(KD):
                                last = pe.transpose(psum[:, 6, k * P:(k + 1) * P], r_in[:, r, k * P:(k + 1) * P], ident[:])
                            last.then_inc(rows_t, 1)

                        def turn_hidden(j):
                            for v in range(halves):
                                pe.wait_ge(hidden, j * halves + v + 1)
                                for q in range(TPC):
                                    last = pe.transpose(psum[:, 4 + v, q * P:(q + 1) * P], h[:, v, q * P:(q + 1) * P], ident[:])
                                last.then_inc(hid_t, 1)

                        def expert_of(j):
                            return pe.value_load(tile_expert[0:1, bass.ds(j, 1)], min_val=0, max_val=NE - 1)

                        def down_product(j, first=False):
                            place = bass.ds(expert_of(j) % ring, 1)
                            pe.wait_ge(hid_c, j * halves + halves)
                            if not first:
                                pe.wait_ge(outc, j)
                            for f in range(NF):
                                last = pe.matmul(psum[:, 7, 0:D], hT[:, f // TPC, (f % TPC) * P:(f % TPC + 1) * P],
                                                 wdown(place, f), start=(f == 0), stop=(f == NF - 1))
                            last.then_inc(down, 1)

                        def tile(i, r, first=False, second=False, last_tile=False):
                            j = 2 * i + r
                            e = expert_of(j)
                            place = bass.ds(e % ring, 1)
                            pe.wait_ge(rows_c, j + 1)
                            pe.wait_ge(w_in[0], (e // 2 + 1) * 16)
                            pe.wait_ge(w_in[1], ((e + 1) // 2) * 16 + 1)
                            for v in range(halves):
                                if not first:
                                    pe.wait_ge(silu, (j - 1) * halves + v + 1)
                                for k in range(KD):
                                    last = pe.matmul(psum[:, v, :], rT[:, r, k, :], wgate(place, k, v),
                                                     start=(k == 0), stop=(k == KD - 1))
                                last.then_inc(gate, 1)
                            if not first:
                                turn_hidden(j - 1)
                            if not last_tile:
                                turn_rows(i + r, 1 - r)
                            for v in range(halves):
                                if not first:
                                    pe.wait_ge(hidden, (j - 1) * halves + v + 1)
                                for k in range(KD):
                                    last = pe.matmul(psum[:, 2 + v, :], rT[:, r, k, :], wup(place, k, v),
                                                     start=(k == 0), stop=(k == KD - 1))
                                last.then_inc(up, 1)
                            if not first:
                                down_product(j - 1, first=second)

                        pe.sem_inc(down, 1)
                        pe.sem_inc(w_in[1], 1)
                        turn_rows(0, 0, first=True)
                        tile(0, 0, first=True)
                        tile(0, 1, second=True)
                        with pe.Fori(1, tiles // 2 - 1) as i:
                            tile(i, 0)
                            tile(i, 1)
                        tile(tiles // 2 - 1, 0)
                        tile(tiles // 2 - 1, 1, last_tile=True)
                        turn_hidden(tiles - 1)
                        down_product(tiles - 1)

                    @block.scalar
                    def _(act):
                        def silu_part(j, first=False):
                            for v in range(halves):
                                act.wait_ge(gate, j * halves + v + 1)
                                if not first:
                                    act.wait_ge(hidden, (j - 1) * halves + v + 1)
                                act.activation(sg[:, v, :], psum[:, v, :], ACT.Silu).then_inc(silu, 1)

                        def rows_part(j, r, first=False):
                            act.wait_ge(rows_t, j + 1)
                            if not first:
                                act.wait_ge(up, (j - 1) * halves)
                            act.copy(rT[:, r, :, :].rearrange("p k t -> p (k t)"), psum[:, 6, 0:D]).then_inc(rows_c, 1)

                        def out_part(i, r, first=False):
                            j = 2 * i + r
                            act.wait_ge(down, j + 2)
                            if not first:
                                act.wait_ge(stored[r], 16 * i)
                            act.copy(r_out[:, r, :], psum[:, 7, 0:D]).then_inc(outc, 1)
                            act.wait_ge(outc, j + 1)
                            act.dma_start(dst[bass.ds(j, 1)].rearrange("j p d -> p (j d)"), r_out[:, r, :]
                                          ).then_inc(stored[r], 16)

                        rows_part(0, 0, first=True)
                        silu_part(0, first=True)
                        rows_part(1, 1, first=True)
                        silu_part(1)
                        rows_part(2, 0)
                        out_part(0, 0, first=True)
                        silu_part(2)
                        rows_part(3, 1)
                        out_part(0, 1, first=True)
                        with act.Fori(1, tiles // 2 - 1) as i:
                            silu_part(2 * i + 1)
                            rows_part(2 * i + 2, 0)
                            out_part(i, 0)
                            silu_part(2 * i + 2)
                            rows_part(2 * i + 3, 1)
                            out_part(i, 1)
                        silu_part(tiles - 1)
                        out_part(tiles // 2 - 1, 0)
                        out_part(tiles // 2 - 1, 1)
                        for r in range(2):
                            act.wait_ge(stored[r], 16 * (tiles // 2))

                    @block.vector
                    def _(dve):
                        def multiply(j, first):
                            for v in range(halves):
                                dve.wait_ge(up, j * halves + v + 1)
                                dve.wait_ge(silu, j * halves + v + 1)
                                if not first:
                                    dve.wait_ge(hid_t, (j - 1) * halves + v + 1)
                                dve.tensor_tensor(h[:, v, :], sg[:, v, :], psum[:, 2 + v, :], ALU.mult).then_inc(hidden, 1)

                        def copy_hidden(j, first):
                            for v in range(halves):
                                dve.wait_ge(hid_t, j * halves + v + 1)
                                if not first:
                                    dve.wait_ge(down, j + 1)
                                dve.tensor_copy(hT[:, v, :], psum[:, 4 + v, :]).then_inc(hid_c, 1)

                        multiply(0, True)
                        copy_hidden(0, True)
                        with dve.Fori(1, tiles) as j:
                            multiply(j, False)
                            copy_hidden(j, False)

        def as_tokens(feat):
            return feat[:].rearrange("p k t -> p (k t)").rearrange("p (i d) -> p i d", d=D)

        def stage_l0_route(own, rows):
            E = E0
            wr = sb("r0_w", [P, KD, E], on=own)
            L = sb("r0_L", [P, NT, E], on=own)
            tmp = sb("r0_tmp", [P, NT, E], on=own)
            onehot = sb("r0_oh", [P, NT, E], on=own)
            top = sb("r0_top", [P, NT], on=own)
            small = sb("r0_small", [P, NT], on=own)
            loaded, done, order, toped, score = (sem("r0_" + n) for n in ("loaded", "done", "order", "toped", "score"))
            with nc.Block() as block:
                @block.sync
                def _(sp):
                    sp.dma_start(wr[:], a["l0_gate"]).then_inc(loaded, 16)

                @block.tensor
                def _(pe):
                    pe.wait_ge(loaded, 16)
                    logits_on_pe(pe, fc, wr, E).then_inc(done, 1)

                @block.scalar
                def _(act):
                    act.wait_ge(toped, 1)
                    act.activation(small[:], top[:], ACT.Sigmoid).then_inc(score, 1)

                @block.vector
                def _(dve):
                    link = chain(dve, order)
                    dve.wait_ge(done, 1)
                    link(dve.tensor_copy(L[:].rearrange("p i e -> p (i e)"), psum[:, 0, 0:NT * E]))
                    pick(dve, link, L[:], top[:], onehot[:], tmp[:], small[:], E)
                    dve.engine_nop().then_inc(toped, 1)
                    dve.wait_ge(score, 1)
                    for i in range(NT):
                        dve.tensor_scalar(rows[:, i, :], ctok[:, i, :], small[:, i:i + 1], None, ALU.mult)
            return onehot

        def stage_add_to_x(tag, terms):
            order = sem(tag + "_order")
            with nc.Block() as block:
                @block.vector
                def _(dve):
                    link = chain(dve, order)
                    for buf, factor in terms:
                        if isinstance(factor, float):
                            link(dve.scalar_tensor_tensor(
                                out=xtok[:].rearrange("p i d -> p (i d)"), in0=buf.rearrange("p i d -> p (i d)"),
                                scalar=factor, in1=xtok[:].rearrange("p i d -> p (i d)"), op0=ALU.mult, op1=ALU.add))
                        else:
                            for i in range(NT):
                                ins = dve.scalar_tensor_tensor(out=xtok[:, i, :], in0=buf[:, i, :],
                                                               scalar=factor[:, i:i + 1], in1=xtok[:, i, :],
                                                               op0=ALU.mult, op1=ALU.add)
                            link(ins)

        def layer0():
            stage_to_features("a0", xtok, fx)
            stage_l0_cond()
            stage_to_tokens("b0", fc, ctok)
            with ExitStack() as own:
                slots = sb("slots0", [P, NT], U32, on=own)
                tile_expert = sb("tile_expert0", [1, SLOT_TILES0], I32, on=own)
                last_tile = sb("last_tile0", [1, E0], I32, on=own)
                rows = as_tokens(fx)
                with ExitStack() as route:
                    onehot = stage_l0_route(route, rows)
                    stage_slots("s0", [onehot], E0, SLOT_TILES0, slots, tile_expert, last_tile)
                stage_tables_zeroed()
                stage_glu("g0", fc, a["l0_shared"], beside=scatter_rows("sc0", rows, rows0_in, slots, 1))
                stage_sorted_glu("e0", SLOT_TILES0, 1, a["l0_routed"], tile_expert, last_tile, rows0_in, rows0_out)
                stage_gather("ga0", rows0_out, slots, [rows])
                stage_add_to_x("x0", [(acc[:], 1.0), (rows, 1.0)])

        def stage_l1_project(w5, U, hm, differ):
            q = acc[:].rearrange("p i d -> p (i d)").rearrange("p (o t) -> p o t", o=KD)
            WQ, WK, WT = 0, 1, 3
            with ExitStack() as own:
                tp = sb("l1_tp", [P, KD, B], on=own)
                m8 = sb("l1p_m8", [P, TPB, S], U8, on=own)
                m1 = sb("l1p_m1", [P, S], U8, on=own)
                ne = sb("l1p_ne", [P, S], on=own)
                cnt = sb("l1p_cnt", [P, TPB], on=own)
                bd = sb("l1_bd", [P, KD, B, P], on=own)
                part = sb("l1_part", [P, KD, B, 2], on=own)
                junk = sb("l1_junk", [P, CH], on=own)
                qmod = sb("l1_qmod", [P, KD, B], on=own)
                qm = sb("l1_qm", [P, KD, B, HEADS], on=own)
                masks, hm1, loaded, tpd, qd, qc, order, ad, asum, qmd, ud, mloaded, flagd, counted = (
                    sem("l1p_" + n) for n in ("masks", "hm1", "loaded", "tpd", "qd", "qc", "order", "ad", "asum", "qmd",
                                              "ud", "mloaded", "flagd", "counted"))
                with nc.Block() as block:
                    @block.sync
                    def _(sp):
                        sp.dma_start(m8[:], a["mask"].rearrange("(i p) s -> p i s", p=P)).then_inc(mloaded, 16)
                        sp.dma_start(m1[:], a["mask"][0, :].partition_broadcast(P)).then_inc(mloaded, 16)
                        sp.dma_start(w5[:], a["l1_w"]).then_inc(loaded, 16)

                    @block.gpsimd
                    def _(pool):
                        full = ones[:].rearrange("p (h e) -> p h e", h=8)
                        pool.affine_select(out=hm[:], in_=full, compare_op=ALU.is_ge, fill=0.0, base=0,
                                           pattern=[[-HW, 8], [0, HW]], channel_multiplier=1).then_inc(hm1, 1)
                        pool.wait_ge(hm1, 1)
                        pool.affine_select(out=hm[:], in_=hm[:], compare_op=ALU.is_ge, fill=0.0, base=HW - 1,
                                           pattern=[[HW, 8], [0, HW]], channel_multiplier=-1).then_inc(masks, 1)

                    @block.tensor
                    def _(pe):
                        pe.wait_ge(loaded, 16)
                        for o in range(KD):
                            for k in range(KD):
                                last = pe.matmul(psum[:, 7, o * B:(o + 1) * B], w5[:, WT, k, o * P:(o + 1) * P],
                                                 condT[:, k, :], start=(k == 0), stop=(k == KD - 1))
                        last.then_inc(tpd, 1)
                        for n in range(8):
                            o, c = n // NCH, n % NCH
                            if n >= 4:
                                pe.wait_ge(qc, n - 3)
                            for k in range(KD):
                                last = pe.matmul(psum[:, n % 4, :], w5[:, WQ, k, o * P:(o + 1) * P],
                                                 fx[:, k, c * CH:(c + 1) * CH], start=(k == 0), stop=(k == KD - 1))
                            last.then_inc(qd, 1)
                        pe.wait_ge(order, 1)
                        pe.wait_ge(qc, 8)
                        for n in range(8):
                            o, b, c = n // 4, n // 2 % 2, n % 2
                            if n >= 4:
                                pe.wait_ge(asum, n - 3)
                            last = pe.matmul(psum[:, n % 4, :], bd[:, o, b, :],
                                             q[:, o, b * S + c * CH:b * S + (c + 1) * CH], start=True, stop=True)
                            last.then_inc(ad, 1)
                        pe.wait_ge(counted, 2 * TPB)
                        pe.matmul(psum[0:1, 6, 0:TPB], ones[:, 0:1], cnt[:], start=True, stop=True).then_inc(flagd, 1)
                        pe.wait_ge(qmd, 1)
                        for d in range(KD):
                            for b in range(B):
                                for o in range(KD):
                                    g = (d * B + b) * HEADS
                                    last = pe.matmul(psum[:, 7, g:g + HEADS], w5[:, WK, o, d * P:(d + 1) * P],
                                                     qm[:, o, b, :], start=(o == 0), stop=(o == KD - 1))
                        last.then_inc(ud, 1)

                    @block.scalar
                    def _(act):
                        for n in range(8):
                            act.wait_ge(qd, n + 1)
                            act.copy(q[:, n // NCH, n % NCH * CH:(n % NCH + 1) * CH], psum[:, n % 4, :]).then_inc(qc, 1)

                    @block.vector
                    def _(dve):
                        dve.memset(qm[:], 0.0)
                        dve.wait_ge(mloaded, 32)
                        for i in range(TPB):
                            if i:
                                dve.wait_ge(counted, 2 * i)
                            dve.tensor_tensor(ne[:], m8[:, i, :], m1[:], ALU.not_equal).then_inc(counted, 1)
                            dve.wait_ge(counted, 2 * i + 1)
                            dve.tensor_reduce(cnt[:, i:i + 1], ne[:], AX_X, ALU.add).then_inc(counted, 1)
                        dve.wait_ge(tpd, 1)
                        dve.tensor_copy(tp[:].rearrange("p o b -> p (o b)"), psum[:, 7, 0:KD * B]).then_inc(masks, 1)
                        dve.wait_ge(masks, 2)
                        for o in range(KD):
                            for b in range(B):
                                last = dve.tensor_scalar(bd[:, o, b, :], hm[:].rearrange("p h e -> p (h e)"),
                                                         tp[:, o, b:b + 1], None, ALU.mult)
                        last.then_inc(order, 1)
                        for n in range(8):
                            o, b, c = n // 4, n // 2 % 2, n % 2
                            dve.wait_ge(ad, n + 1)
                            if n:
                                dve.wait_ge(asum, n)
                            dve.tensor_tensor_reduce(junk[:], q[:, o, b * S + c * CH:b * S + (c + 1) * CH],
                                                     psum[:, n % 4, :], 1.0, 0.0, ALU.mult, ALU.add,
                                                     part[:, o, b, c:c + 1]).then_inc(asum, 1)
                        dve.wait_ge(asum, 8)
                        dve.tensor_tensor(qmod[:], part[:, :, :, 0], part[:, :, :, 1], ALU.add).then_inc(order, 1)
                        dve.wait_ge(order, 2)
                        for o in range(KD):
                            for b in range(B):
                                last = dve.tensor_scalar(qm[:, o, b, o * 8:(o + 1) * 8], hm[:, :, 0],
                                                         qmod[:, o, b:b + 1], float(HW) ** -0.5, ALU.mult, ALU.mult)
                        last.then_inc(qmd, 1)
                        dve.wait_ge(ud, 1)
                        dve.tensor_copy(U[:].rearrange("p d b h -> p (d b h)"), psum[:, 7, 0:KD * B * HEADS])
                        dve.wait_ge(flagd, 1)
                        dve.tensor_reduce(cnt[0:1, 0:1], psum[0:1, 6, 0:TPB], AX_X, ALU.add).then_inc(counted, 1)
                        dve.wait_ge(counted, 2 * TPB + 1)
                        dve.tensor_copy(differ[:], cnt[0:1, 0:1])

        def stage_l1_attend(U):
            with ExitStack() as own:
                m8 = sb("l1_m8", [P, TPB, S], U8, on=own)
                lim = sb("l1_lim", [P, TPB, S], on=own)
                ub = sb("l1_ub", [P, KD, P], on=own)
                row = sb("l1_row", [P, S], on=own)
                ms = sb("l1_ms", [P, 2, S], on=own)
                pT = sb("l1_pT", [P, S], on=own)
                mx = sb("l1_mx", [P, TPB], on=own)
                spare = sb("l1_spare", [P, 1], on=own)
                sums = sb("l1_sums", [P, TPB], on=own)
                rs = sb("l1_rs", [P, TPB], on=own)
                loaded, lims, ubd, sd, rowc, masked, negd, expd, td, tcv, tca, pvd, rsd, od = (
                    sem("l1a_" + n) for n in ("loaded", "lims", "ubd", "sd", "rowc", "masked", "negd", "expd", "td",
                                              "tcv", "tca", "pvd", "rsd", "od"))
                half = S // 2
                with nc.Block() as block:
                    @block.sync
                    def _(sp):
                        sp.dma_start(m8[:], a["mask"].rearrange("(i p) s -> p i s", p=P)).then_inc(loaded, 16)

                    def heads(eng, body):
                        body(0, 0, 0, True)
                        with eng.Fori(1, HEADS) as h:
                            body(0, h, h, False)
                        with eng.Fori(0, HEADS) as h:
                            body(1, h, h + HEADS, False)

                    @block.tensor
                    def _(pe):
                        def body(b, h, g, first):
                            pe.wait_ge(ubd, g + 1)
                            if not first:
                                pe.wait_ge(rowc, g)
                            for c in range(2):
                                for k in range(KD):
                                    last = pe.matmul(psum[:, c, :], ub[:, k, :],
                                                     fx[:, k, b * S + c * CH:b * S + (c + 1) * CH],
                                                     start=(k == 0), stop=(k == KD - 1))
                            last.then_inc(sd, 1)
                            for i in range(TPB):
                                pe.wait_ge(expd, TPB * g + i + 1)
                                if not (first and i == 0):
                                    pe.wait_ge(tcv, TPB * g + i)
                                    pe.wait_ge(tca, TPB * g + i)
                                for s in range(8):
                                    last = pe.transpose(psum[:, 2 + s // 4, (s % 4) * P:(s % 4 + 1) * P],
                                                        ms[:, i % 2, s * P:(s + 1) * P], ident[:])
                                last.then_inc(td, 1)
                                pe.wait_ge(tcv, TPB * g + i + 1)
                                pe.wait_ge(tca, TPB * g + i + 1)
                                if i == 0 and not first:
                                    pe.wait_ge(od, g)
                                for s in range(8):
                                    last = pe.matmul(psum[:, 6, i * HW:(i + 1) * HW], pT[:, s * P:(s + 1) * P],
                                                     ctok[:, b * TPB + s, bass.ds(h * HW, HW)],
                                                     start=(s == 0), stop=(s == 7))
                                last.then_inc(pvd, 1)
                        heads(pe, body)

                    @block.scalar
                    def _(act):
                        def body(b, h, g, first):
                            act.wait_ge(sd, g + 1)
                            if not first:
                                act.wait_ge(masked, TPB * g)
                            act.copy(row[:], psum[:, 0:2, :].rearrange("p c t -> p (c t)")).then_inc(rowc, 1)
                            for i in range(TPB):
                                act.wait_ge(negd, TPB * g + i + 1)
                                if i == 0 and not first:
                                    act.wait_ge(rsd, g)
                                act.activation(ms[:, i % 2, :], ms[:, i % 2, :], ACT.Exp, bias=mx[:, i:i + 1],
                                               accum_out=sums[:, i:i + 1]).then_inc(expd, 1)
                                act.wait_ge(td, TPB * g + i + 1)
                                if not (first and i == 0):
                                    act.wait_ge(pvd, TPB * g + i)
                                act.copy(pT[:, half:S], psum[:, 3, :]).then_inc(tca, 1)
                        heads(act, body)

                    @block.vector
                    def _(dve):
                        dve.wait_ge(loaded, 16)
                        dve.tensor_scalar(lim[:], m8[:], FMAX, -FMAX, ALU.mult, ALU.add).then_inc(lims, 1)
                        dve.wait_ge(lims, 1)

                        def body(b, h, g, first):
                            if not first:
                                dve.wait_ge(sd, g)
                            dve.tensor_copy(ub[:], U[:, :, b, bass.ds(h, 1)].to_broadcast([P, KD, P])).then_inc(ubd, 1)
                            for i in range(TPB):
                                if i == 0:
                                    dve.wait_ge(rowc, g + 1)
                                if not (first and i < 2):
                                    dve.wait_ge(td, TPB * g + i - 1)
                                    if i < 2:
                                        dve.wait_ge(expd, TPB * g)
                                dve.memset(spare[:], 0.0)
                                dve.tensor_tensor_reduce(ms[:, i % 2, :], row[:], lim[:, i, :], 1.0, -FMAX, ALU.add,
                                                         ALU.max, mx[:, i:i + 1]).then_inc(masked, 1)
                                dve.wait_ge(masked, TPB * g + i + 1)
                                dve.tensor_scalar(mx[:, i:i + 1], mx[:, i:i + 1], -1.0, None, ALU.mult).then_inc(negd, 1)
                                if i >= 1:
                                    transposed(g, i - 1, first)
                            transposed(g, TPB - 1, first)
                            dve.wait_ge(expd, TPB * g + TPB)
                            dve.reciprocal(rs[:], sums[:]).then_inc(rsd, 1)
                            dve.wait_ge(rsd, g + 1)
                            dve.wait_ge(pvd, TPB * g + TPB)
                            dve.tensor_tensor(acc[:, b * TPB:(b + 1) * TPB, bass.ds(h * HW, HW)],
                                              psum[:, 6, 0:TPB * HW].rearrange("p (i e) -> p i e", e=HW),
                                              rs[:].unsqueeze(2).to_broadcast([P, TPB, HW]), ALU.mult).then_inc(od, 1)

                        def transposed(g, i, first):
                            dve.wait_ge(td, TPB * g + i + 1)
                            if not (first and i == 0):
                                dve.wait_ge(pvd, TPB * g + i)
                            dve.tensor_copy(pT[:, 0:half], psum[:, 2, :]).then_inc(tcv, 1)
                        heads(dve, body)

        def stage_rows_times(tag, feat, w, tok):
            done, copied = sem(tag + "_done"), sem(tag + "_copied")
            with nc.Block() as block:
                @block.tensor
                def _(pe):
                    for n in range(8):
                        if n >= 4:
                            pe.wait_ge(copied, n - 3)
                        for i in range(2):
                            for k in range(KD):
                                last = pe.matmul(psum[:, n % 4, i * D:(i + 1) * D],
                                                 feat[:, k, (2 * n + i) * P:(2 * n + i + 1) * P], w[:, k, :],
                                                 start=(k == 0), stop=(k == KD - 1))
                        last.then_inc(done, 1)

                @block.vector
                def _(dve):
                    for n in range(8):
                        dve.wait_ge(done, n + 1)
                        dve.tensor_copy(tok[:, 2 * n:2 * n + 2, :].rearrange("p i d -> p (i d)"),
                                        psum[:, n % 4, :]).then_inc(copied, 1)

        def stage_l1_gating(rw, shared=None):
            E = E1
            n = NT if shared is None else B

            def over_e(v, E):
                return v.unsqueeze(2).to_broadcast([P, n, E])
            tag = "g1_" if shared is None else "g1s_"
            with ExitStack() as own:
                sim = sb(tag + "sim", [P, KD, E], on=own)
                sim2 = sb(tag + "sim2", [P, KD, E], on=own)
                gb = sb(tag + "gb", [P, E], on=own)
                ns = sb(tag + "ns", [P, E], on=own)
                ss = sb(tag + "ss", [P, n], on=own)
                junk = sb(tag + "junk", [P, D], on=own)
                L, tmp, oh1, oh2, gated = (sb(tag + "" + m, [P, n, E], on=own) for m in ("L", "tmp", "oh1", "oh2", "gated"))
                top, small = (sb(tag + "" + m, [P, n], on=own) for m in ("top", "small"))
                loaded, sq, done, order, roots, rooted, shifted, expd = (
                    sem(tag + m) for m in ("loaded", "sq", "done", "order", "roots", "rooted", "shifted", "expd"))
                with nc.Block() as block:
                    @block.sync
                    def _(sp):
                        sp.dma_start(sim[:], a["l1_sim"]).then_inc(loaded, 16)
                        sp.dma_start(gb[:], a["l1_gates"].partition_broadcast(P)).then_inc(loaded, 16)

                    @block.tensor
                    def _(pe):
                        pe.wait_ge(loaded, 32)
                        if shared is None:
                            logits_on_pe(pe, fc, sim, E)
                        else:
                            for b in range(B):
                                for k in range(KD):
                                    pe.matmul(psum[:, 0, b * E:(b + 1) * E], shared[:, k, b, :], sim[:, k, :],
                                              start=(k == 0), stop=(k == KD - 1))
                            for b in range(B):
                                for k in range(KD):
                                    pe.matmul(psum[:, 2, b:b + 1], shared[:, k, b, :], shared[:, k, b, 0:1],
                                              start=(k == 0), stop=(k == KD - 1))
                        pe.wait_ge(sq, 1)
                        for k in range(KD):
                            last = pe.matmul(psum[:, 1, 0:E], ones[:], sim2[:, k, :], start=(k == 0), stop=(k == KD - 1))
                        last.then_inc(done, 1)

                    @block.scalar
                    def _(act):
                        act.wait_ge(loaded, 32)
                        act.activation(gb[:], gb[:], ACT.Sigmoid).then_inc(rooted, 1)
                        act.wait_ge(roots, 1)
                        act.activation(ns[:], ns[:], ACT.Sqrt)
                        act.activation(ss[:], ss[:], ACT.Sqrt).then_inc(rooted, 1)
                        act.wait_ge(shifted, 1)
                        act.activation(tmp[:], tmp[:], ACT.Exp).then_inc(expd, 1)

                    @block.vector
                    def _(dve):
                        link = chain(dve, order)
                        dve.wait_ge(loaded, 32)
                        dve.tensor_tensor(sim2[:], sim[:], sim[:], ALU.mult).then_inc(sq, 1)
                        for i in range(NT if shared is None else 0):
                            link(dve.tensor_tensor_reduce(junk[:], ctok[:, i, :], ctok[:, i, :], 1.0, 0.0, ALU.mult,
                                                          ALU.add, ss[:, i:i + 1]))
                        if shared is None:
                            link(dve.tensor_scalar(ss[:], ss[:], 1e-12, None, ALU.add))
                        dve.wait_ge(done, 1)
                        if shared is not None:
                            link(dve.tensor_scalar(ss[:], psum[:, 2, 0:B], 1e-12, None, ALU.add))
                        dve.tensor_scalar(ns[:], psum[:, 1, 0:E], 1e-12, None, ALU.add).then_inc(roots, 1)
                        dve.wait_ge(rooted, 2)
                        link(dve.reciprocal(ns[:], ns[:]))
                        link(dve.reciprocal(ss[:], ss[:]))
                        link(dve.tensor_tensor(L[:], psum[:, 0, 0:n * E].rearrange("p (i e) -> p i e", e=E),
                                               over_e(ss[:], E), ALU.mult))
                        link(dve.tensor_tensor(L[:], L[:], ns[:].unsqueeze(1).to_broadcast([P, n, E]), ALU.mult))
                        link(dve.tensor_tensor(L[:], L[:], gb[:].unsqueeze(1).to_broadcast([P, n, E]), ALU.subtract))
                        pick(dve, link, L[:], top[:], oh1[:], tmp[:], small[:], E, n)
                        link(dve.scalar_tensor_tensor(out=gated[:], in0=oh1[:], scalar=-1e30, in1=L[:],
                                                      op0=ALU.mult, op1=ALU.add))
                        pick(dve, link, gated[:], small[:], oh2[:], tmp[:], top[:], E, n)
                        link(dve.tensor_tensor(oh1[:], oh1[:], oh2[:], ALU.add))
                        link(dve.tensor_scalar(gated[:], L[:], 0.0, None, ALU.max))
                        link(dve.tensor_scalar(L[:], gated[:], 0.0, None, ALU.is_gt))
                        link(dve.tensor_reduce(small[:], L[:], AX_X, ALU.max))
                        link(dve.tensor_scalar(small[:], small[:], 0.0, None, ALU.is_equal))
                        link(dve.tensor_tensor(oh1[:], oh1[:], over_e(small[:], E), ALU.mult))
                        link(dve.tensor_tensor(L[:], L[:], oh1[:], ALU.add))
                        link(dve.tensor_reduce(top[:], gated[:], AX_X, ALU.max))
                        dve.tensor_tensor(tmp[:], gated[:], over_e(top[:], E), ALU.subtract).then_inc(shifted, 1)
                        dve.wait_ge(expd, 1)
                        link(dve.tensor_tensor(tmp[:], tmp[:], L[:], ALU.mult))
                        link(dve.tensor_reduce(small[:], tmp[:], AX_X, ALU.add))
                        link(dve.reciprocal(small[:], small[:]))
                        dve.tensor_tensor(rw[:], tmp[:], over_e(small[:], E), ALU.mult)

        def stage_l1_qkv(wbuf, rw, qkv):
            C3 = 3 * H1
            w = wbuf[:].rearrange("p r n -> p (r n)").rearrange("p (e k c) -> p e k c", e=E1, k=KD)
            loaded, cleared, done, added = (sem("q1_" + n) for n in ("loaded", "cleared", "done", "added"))
            with nc.Block() as block:
                @block.sync
                def _(sp):
                    sp.dma_start(w, a["l1_qkv"]).then_inc(loaded, 16)

                @block.tensor
                def _(pe):
                    def expert(e, first):
                        for i in range(NT):
                            if not (first and i < 4):
                                pe.wait_ge(added, NT * e + i - 3)
                            for k in range(KD):
                                last = pe.matmul(psum[:, i % 4, 0:C3], fc[:, k, i * P:(i + 1) * P],
                                                 w[:, bass.ds(e, 1), k, :].rearrange("p e c -> p (e c)"),
                                                 start=(k == 0), stop=(k == KD - 1))
                            last.then_inc(done, 1)
                    pe.wait_ge(loaded, 16)
                    expert(0, True)
                    with pe.Fori(1, E1) as e:
                        expert(e, False)

                @block.vector
                def _(dve):
                    dve.memset(qkv[:], 0.0).then_inc(cleared, 1)
                    dve.wait_ge(cleared, 1)

                    def expert(e, first):
                        for i in range(NT):
                            dve.wait_ge(done, NT * e + i + 1)
                            if not first:
                                dve.wait_ge(added, NT * (e - 1) + i + 1)
                            dve.scalar_tensor_tensor(out=qkv[:, i, :], in0=psum[:, i % 4, 0:C3],
                                                     scalar=rw[:, i, bass.ds(e, 1)], in1=qkv[:, i, :],
                                                     op0=ALU.mult, op1=ALU.add).then_inc(added, 1)
                    expert(0, True)
                    with dve.Fori(1, E1) as e:
                        expert(e, False)

        def stage_l1_causal(qkv, aoT, rinv):
            qk = acc[:].rearrange("p i d -> p (i d)").rearrange("p (o t) -> p o t", o=2)
            scale = float(H1) ** -0.5
            with ExitStack() as own:
                cm = sb("c1_cm", [P, P], on=own)
                zero = sb("c1_zero", [P, P], on=own)
                sm = sb("c1_sm", [P, 2, S], on=own)
                pT = sb("c1_pT", [P, 2, S], on=own)
                mx = sb("c1_mx", [P, NT], on=own)
                sums = sb("c1_sums", [P, NT], on=own)
                cleared, cmd, td, tc, sd, scaled, sc2, maxd, negd, expd, ptd, ptc, pvd, pvc = (
                    sem("c1_" + n) for n in ("cleared", "cmd", "td", "tc", "sd", "scaled", "sc2", "maxd", "negd", "expd",
                                             "ptd", "ptc", "pvd", "pvc"))
                with nc.Block() as block:
                    @block.gpsimd
                    def _(pool):
                        pool.memset(zero[:], 0.0).then_inc(cleared, 1)
                        pool.wait_ge(cleared, 1)
                        pool.affine_select(out=cm[:], in_=zero[:], compare_op=ALU.is_ge, fill=-FMAX, base=0,
                                           pattern=[[-1, P]], channel_multiplier=1).then_inc(cmd, 1)

                    @block.tensor
                    def _(pe):
                        for n in range(8):
                            o, c = n // NCH, n % NCH
                            if n >= 2:
                                pe.wait_ge(tc, n - 1)
                            for t in range(TPC):
                                last = pe.transpose(psum[:, n % 2, t * P:(t + 1) * P],
                                                    qkv[:, c * TPC + t, o * H1:(o + 1) * H1], ident[:])
                            last.then_inc(td, 1)
                        pe.wait_ge(tc, 8)

                        def scores(n):
                            b, i = n // TPB, n % TPB
                            if n >= 1:
                                pe.wait_ge(sc2, n)
                            for c in range(i // TPC + 1):
                                w = min(CH, (i + 1) * P - c * CH)
                                last = pe.matmul(psum[:, c, 0:w], qk[:, 0, n * P:(n + 1) * P],
                                                 qk[:, 1, b * S + c * CH:b * S + c * CH + w], start=True, stop=True)
                            last.then_inc(sd, 1)

                        scores(0)
                        for n in range(NT):
                            b, i = n // TPB, n % TPB
                            if n + 1 < NT:
                                scores(n + 1)
                            pe.wait_ge(expd, n + 1)
                            if n >= 1:
                                pe.wait_ge(ptc, n)
                            for s in range(i + 1):
                                last = pe.transpose(psum[:, 2 + s // TPC, (s % TPC) * P:(s % TPC + 1) * P],
                                                    sm[:, n % 2, s * P:(s + 1) * P], ident[:])
                            last.then_inc(ptd, 1)
                            pe.wait_ge(ptc, n + 1)
                            if n >= 2:
                                pe.wait_ge(pvc, n - 1)
                            for s in range(i + 1):
                                last = pe.matmul(psum[:, 4 + n % 2, 0:P], qkv[:, b * TPB + s, 2 * H1:3 * H1],
                                                 pT[:, n % 2, s * P:(s + 1) * P], start=(s == 0), stop=(s == i))
                            last.then_inc(pvd, 1)

                    @block.scalar
                    def _(act):
                        for n in range(8):
                            act.wait_ge(td, n + 1)
                            act.copy(qk[:, n // NCH, n % NCH * CH:(n % NCH + 1) * CH], psum[:, n % 2, :]).then_inc(tc, 1)
                        for n in range(NT):
                            w = (n % TPB + 1) * P
                            act.wait_ge(negd, n + 1)
                            act.activation(sm[:, n % 2, 0:w], sm[:, n % 2, 0:w], ACT.Exp, bias=mx[:, n:n + 1],
                                           accum_out=sums[:, n:n + 1]).then_inc(expd, 1)
                            act.wait_ge(pvd, n + 1)
                            act.copy(aoT[:, n * P:(n + 1) * P], psum[:, 4 + n % 2, 0:P]).then_inc(pvc, 1)

                    @block.vector
                    def _(dve):
                        dve.wait_ge(cmd, 1)

                        def softmax_rows(n):
                            i = n % TPB
                            w = (i + 1) * P
                            dve.wait_ge(sd, n + 1)
                            if n >= 2:
                                dve.wait_ge(ptd, n - 1)
                            flat = psum[:, 0:2, :].rearrange("p c t -> p (c t)")
                            if i:
                                dve.tensor_scalar(sm[:, n % 2, 0:w - P], flat[:, 0:w - P], scale, None, ALU.mult)
                            dve.scalar_tensor_tensor(out=sm[:, n % 2, w - P:w], in0=flat[:, w - P:w], scalar=scale,
                                                     in1=cm[:], op0=ALU.mult, op1=ALU.add).then_inc(sc2, 1)
                            dve.wait_ge(sc2, n + 1)
                            dve.tensor_reduce(mx[:, n:n + 1], sm[:, n % 2, 0:w], AX_X, ALU.max).then_inc(maxd, 1)
                            dve.wait_ge(maxd, n + 1)
                            dve.tensor_scalar(mx[:, n:n + 1], mx[:, n:n + 1], -1.0, None, ALU.mult).then_inc(negd, 1)

                        softmax_rows(0)
                        for n in range(NT):
                            if n + 1 < NT:
                                softmax_rows(n + 1)
                            w = (n % TPB + 1) * P
                            dve.wait_ge(ptd, n + 1)
                            if n >= 2:
                                dve.wait_ge(pvd, n - 1)
                            dve.tensor_copy(pT[:, n % 2, 0:w], psum[:, 2:4, :].rearrange("p c t -> p (c t)")[:, 0:w]
                                            ).then_inc(ptc, 1)
                        dve.wait_ge(expd, NT)
                        dve.reciprocal(rinv[:], sums[:])

        def stage_l1_out(wbuf, rw, rinv, aoT):
            w = wbuf[:, 0, 0:E1 * D].rearrange("p (e c) -> p e c", c=D)
            loaded, ready, done, added = (sem("o1_" + n) for n in ("loaded", "ready", "done", "added"))
            with nc.Block() as block:
                @block.sync
                def _(sp):
                    sp.dma_start(w, a["l1_o"]).then_inc(loaded, 16)

                @block.tensor
                def _(pe):
                    def expert(e, first):
                        for i in range(NT):
                            if not (first and i < 4):
                                pe.wait_ge(added, NT * e + i - 3)
                            pe.matmul(psum[:, i % 4, 0:D], aoT[:, i * P:(i + 1) * P],
                                      w[:, bass.ds(e, 1), :].rearrange("p e c -> p (e c)"),
                                      start=True, stop=True).then_inc(done, 1)
                    pe.wait_ge(loaded, 16)
                    expert(0, True)
                    with pe.Fori(1, E1) as e:
                        expert(e, False)

                @block.vector
                def _(dve):
                    dve.tensor_tensor(rw[:], rw[:], over_e(rinv[:], E1), ALU.mult).then_inc(ready, 1)
                    dve.wait_ge(ready, 1)

                    def expert(e, first):
                        for i in range(NT):
                            dve.wait_ge(done, NT * e + i + 1)
                            if not first:
                                dve.wait_ge(added, NT * (e - 1) + i + 1)
                            dve.scalar_tensor_tensor(out=xtok[:, i, :], in0=psum[:, i % 4, 0:D],
                                                     scalar=rw[:, i, bass.ds(e, 1)], in1=xtok[:, i, :],
                                                     op0=ALU.mult, op1=ALU.add).then_inc(added, 1)
                    expert(0, True)
                    with dve.Fori(1, E1) as e:
                        expert(e, False)

        def stage_l1_same_rows(outer, w5, U, hm):
            WV, WO = 2, 4
            w = sb("f1_wbuf", [P, 4 * UNIT], on=outer)[:]
            wv = w[:, 0:E1 * KD * H1].rearrange("p (e k c) -> p e k c", e=E1, k=KD)
            wo = w[:, E1 * KD * H1:E1 * (KD * H1 + D)].rearrange("p (e c) -> p e c", c=D)
            cb = sb("f1_cb", [P, KD, B, P], on=outer)
            c = sb("f1_c", [P, KD, B], on=outer)
            rw = sb("f1_rw", [P, B, E1], on=outer)
            wloaded = sem("f1_wloaded")
            with ExitStack() as own:
                m1 = sb("f1_m1", [HEADS, S], U8, on=own)
                lim = sb("f1_lim", [HEADS, S], on=own)
                pr = sb("f1_pr", [HEADS, B, S], on=own)
                mx = sb("f1_mx", [HEADS, B], on=own)
                sums = sb("f1_sums", [HEADS, B], on=own)
                pT = sb("f1_pT", [P, B, TPB * HEADS], on=own)
                z = sb("f1_z", [HEADS, B, D], on=own)
                zT = sb("f1_zT", [P, B, KD, HEADS], on=own)
                oh = sb("f1_oh", [P, B, KD, 8], on=own)
                o = sb("f1_o", [P, KD, B], on=own)
                idle = sb("f1_idle", [1, 1], on=own)
                loaded, lims, sd, maxd, expd, pd, pc, zd, zc, ztd, ztc, ohd, od, cd, order = (
                    sem("f1_" + n) for n in ("loaded", "lims", "sd", "maxd", "expd", "pd", "pc", "zd", "zc", "ztd", "ztc",
                                             "ohd", "od", "cd", "order"))
                with nc.Block() as block:
                    @block.sync
                    def _(sp):
                        sp.dma_start(m1[:], a["mask"][0, :].partition_broadcast(HEADS)).then_inc(loaded, 16)
                        for k in range(KD):
                            sp.dma_start(wv[:, :, k, :], a["l1_qkv"][:, :, k, 2 * H1:3 * H1]).then_inc(wloaded, 16)
                        sp.dma_start(wo, a["l1_o"]).then_inc(wloaded, 16)

                    @block.gpsimd
                    def _(pool):
                        pool.memset(idle[:], 0.0)

                    @block.tensor
                    def _(pe):
                        for b in range(B):
                            for ch in range(2):
                                for k in range(KD):
                                    last = pe.matmul(psum[0:HEADS, 2 * b + ch, :], U[:, k, b, :],
                                                     fx[:, k, b * S + ch * CH:b * S + (ch + 1) * CH],
                                                     start=(k == 0), stop=(k == KD - 1))
                            last.then_inc(sd, 1)
                        for b in range(B):
                            pe.wait_ge(expd, b + 1)
                            for s in range(TPB):
                                last = pe.transpose(psum[:, 4 + b, s * HEADS:(s + 1) * HEADS],
                                                    pr[:, b, s * P:(s + 1) * P], ident[0:HEADS, 0:HEADS])
                            last.then_inc(pd, 1)
                        for b in range(B):
                            pe.wait_ge(pc, b + 1)
                            for s in range(TPB):
                                last = pe.matmul(psum[0:HEADS, 6 + b, 0:D], pT[:, b, s * HEADS:(s + 1) * HEADS],
                                                 xtok[:, b * TPB + s, :], start=(s == 0), stop=(s == TPB - 1))
                            last.then_inc(zd, 1)
                        pe.wait_ge(zc, 2)
                        for b in range(B):
                            for k in range(KD):
                                g = (b * KD + k) * HEADS
                                last = pe.transpose(psum[:, 0, g:g + HEADS], z[:, b, k * P:(k + 1) * P],
                                                    ident[0:HEADS, 0:HEADS])
                        last.then_inc(ztd, 1)
                        pe.wait_ge(ztc, 1)
                        for b in range(B):
                            for f in range(KD):
                                g = (b * KD + f) * 8
                                for k in range(KD):
                                    last = pe.matmul(psum[:, 1, g:g + 8], w5[:, WV, k, f * P:(f + 1) * P],
                                                     zT[:, b, k, f * 8:(f + 1) * 8], start=(k == 0), stop=(k == KD - 1))
                        last.then_inc(ohd, 1)
                        pe.wait_ge(od, 1)
                        for f in range(KD):
                            for k in range(KD):
                                last = pe.matmul(psum[:, 2, f * B:(f + 1) * B], w5[:, WO, k, f * P:(f + 1) * P],
                                                 o[:, k, :], start=(k == 0), stop=(k == KD - 1))
                        last.then_inc(cd, 1)

                    @block.scalar
                    def _(act):
                        for b in range(B):
                            act.wait_ge(maxd, b + 1)
                            act.activation(pr[:, b, :], pr[:, b, :], ACT.Exp, bias=mx[:, b:b + 1],
                                           accum_out=sums[:, b:b + 1]).then_inc(expd, 1)

                    @block.vector
                    def _(dve):
                        link = chain(dve, order)
                        dve.wait_ge(loaded, 16)
                        link(dve.tensor_scalar(lim[:], m1[:], FMAX, -FMAX, ALU.mult, ALU.add))
                        for b in range(B):
                            dve.wait_ge(sd, b + 1)
                            link(dve.tensor_tensor_reduce(pr[:, b, :], psum[0:HEADS, 2 * b:2 * b + 2, :].rearrange(
                                "p c t -> p (c t)"), lim[:], 1.0, -FMAX, ALU.add, ALU.max, mx[:, b:b + 1]))
                            dve.tensor_scalar(mx[:, b:b + 1], mx[:, b:b + 1], -1.0, None, ALU.mult).then_inc(maxd, 1)
                        for b in range(B):
                            dve.wait_ge(pd, b + 1)
                            dve.tensor_copy(pT[:, b, :], psum[:, 4 + b, 0:TPB * HEADS]).then_inc(pc, 1)
                        dve.wait_ge(expd, B)
                        link(dve.reciprocal(sums[:], sums[:]))
                        for b in range(B):
                            dve.wait_ge(zd, b + 1)
                            dve.tensor_scalar(z[:, b, :], psum[0:HEADS, 6 + b, 0:D], sums[:, b:b + 1], None,
                                              ALU.mult).then_inc(zc, 1)
                        dve.wait_ge(ztd, 1)
                        dve.tensor_copy(zT[:].rearrange("p b k h -> p (b k h)"), psum[:, 0, 0:B * KD * HEADS]).then_inc(ztc, 1)
                        dve.wait_ge(ohd, 1)
                        link(dve.tensor_tensor(oh[:].rearrange("p b k h -> p (b k) h"),
                                               psum[:, 1, 0:B * KD * 8].rearrange("p (g h) -> p g h", h=8),
                                               hm[:, :, 0].unsqueeze(1).to_broadcast([P, B * KD, 8]), ALU.mult))
                        for b in range(B):
                            last = dve.tensor_reduce(o[:, :, b], oh[:, b, :, :], AX_X, ALU.add)
                        last.then_inc(od, 1)
                        dve.wait_ge(cd, 1)
                        link(dve.tensor_copy(c[:].rearrange("p k b -> p (k b)"), psum[:, 2, 0:KD * B]))
                        dve.tensor_copy(cb[:], c[:].unsqueeze(3).to_broadcast([P, KD, B, P]))

            stage_l1_gating(rw, shared=cb)

            with ExitStack() as own:
                vw = sb("f1_vw", [P, B, E1], on=own)
                v = sb("f1_v", [P, B], on=own)
                av = sb("f1_av", [P, E1, B], on=own)
                row = sb("f1_row", [P, KD, B], on=own)
                rowb = sb("f1_rowb", [P, KD, B, P], on=own)
                vd, avd, outd, spread, turned, order = (
                    sem("f1_" + n) for n in ("vd", "avd", "outd", "spread", "turned", "order2"))
                with nc.Block() as block:
                    @block.tensor
                    def _(pe):
                        pe.wait_ge(wloaded, 48)
                        for e in range(E1):
                            for k in range(KD):
                                last = pe.matmul(psum[:, 0, e * B:(e + 1) * B], wv[:, e, k, :], c[:, k, :],
                                                 start=(k == 0), stop=(k == KD - 1))
                        last.then_inc(vd, 1)
                        pe.wait_ge(avd, 1)
                        for f in range(KD):
                            for e in range(E1):
                                last = pe.matmul(psum[:, 1, f * B:(f + 1) * B], wo[:, e, f * P:(f + 1) * P], av[:, e, :],
                                                 start=(e == 0), stop=(e == E1 - 1))
                        last.then_inc(outd, 1)
                        pe.wait_ge(spread, 1)
                        for b in range(B):
                            for k in range(KD):
                                last = pe.transpose(psum[:, 2 + b, k * P:(k + 1) * P], rowb[:, k, b, :], ident[:])
                            last.then_inc(turned, 1)

                    @block.vector
                    def _(dve):
                        link = chain(dve, order)
                        dve.wait_ge(vd, 1)
                        link(dve.tensor_tensor(vw[:], psum[:, 0, 0:E1 * B].rearrange("p (e b) -> p b e", b=B), rw[:],
                                               ALU.mult))
                        link(dve.tensor_reduce(v[:], vw[:], AX_X, ALU.add))
                        for b in range(B):
                            last = dve.tensor_scalar(av[:, :, b], rw[:, b, :], v[:, b:b + 1], None, ALU.mult)
                        last.then_inc(avd, 1)
                        dve.wait_ge(outd, 1)
                        link(dve.tensor_copy(row[:].rearrange("p k b -> p (k b)"), psum[:, 1, 0:KD * B]))
                        dve.tensor_copy(rowb[:], row[:].unsqueeze(3).to_broadcast([P, KD, B, P])).then_inc(spread, 1)
                        for b in range(B):
                            for k in range(KD):
                                dve.tensor_scalar(fx[:, k, b * S:(b + 1) * S], fx[:, k, b * S:(b + 1) * S],
                                                  row[:, k, b:b + 1], None, ALU.add)
                        for b in range(B):
                            dve.wait_ge(turned, b + 1)
                            half = xtok[:, b * TPB:(b + 1) * TPB, :]
                            dve.tensor_tensor(half, half, psum[:, 2 + b, 0:D].unsqueeze(1).to_broadcast([P, TPB, D]),
                                              ALU.add)

        def with_own_semaphores(part, *given):
            before = nc.snapshot_sems()
            part(*given)
            nc.all_engine_barrier()
            nc.clear_and_free_semaphores(nc.allocated_since(before))
            nc.all_engine_barrier()

        def layer1():
            with ExitStack() as own:
                w5 = sb("l1_w5", [P, 5, KD, D], on=own)
                U = sb("l1_U", [P, KD, B, HEADS], on=own)
                hm = sb("l1_headmask", [P, 8, HW], on=own)
                differ = sb("l1_differ", [1, 1], I32, on=own)

                def projections():
                    stage_to_features("a1", xtok, fx)
                    stage_l1_project(w5, U, hm, differ)

                def all_rows_masked_alike():
                    with ExitStack() as outer:
                        stage_l1_same_rows(outer, w5, U, hm)

                def any_mask():
                    stage_rows_times("v1", fx, w5[:, 2, :, :], ctok)
                    stage_l1_attend(U)
                    stage_to_features("o1", acc, fc)
                    stage_rows_times("w1", fc, w5[:, 4, :, :], ctok)
                    stage_to_features("b1", ctok, fc)
                    with ExitStack() as own2:
                        wbuf = sb("l1_wbuf", [P, 2, 2 * UNIT], on=own2)
                        rw = sb("l1_rw", [P, NT, E1], on=own2)
                        rinv = sb("l1_rinv", [P, NT], on=own2)
                        qkv = sb("l1_qkv", [P, NT, 3 * H1], on=own2)
                        aoT = fx[:, 0, :]
                        stage_l1_gating(rw)
                        stage_l1_qkv(wbuf, rw, qkv)
                        stage_l1_causal(qkv, aoT, rinv)
                        stage_l1_out(wbuf, rw, rinv, aoT)
                    stage_to_features("a2", xtok, fx)

                with_own_semaphores(projections)
                count = nc.values_load(differ[0:1, 0:1], min_val=0, max_val=S * S)
                with nc.If(count == 0):
                    with_own_semaphores(all_rows_masked_alike)
                with nc.Else():
                    with_own_semaphores(any_mask)
                nc.end_all_ifs()

        def stage_sigmoid_top2(tag, router, bias, gates):
            E = E2
            with ExitStack() as own:
                wr = sb(tag + "_w", [P, 2 * KD, E], on=own)
                bb = sb(tag + "_b", [P, E], on=own)
                cb = sb(tag + "_cb", [P, KD, B, P], on=own)
                s, sel, tmp, oh1, oh2 = (sb(f"{tag}_{n}", [P, NT, E], on=own) for n in ("s", "sel", "tmp", "oh1", "oh2"))
                top, small, good = (sb(f"{tag}_{n}", [P, NT], on=own) for n in ("top", "small", "good"))
                loaded, spread, done, sig, order = (sem(f"{tag}_{n}") for n in ("loaded", "spread", "done", "sig", "order"))
                with nc.Block() as block:
                    @block.sync
                    def _(sp):
                        sp.dma_start(wr[:], router).then_inc(loaded, 16)
                        sp.dma_start(bb[:], bias.partition_broadcast(P)).then_inc(loaded, 16)

                    @block.tensor
                    def _(pe):
                        pe.wait_ge(loaded, 32)
                        pe.wait_ge(spread, 1)
                        logits_on_pe(pe, fx, wr, E, extra=cb).then_inc(done, 1)

                    @block.scalar
                    def _(act):
                        act.wait_ge(done, 1)
                        act.activation(s[:].rearrange("p i e -> p (i e)"), psum[:, 0, 0:NT * E], ACT.Sigmoid).then_inc(sig, 1)

                    @block.vector
                    def _(dve):
                        link = chain(dve, order)
                        dve.tensor_copy(cb[:], condT[:].unsqueeze(3).to_broadcast([P, KD, B, P])).then_inc(spread, 1)
                        dve.wait_ge(loaded, 32)
                        dve.wait_ge(sig, 1)
                        link(dve.tensor_tensor(sel[:], s[:], bb[:].unsqueeze(1).to_broadcast([P, NT, E]), ALU.add))
                        pick(dve, link, sel[:], top[:], oh1[:], tmp[:], small[:], E)
                        link(dve.scalar_tensor_tensor(out=sel[:], in0=oh1[:], scalar=-1e30, in1=sel[:],
                                                      op0=ALU.mult, op1=ALU.add))
                        pick(dve, link, sel[:], top[:], oh2[:], tmp[:], small[:], E)
                        link(dve.tensor_tensor(oh1[:], oh1[:], oh2[:], ALU.add))
                        link(dve.tensor_tensor(tmp[:], s[:], oh1[:], ALU.mult))
                        link(dve.tensor_reduce(top[:], tmp[:], AX_X, ALU.add))
                        link(dve.tensor_scalar(good[:], top[:], 1e-9, None, ALU.is_gt))
                        link(dve.tensor_scalar(top[:], top[:], 1e-9, None, ALU.add))
                        link(dve.reciprocal(top[:], top[:]))
                        link(dve.tensor_tensor(top[:], top[:], good[:], ALU.mult))
                        link(dve.tensor_scalar(good[:], good[:], -0.5, 0.5, ALU.mult, ALU.add))
                        link(dve.tensor_tensor(tmp[:], tmp[:], over_e(top[:], E), ALU.mult))
                        link(dve.tensor_tensor(oh1[:], oh1[:], over_e(good[:], E), ALU.mult))
                        dve.tensor_tensor(gates[:], tmp[:], oh1[:], ALU.add)

        def stage_softmax_route(tag, own, E, router, picks):
            wr = sb(tag + "_w", [P, KD, E], on=own)
            pr, tmp = (sb(f"{tag}_{n}", [P, NT, E], on=own) for n in ("pr", "tmp"))
            ohs = [sb(f"{tag}_oh{n}", [P, NT, E], on=own) for n in range(picks)]
            tops = [sb(f"{tag}_top{n}", [P, NT], on=own) for n in range(picks)]
            small = sb(tag + "_small", [P, NT], on=own)
            loaded, done, shifted, expd, order = (sem(f"{tag}_{n}") for n in ("loaded", "done", "shifted", "expd", "order"))
            with nc.Block() as block:
                @block.sync
                def _(sp):
                    sp.dma_start(wr[:], router).then_inc(loaded, 16)

                @block.tensor
                def _(pe):
                    pe.wait_ge(loaded, 16)
                    logits_on_pe(pe, fc, wr, E).then_inc(done, 1)

                @block.scalar
                def _(act):
                    act.wait_ge(shifted, 1)
                    act.activation(pr[:], pr[:], ACT.Exp).then_inc(expd, 1)

                @block.vector
                def _(dve):
                    link = chain(dve, order)
                    dve.wait_ge(done, 1)
                    link(dve.tensor_copy(tmp[:].rearrange("p i e -> p (i e)"), psum[:, 0, 0:NT * E]))
                    link(dve.tensor_reduce(small[:], tmp[:], AX_X, ALU.max))
                    dve.tensor_tensor(pr[:], tmp[:], over_e(small[:], E), ALU.subtract).then_inc(shifted, 1)
                    dve.wait_ge(expd, 1)
                    link(dve.tensor_reduce(small[:], pr[:], AX_X, ALU.add))
                    link(dve.reciprocal(small[:], small[:]))
                    link(dve.tensor_tensor(pr[:], pr[:], over_e(small[:], E), ALU.mult))
                    for n in range(picks):
                        pick(dve, link, pr[:], tops[n][:], ohs[n][:], tmp[:], small[:], E)
                        if n + 1 < picks:
                            link(dve.scalar_tensor_tensor(out=pr[:], in0=ohs[n][:], scalar=-BIG, in1=pr[:],
                                                          op0=ALU.mult, op1=ALU.add))
            return ohs, tops

        def layer2():
            with ExitStack() as own:
                gates = sb("gates2", [P, NT, E2], on=own)
                stage_sigmoid_top2("t2", a["l2_router"], a["l2_bias"], gates)
                stage_glu("g2", fx, a["l2c_shared"])
                stage_gelu_experts("x2", fx, a["l2c_routed"], gates, 0.5, 0.25)
            stage_to_features("b2", ctok, fc)
            with ExitStack() as own:
                slots = sb("slots2", [P, 2 * NT], U32, on=own)
                tile_expert = sb("tile_expert2", [1, SLOT_TILES2], I32, on=own)
                last_tile = sb("last_tile2", [1, E2], I32, on=own)
                halves = [sb(f"half_top{n}", [P, NT], on=own) for n in range(2)]
                with ExitStack() as route:
                    ohs, tops = stage_softmax_route("r2", route, E2, a["l2_gate"], 2)
                    with nc.Block() as block:
                        @block.vector
                        def _(dve):
                            for n in range(2):
                                dve.tensor_scalar(halves[n][:], tops[n][:], 0.5, None, ALU.mult)
                    stage_slots("s2", ohs, E2, SLOT_TILES2, slots, tile_expert, last_tile)
                stage_glu("h2", fc, a["l2f_shared"], beside=scatter_rows("sc2", ctok, rows2_in, slots, 2))
                stage_sorted_glu("e2", SLOT_TILES2, 2, a["l2f_routed"], tile_expert, last_tile, rows2_in, rows2_out)
                bufs = [as_tokens(fx), as_tokens(fc)]
                stage_gather("ga2", rows2_out, slots, bufs)
                stage_add_to_x("x2", [(acc[:], 0.5 / 8), (bufs[0], halves[0]), (bufs[1], halves[1])])

        def stage_capacity_slots(onehot, top, slots):
            E = E3
            with ExitStack() as own:
                val = sb("s3_val", [P, NT, E], on=own)
                vT = sb("s3_vT", [E, T], on=own)
                work = sb("s3_work", [E, T], on=own)
                best = sb("s3_best", [E, 8], on=own)
                base = sb("s3_base", [E, 1], on=own)
                cum = sb("s3_cum", [E, T], on=own)
                valued, turned, copied, iotas, cols, order = (
                    sem("s3_" + n) for n in ("valued", "turned", "copied", "iotas", "cols", "order"))
                with nc.Block() as block:
                    @block.gpsimd
                    def _(pool):
                        pool.iota(base[:], pattern=[[0, 1]], base=-1 - DROPPED, channel_multiplier=CAP,
                                  allow_small_or_imprecise_dtypes=True).then_inc(iotas, 1)

                    @block.tensor
                    def _(pe):
                        pe.wait_ge(valued, 1)
                        for g in range(NCH):
                            for q in range(TPC):
                                last = pe.transpose(psum[0:E, g, q * P:(q + 1) * P], val[:, g * TPC + q, :], ident[:])
                            last.then_inc(turned, 1)
                        pe.wait_ge(iotas, 2)
                        for i in range(NT):
                            last = pe.matmul(psum[:, 6, i:i + 1], cum[:, i * P:(i + 1) * P], ones[0:E, 0:1],
                                             start=True, stop=True)
                        last.then_inc(cols, 1)

                    @block.scalar
                    def _(act):
                        for g in range(NCH):
                            act.wait_ge(turned, g + 1)
                            act.copy(vT[:, g * CH:(g + 1) * CH], psum[0:E, g, :])
                            act.copy(work[:, g * CH:(g + 1) * CH], psum[0:E, g, :]).then_inc(copied, 1)

                    @block.vector
                    def _(dve):
                        link = chain(dve, order)
                        dve.tensor_tensor(val[:], onehot[:], over_e(top[:], E), ALU.mult).then_inc(valued, 1)
                        dve.wait_ge(copied, NCH)
                        for _ in range(CAP // 8):
                            link(dve.max(best[:], work[:]))
                            link(dve.match_replace(work[:], best[:], work[:], -1.0))
                        link(dve.tensor_scalar(work[:], work[:], 0.0, None, ALU.is_lt))
                        link(dve.tensor_scalar(vT[:], vT[:], 0.0, None, ALU.is_gt))
                        link(dve.tensor_tensor(vT[:], vT[:], work[:], ALU.mult))
                        link(dve.tensor_tensor_scan(cum[:], ones[0:E, 0:1].to_broadcast([E, T]), vT[:], 0.0,
                                                    ALU.mult, ALU.add))
                        dve.wait_ge(iotas, 1)
                        dve.scalar_tensor_tensor(out=cum[:], in0=cum[:], scalar=base[:, 0:1], in1=vT[:],
                                                 op0=ALU.add, op1=ALU.mult).then_inc(iotas, 1)
                        dve.wait_ge(cols, 1)
                        dve.tensor_scalar(slots[:], psum[:, 6, 0:NT], float(DROPPED), None, ALU.add)

        def stage_capacity_experts():
            NF = 4
            W = KD * FU + NF * D
            R2 = CAP - P
            with ExitStack() as own:
                w = sb("e3_w", [P, 2, W + NF], on=own)
                b2 = sb("e3_b2", [P, 2, D], on=own)
                ra = sb("e3_ra", [P, 2, D], on=own)
                rb = sb("e3_rb", [R2, 2, D], on=own)
                rT = sb("e3_rT", [P, 2, KD, CAP], on=own)
                hT = sb("e3_hT", [P, NF, CAP], on=own)
                oa = sb("e3_oa", [P, 2, D], on=own)
                ob = sb("e3_ob", [R2, 2, D], on=own)
                x_in = [sem(f"e3_x_in{r}") for r in range(2)]
                w_in = [sem(f"e3_w_in{r}") for r in range(2)]
                stored = [sem(f"e3_stored{r}") for r in range(2)]
                rows_t, rows_c, up, hidden, down, outc = (
                    sem("e3_" + n) for n in ("rows_t", "rows_c", "up", "hidden", "down", "outc"))
                src = rows3_in.rearrange("(e c) d -> e c d", c=CAP)
                dst = rows3_out.rearrange("(e c) d -> e c d", c=CAP)
                with nc.Block() as block:
                    @block.sync
                    def _(sp):
                        def load(i, r, first):
                            e = 2 * i + r
                            if not first:
                                sp.wait_ge(rows_t, e - 1)
                            sp.dma_start(ra[:, r, :], src[bass.ds(e, 1), 0:P].rearrange("e c d -> c (e d)")).then_inc(x_in[r], 16)
                            sp.dma_start(rb[:, r, :], src[bass.ds(e, 1), P:CAP].rearrange("e c d -> c (e d)")).then_inc(x_in[r], 16)
                            if not first:
                                sp.wait_ge(outc, 2 * (e - 1))
                            sp.dma_start(w[:, r, :], a["l3_experts"][bass.ds(e, 1)].rearrange("e p n -> p (e n)")
                                         ).then_inc(w_in[r], 16)
                            sp.dma_start(b2[:, r, :], a["l3_b2"][bass.ds(e, 1)].rearrange("e d -> (e d)").partition_broadcast(P)
                                         ).then_inc(w_in[r], 16)
                        load(0, 0, True)
                        load(0, 1, True)
                        with sp.Fori(1, E3 // 2) as i:
                            load(i, 0, False)
                            load(i, 1, False)

                    @block.tensor
                    def _(pe):
                        def turn(i, r, first=False):
                            pe.wait_ge(x_in[r], 32 * i + 32)
                            if not first:
                                pe.wait_ge(rows_c, 2 * i + r)
                            for k in range(KD):
                                pe.transpose(psum[:, 6, k * CAP:k * CAP + P], ra[:, r, k * P:(k + 1) * P], ident[:])
                                last = pe.transpose(psum[:, 6, k * CAP + P:(k + 1) * CAP], rb[:, r, k * P:(k + 1) * P],
                                                    ident[0:R2, 0:R2])
                            last.then_inc(rows_t, 1)

                        def expert(i, r, first=False, last_expert=False):
                            e = 2 * i + r
                            pe.wait_ge(rows_c, e + 1)
                            pe.wait_ge(w_in[r], 32 * i + 32)
                            if not first:
                                pe.wait_ge(hidden, NF * e)
                            for f in range(NF):
                                for k in range(KD):
                                    last = pe.matmul(psum[:, f, 0:CAP],
                                                     w[:, r, k * FU + f * P:k * FU + (f + 1) * P], rT[:, r, k, :],
                                                     start=(k == 0), stop=(k == KD - 1))
                                last.then_inc(up, 1)
                            if not last_expert:
                                turn(i + r, 1 - r)
                            pe.wait_ge(hidden, NF * e + NF)
                            for part, (c0, c1) in enumerate(((0, P), (P, CAP))):
                                if not first:
                                    pe.wait_ge(outc, 2 * (e - 1) + part + 1)
                                for f in range(NF):
                                    last = pe.matmul(psum[0:c1 - c0, 4 + part, 0:D], hT[:, f, c0:c1],
                                                     w[:, r, KD * FU + f * D:KD * FU + (f + 1) * D],
                                                     start=(f == 0), stop=(f == NF - 1))
                                last.then_inc(down, 1)

                        turn(0, 0, first=True)
                        expert(0, 0, first=True)
                        expert(0, 1)
                        with pe.Fori(1, E3 // 2 - 1) as i:
                            expert(i, 0)
                            expert(i, 1)
                        expert(E3 // 2 - 1, 0)
                        expert(E3 // 2 - 1, 1, last_expert=True)

                    @block.scalar
                    def _(act):
                        def rows(i, r, first):
                            e = 2 * i + r
                            act.wait_ge(rows_t, e + 1)
                            if not first:
                                act.wait_ge(up, NF * (e - 1))
                            act.copy(rT[:, r, :, :].rearrange("p k t -> p (k t)"), psum[:, 6, 0:KD * CAP]).then_inc(rows_c, 1)

                        def gelu(i, r, first):
                            e = 2 * i + r
                            for f in range(NF):
                                act.wait_ge(up, NF * e + f + 1)
                                if not first:
                                    act.wait_ge(down, 2 * e)
                                act.activation(hT[:, f, :], psum[:, f, 0:CAP],
                                               ACT.Gelu_apprx_tanh, bias=w[:, r, W + f:W + f + 1]).then_inc(hidden, 1)
                        rows(0, 0, True)
                        gelu(0, 0, True)
                        rows(0, 1, True)
                        gelu(0, 1, False)
                        with act.Fori(1, E3 // 2) as i:
                            for r in range(2):
                                rows(i, r, False)
                                gelu(i, r, False)

                    @block.vector
                    def _(dve):
                        def outs(i, r, first):
                            e = 2 * i + r
                            if not first:
                                dve.wait_ge(stored[r], 32 * i)
                            dve.wait_ge(w_in[r], 32 * i + 32)
                            dve.wait_ge(down, 2 * e + 1)
                            dve.tensor_tensor(oa[:, r, :], psum[:, 4, 0:D], b2[:, r, :], ALU.add).then_inc(outc, 1)
                            dve.wait_ge(down, 2 * e + 2)
                            dve.tensor_tensor(ob[:, r, :], psum[0:R2, 5, 0:D], b2[0:R2, r, :], ALU.add).then_inc(outc, 1)
                        outs(0, 0, True)
                        outs(0, 1, True)
                        with dve.Fori(1, E3 // 2) as i:
                            outs(i, 0, False)
                            outs(i, 1, False)

                    @block.gpsimd
                    def _(pool):
                        with pool.Fori(0, E3 // 2) as i:
                            for r in range(2):
                                e = 2 * i + r
                                pool.wait_ge(outc, 2 * e + 2)
                                pool.dma_start(dst[bass.ds(e, 1), 0:P].rearrange("e c d -> c (e d)"), oa[:, r, :]).then_inc(stored[r], 16)
                                pool.dma_start(dst[bass.ds(e, 1), P:CAP].rearrange("e c d -> c (e d)"), ob[:, r, :]).then_inc(stored[r], 16)
                        for r in range(2):
                            pool.wait_ge(stored[r], 32 * (E3 // 2))

        def layer3():
            stage_to_features("a3", xtok, fx)
            with ExitStack() as own:
                gates = sb("gates3", [P, NT, E2], on=own)
                stage_sigmoid_top2("t3", a["l3_router"], a["l3_bias"], gates)
                stage_glu("g3", fx, a["l3c_shared"])
                stage_gelu_experts("x3", fx, a["l3c_routed"], gates, 1.0, 1.0 / 3.0)
            stage_to_features("b3", ctok, fc)
            with ExitStack() as own:
                slots = sb("slots3", [P, NT], U32, on=own)
                ohs, tops = stage_softmax_route("r3", own, E3, a["l3_gate"], 1)
                stage_capacity_slots(ohs[0], tops[0], slots)
                stage_scatter("sc3", ctok, rows3_in, slots, 1, bound=E3 * CAP - 1)
                stage_capacity_experts()
                stage_gather("ga3", rows3_out, slots, [ctok], bound=E3 * CAP - 1)
                stage_add_to_x("x3", [(ctok[:], 1.0)])

        def stage_store():
            stored = sem("stored")
            with nc.Block() as block:
                @block.sync
                def _(sp):
                    sp.dma_start(out.rearrange("(i p) d -> p i d", p=P), xtok[:]).then_inc(stored, 16)
                    sp.wait_ge(stored, 16)

        with_own_semaphores(stage_load)
        with_own_semaphores(layer0)
        layer1()
        with_own_semaphores(layer2)
        with_own_semaphores(layer3)
        with_own_semaphores(stage_store)


def kernel(**inputs):
    import numpy as np
    import concourse.bacc as bacc
    from concourse.bass_utils import run_bass_kernel_spmd

    v = {k: np.asarray(x) for k, x in inputs.items()}

    def rows(w):
        *lead, n, m = w.shape
        w = w.reshape(*lead, n // P, P, m)
        return np.moveaxis(w, -3, -2).reshape(*lead, P, n // P * m)

    def unit(gate, up, down):
        return np.concatenate([rows(gate), rows(up), rows(down)], axis=-1)

    def swap(w):
        return np.swapaxes(w, -1, -2)

    w1s = v["L2_ffn_w1_s"].transpose(1, 0, 2).reshape(D, 2, FU).transpose(1, 0, 2)
    w3s = v["L2_ffn_w3_s"].transpose(1, 0, 2).reshape(D, 2, FU).transpose(1, 0, 2)
    w2s = v["L2_ffn_w2_s"].reshape(2, FU, D)
    arrays = {
        "x": v["x"].reshape(T, D),
        "condT": rows(swap(v["cond_1024"])).reshape(P, KD, B),
        "mask": v["mask_SxS_bk0"],
        "l0_cond_w": rows(v["L0_cond_weight"]).reshape(P, KD, D),
        "l0_gate": rows(v["L0_ffn_gate_w"]).reshape(P, KD, E0),
        "l0_shared": unit(v["L0_ffn_shared_gate_w"], v["L0_ffn_shared_up_w"], v["L0_ffn_shared_down_w"])[None],
        "l0_routed": unit(v["L0_ffn_routed_gate_w"], v["L0_ffn_routed_up_w"], v["L0_ffn_routed_down_w"]),
        "l1_w": np.stack([rows(w).reshape(P, KD, D) for w in (
            swap(v["L1_cond_Wq"]), v["L1_cond_Wk"], swap(v["L1_cond_Wv"]), swap(v["L1_cond_Wt"]),
            swap(v["L1_cond_Wo"]))], axis=1),
        "l1_sim": rows(v["L1_ffn_sim_matrix"]).reshape(P, KD, E1),
        "l1_gates": v["L1_ffn_gates"],
        "l1_qkv": rows(np.concatenate([v["L1_ffn_q_proj"], v["L1_ffn_k_proj"], v["L1_ffn_v_proj"]], axis=-1)
                       ).reshape(E1, P, KD, 3 * H1).transpose(1, 0, 2, 3),
        "l1_o": v["L1_ffn_o_proj"].transpose(1, 0, 2),
        "l2_router": rows(swap(v["L2_cond_W_router"])).reshape(P, 2 * KD, E2),
        "l2_bias": v["L2_cond_router_bias"],
        "l2c_shared": unit(swap(v["L2_cond_s_w1"]), swap(v["L2_cond_s_w3"]), swap(v["L2_cond_s_w2"])),
        "l2c_routed": np.concatenate([rows(swap(v["L2_cond_r_w1"])), rows(swap(v["L2_cond_r_w2"]))], axis=-1),
        "l2_gate": rows(swap(v["L2_ffn_gate_W"])).reshape(P, KD, E2),
        "l2f_shared": unit(w1s, w3s, w2s),
        "l2f_routed": unit(v["L2_ffn_w1_e"], v["L2_ffn_w3_e"], v["L2_ffn_w2_e"]),
        "l3_router": rows(v["L3_cond_router_W"]).reshape(P, 2 * KD, E2),
        "l3_bias": v["L3_cond_router_bias"],
        "l3c_shared": unit(v["L3_cond_w1"], v["L3_cond_w3"], v["L3_cond_w2"])[None],
        "l3c_routed": np.concatenate([rows(v["L3_cond_W1e"]), rows(v["L3_cond_W2e"])], axis=-1),
        "l3_gate": rows(v["L3_ffn_Wg"]).reshape(P, KD, E3),
        "l3_experts": np.concatenate([rows(v["L3_ffn_W1"]), rows(v["L3_ffn_W2"]),
                                      rows(v["L3_ffn_b1"][:, :, None])], axis=-1),
        "l3_b2": v["L3_ffn_b2"],
    }
    nc = bacc.Bacc("TRN2", target_bir_lowering=False, num_devices=1)
    arrays = {f"in_{k}": np.ascontiguousarray(x) for k, x in arrays.items()}
    args = {k[3:]: nc.dram_tensor(k, x.shape, mybir.dt.from_np(x.dtype), kind="ExternalInput").ap()
            for k, x in arrays.items()}
    out = nc.dram_tensor("out_x", (T, D), F32, kind="ExternalOutput").ap()
    build(nc, args, out)
    got = run_bass_kernel_spmd(nc, [arrays], core_ids=[0]).results[0]["out_x"]
    return got.reshape(B, S, D)
```
